# Optimizing a Trainium2 kernel written in Bass

```python
import numpy as np
import jax
import jax.numpy as jnp

def _softmax(x, axis=-1):
    return jax.nn.softmax(x, axis=axis)

def _gelu(x):
    return jax.nn.gelu(x, approximate=True)

def _silu(x):
    return jax.nn.silu(x)

def _sigmoid(x):
    return jax.nn.sigmoid(x)

def _layernorm(x, axis=-1, eps=1e-05):
    m = jnp.mean(x, axis=axis, keepdims=True)
    v = jnp.var(x, axis=axis, keepdims=True)
    return (x - m) / jnp.sqrt(v + eps)

def _scatter_add(tgt, idx, src, axis=0):
    return tgt.at[idx].add(src)

def _segment_sum(src, seg, n):
    return jax.ops.segment_sum(src, seg, n)
kernel_name = 'mk_decoder_preln_d2_seqx_r8_8dbec2'

def setup_inputs(seed: int=0):
    np.random.seed(seed)
    _w = jnp.asarray

    def _rec_inputs():
        import jax
        import jax.numpy as jnp
        _rk = jax.random.key(seed)
        x = -0.0002928 + 1 * jax.random.normal(jax.random.fold_in(_rk, 1), (2, 512, 128), jnp.float32)
        _lenS = 512 - jax.random.randint(jax.random.fold_in(_rk, 7), (2,), 0, max(1, 512 // 4) + 1, jnp.int32)
        _lenS2 = 77 - jax.random.randint(jax.random.fold_in(_rk, 8), (2,), 0, max(1, 77 // 4) + 1, jnp.int32)
        _ctx_1024P = jax.random.normal(jax.random.fold_in(_rk, 11), (2, 16, 128), jnp.float32)
        _ctx_1024c = jax.random.dirichlet(jax.random.fold_in(_rk, 511), 0.3 * jnp.ones((16,), jnp.float32), (2, 77))
        _ctx_1024t = jnp.einsum('bsk,bkd->bsd', _ctx_1024c, _ctx_1024P)
        _ctx_1024t = _ctx_1024t * jax.lax.rsqrt(jnp.mean(jnp.square(_ctx_1024t)) + 1e-12) * 0.953939
        ctx_1024 = -1.39393e-06 + 0.999914 * (_ctx_1024t + 0.3 * jax.random.normal(jax.random.fold_in(_rk, 611), (2, 77, 128), jnp.float32))
        return (x, ctx_1024)
    x, ctx_1024 = _rec_inputs()

    def _L0_attn_setup():
        import jax, jax.numpy as jnp
        import numpy as np
        from math import sqrt
        D_MODEL = 128
        B, T = (4, 512)
        key = jax.random.key(seed)
        kx, kqk, kvo = jax.random.split(key, 3)
        x = jax.random.normal(kx, (B, T, D_MODEL), dtype=jnp.float32)
        limit = sqrt(6.0 / (2 * D_MODEL))
        QK = jax.random.uniform(kqk, (D_MODEL, D_MODEL), minval=-limit, maxval=limit, dtype=jnp.float32)
        VO = jax.random.uniform(kvo, (D_MODEL, D_MODEL), minval=-limit, maxval=limit, dtype=jnp.float32)
        return {'x': x, 'QK': QK, 'VO': VO}
    _L0_attn_all = _L0_attn_setup()
    _L0_attn_in = {k: v for k, v in _L0_attn_all.items() if k in ('QK', 'VO')}
    del _L0_attn_all

    def _L0_xattn_setup():
        import jax, jax.numpy as jnp
        import numpy as np
        EMBED_DIM = 128
        NUM_HEADS = 16
        HEAD_DIM = EMBED_DIM // NUM_HEADS
        B, T_Q, T_K = (2, 256, 256)
        key = jax.random.key(seed)
        ks = jax.random.split(key, 11)
        s = 1.0 / np.sqrt(EMBED_DIM)
        return {'query': jax.random.normal(ks[0], (B, T_Q, EMBED_DIM), jnp.float32), 'key': jax.random.normal(ks[1], (B, T_K, EMBED_DIM), jnp.float32), 'value': jax.random.normal(ks[2], (B, T_K, EMBED_DIM), jnp.float32), 'Wq': jax.random.normal(ks[3], (EMBED_DIM, EMBED_DIM), jnp.float32) * s, 'bq': jnp.zeros((EMBED_DIM,), jnp.float32), 'Wk': jax.random.normal(ks[4], (EMBED_DIM, EMBED_DIM), jnp.float32) * s, 'bk': jnp.zeros((EMBED_DIM,), jnp.float32), 'Wv': jax.random.normal(ks[5], (EMBED_DIM, EMBED_DIM), jnp.float32) * s, 'bv': jnp.zeros((EMBED_DIM,), jnp.float32), 'Wo': jax.random.normal(ks[6], (EMBED_DIM, EMBED_DIM), jnp.float32) * s, 'bo': jnp.zeros((EMBED_DIM,), jnp.float32)}
    _L0_xattn_all = _L0_xattn_setup()
    _L0_xattn_in = {k: v for k, v in _L0_xattn_all.items() if k in ('Wq', 'bq', 'Wk', 'bk', 'Wv', 'bv', 'Wo', 'bo')}
    del _L0_xattn_all

    def _L0_ffn_setup():
        import jax, jax.numpy as jnp
        import numpy as np
        CAPACITY_FACTOR = 1.25
        key = jax.random.key(seed)
        ks = jax.random.split(key, 6)
        B, S, H, E = (4, 512, 128, 8)
        scale = 1.0 / np.sqrt(H)
        return {'tokens': jax.random.normal(ks[0], (B, S, H), dtype=jnp.float32), 'gate_w': jax.random.normal(ks[1], (E, H), dtype=jnp.float32) * scale, 'w1': jax.random.normal(ks[2], (E, H, H), dtype=jnp.float32) * scale, 'b1': jax.random.normal(ks[3], (E, H), dtype=jnp.float32) * 0.01, 'w2': jax.random.normal(ks[4], (E, H, H), dtype=jnp.float32) * scale, 'b2': jax.random.normal(ks[5], (E, H), dtype=jnp.float32) * 0.01}
    _L0_ffn_all = _L0_ffn_setup()
    _L0_ffn_in = {k: v for k, v in _L0_ffn_all.items() if k in ('gate_w', 'w1', 'b1', 'w2', 'b2')}
    del _L0_ffn_all

    def _L1_attn_setup():
        import jax, jax.numpy as jnp
        import numpy as np
        NUM_HEADS = 16
        CLIP = 16
        key = jax.random.key(seed)
        ks = jax.random.split(key, 7)
        d = 128
        return {'x': jax.random.normal(ks[0], (2, 256, d), dtype=jnp.float32), 'Wq': jax.random.normal(ks[1], (d, d), dtype=jnp.float32) / np.sqrt(d), 'Wk': jax.random.normal(ks[2], (d, d), dtype=jnp.float32) / np.sqrt(d), 'Wv': jax.random.normal(ks[3], (d, d), dtype=jnp.float32) / np.sqrt(d), 'Wo': jax.random.normal(ks[4], (d, d), dtype=jnp.float32) / np.sqrt(d), 'bo': jax.random.normal(ks[5], (d,), dtype=jnp.float32) * 0.01, 'rel_emb': jax.random.normal(ks[6], (CLIP + 1,), dtype=jnp.float32)}
    _L1_attn_all = _L1_attn_setup()
    _L1_attn_in = {k: v for k, v in _L1_attn_all.items() if k in ('Wq', 'Wk', 'Wv', 'Wo', 'bo', 'rel_emb')}
    del _L1_attn_all

    def _L1_xattn_setup():
        import jax, jax.numpy as jnp
        import numpy as np
        B, T, E, H = (4, 1024, 128, 16)
        D = E // H
        SCALE = 1.0 / np.sqrt(D).astype(np.float32)
        EPS_FM = 1e-06
        EPS_Z = 1e-08

        def _heads(x):
            b, t, _ = x.shape
            return x.reshape(b, t, H, D).transpose(0, 2, 1, 3)

        def _feature_map(x):
            return jax.nn.relu(x) + EPS_FM
        key = jax.random.key(seed)
        ks = jax.random.split(key, 11)
        s = 1.0 / np.sqrt(E).astype(np.float32)
        return {'query': jax.random.normal(ks[0], (B, T, E), jnp.float32), 'key': jax.random.normal(ks[1], (B, T, E), jnp.float32), 'value': jax.random.normal(ks[2], (B, T, E), jnp.float32), 'Wq': jax.random.normal(ks[3], (E, E), jnp.float32) * s, 'bq': jax.random.normal(ks[4], (E,), jnp.float32) * 0.01, 'Wk': jax.random.normal(ks[5], (E, E), jnp.float32) * s, 'bk': jax.random.normal(ks[6], (E,), jnp.float32) * 0.01, 'Wv': jax.random.normal(ks[7], (E, E), jnp.float32) * s, 'bv': jax.random.normal(ks[8], (E,), jnp.float32) * 0.01, 'Wo': jax.random.normal(ks[9], (E, E), jnp.float32) * s, 'bo': jax.random.normal(ks[10], (E,), jnp.float32) * 0.01}
    _L1_xattn_all = _L1_xattn_setup()
    _L1_xattn_in = {k: v for k, v in _L1_xattn_all.items() if k in ('Wq', 'bq', 'Wk', 'bk', 'Wv', 'bv', 'Wo', 'bo')}
    del _L1_xattn_all

    def _L1_ffn_setup():
        import jax, jax.numpy as jnp
        import numpy as np
        E, K = (8, 2)
        key = jax.random.key(seed)
        ks = jax.random.split(key, 5)
        B, S, H, I = (2, 128, 128, 512)
        scale_h = 1.0 / np.sqrt(H)
        scale_i = 1.0 / np.sqrt(I)
        return {'hidden_states': jax.random.normal(ks[0], (B, S, H), jnp.float32), 'conf_w': jax.random.normal(ks[1], (E, H), jnp.float32) * 0.1 * scale_h, 'conf_b': jnp.zeros((E,), jnp.float32), 'gate_w': jax.random.normal(ks[2], (E, I, H), jnp.float32) * scale_h, 'up_w': jax.random.normal(ks[3], (E, I, H), jnp.float32) * scale_h, 'down_w': jax.random.normal(ks[4], (E, H, I), jnp.float32) * scale_i, 'wealth': jnp.ones((E,), jnp.float32)}
    _L1_ffn_all = _L1_ffn_setup()
    _L1_ffn_in = {k: v for k, v in _L1_ffn_all.items() if k in ('conf_w', 'conf_b', 'gate_w', 'up_w', 'down_w', 'wealth')}
    del _L1_ffn_all
    return {'x': x, 'ctx_1024': ctx_1024, 'L0_attn_QK': _L0_attn_in['QK'], 'L0_attn_VO': _L0_attn_in['VO'], 'L0_xattn_Wq': _L0_xattn_in['Wq'], 'L0_xattn_bq': _L0_xattn_in['bq'], 'L0_xattn_Wk': _L0_xattn_in['Wk'], 'L0_xattn_bk': _L0_xattn_in['bk'], 'L0_xattn_Wv': _L0_xattn_in['Wv'], 'L0_xattn_bv': _L0_xattn_in['bv'], 'L0_xattn_Wo': _L0_xattn_in['Wo'], 'L0_xattn_bo': _L0_xattn_in['bo'], 'L0_ffn_gate_w': _L0_ffn_in['gate_w'], 'L0_ffn_w1': _L0_ffn_in['w1'], 'L0_ffn_b1': _L0_ffn_in['b1'], 'L0_ffn_w2': _L0_ffn_in['w2'], 'L0_ffn_b2': _L0_ffn_in['b2'], 'L1_attn_Wq': _L1_attn_in['Wq'], 'L1_attn_Wk': _L1_attn_in['Wk'], 'L1_attn_Wv': _L1_attn_in['Wv'], 'L1_attn_Wo': _L1_attn_in['Wo'], 'L1_attn_bo': _L1_attn_in['bo'], 'L1_attn_rel_emb': _L1_attn_in['rel_emb'], 'L1_xattn_Wq': _L1_xattn_in['Wq'], 'L1_xattn_bq': _L1_xattn_in['bq'], 'L1_xattn_Wk': _L1_xattn_in['Wk'], 'L1_xattn_bk': _L1_xattn_in['bk'], 'L1_xattn_Wv': _L1_xattn_in['Wv'], 'L1_xattn_bv': _L1_xattn_in['bv'], 'L1_xattn_Wo': _L1_xattn_in['Wo'], 'L1_xattn_bo': _L1_xattn_in['bo'], 'L1_ffn_conf_w': _L1_ffn_in['conf_w'], 'L1_ffn_conf_b': _L1_ffn_in['conf_b'], 'L1_ffn_gate_w': _L1_ffn_in['gate_w'], 'L1_ffn_up_w': _L1_ffn_in['up_w'], 'L1_ffn_down_w': _L1_ffn_in['down_w'], 'L1_ffn_wealth': _L1_ffn_in['wealth']}

def reference(x, ctx_1024, L0_attn_QK, L0_attn_VO, L0_xattn_Wq, L0_xattn_bq, L0_xattn_Wk, L0_xattn_bk, L0_xattn_Wv, L0_xattn_bv, L0_xattn_Wo, L0_xattn_bo, L0_ffn_gate_w, L0_ffn_w1, L0_ffn_b1, L0_ffn_w2, L0_ffn_b2, L1_attn_Wq, L1_attn_Wk, L1_attn_Wv, L1_attn_Wo, L1_attn_bo, L1_attn_rel_emb, L1_xattn_Wq, L1_xattn_bq, L1_xattn_Wk, L1_xattn_bk, L1_xattn_Wv, L1_xattn_bv, L1_xattn_Wo, L1_xattn_bo, L1_ffn_conf_w, L1_ffn_conf_b, L1_ffn_gate_w, L1_ffn_up_w, L1_ffn_down_w, L1_ffn_wealth):
    import jax
    import jax.numpy as jnp

    def _L0_attn_ref(x, QK, VO):
        import jax, jax.numpy as jnp
        import numpy as np
        from math import sqrt
        D_MODEL = 128
        B, T = (4, 512)
        d_model = QK.shape[0]
        xQK = jnp.einsum('btd,de->bte', x, QK)
        scores = jnp.einsum('bte,bue->btu', xQK, x) / sqrt(d_model)
        attn = jax.nn.softmax(scores, axis=2)
        av = jnp.einsum('btu,bud->btd', attn, x)
        return jnp.einsum('btd,de->bte', av, VO)

    def _L0_xattn_ref(query, key, value, Wq, bq, Wk, bk, Wv, bv, Wo, bo):
        import jax, jax.numpy as jnp
        import numpy as np
        EMBED_DIM = 128
        NUM_HEADS = 16
        HEAD_DIM = EMBED_DIM // NUM_HEADS
        B, T_Q, T_K = (2, 256, 256)
        b, tq, _ = query.shape
        tk = key.shape[1]
        q = (query @ Wq.T + bq).reshape(b, tq, NUM_HEADS, HEAD_DIM).transpose(0, 2, 1, 3)
        k = (key @ Wk.T + bk).reshape(b, tk, NUM_HEADS, HEAD_DIM).transpose(0, 2, 1, 3)
        v = (value @ Wv.T + bv).reshape(b, tk, NUM_HEADS, HEAD_DIM).transpose(0, 2, 1, 3)
        scores = jnp.einsum('bhqd,bhkd->bhqk', q, k) / np.sqrt(HEAD_DIM)
        attn = jax.nn.softmax(scores, axis=-1)
        attn = jnp.nan_to_num(attn, nan=0.0)
        out = jnp.einsum('bhqk,bhkd->bhqd', attn, v)
        out = out.transpose(0, 2, 1, 3).reshape(b, tq, EMBED_DIM)
        return out @ Wo.T + bo

    def _L0_ffn_ref(tokens, gate_w, w1, b1, w2, b2):
        import jax, jax.numpy as jnp
        import numpy as np
        CAPACITY_FACTOR = 1.25
        B, S, H = tokens.shape
        E = gate_w.shape[0]
        N = B * S
        cap = int(CAPACITY_FACTOR * N / E)
        x = tokens.reshape(N, H)
        probs = jax.nn.softmax(x @ gate_w.T, axis=-1)
        top2_w, top2_idx = jax.lax.top_k(probs, 2)
        a_e = top2_idx.reshape(-1)
        a_w = top2_w.reshape(-1)
        tok_id = jnp.arange(2 * N) // 2
        counts = jnp.bincount(a_e, length=E)
        keep = counts <= cap
        valid = keep[a_e]
        onehot = jax.nn.one_hot(a_e, E, dtype=jnp.int32)
        pos = jnp.take_along_axis(jnp.cumsum(onehot, axis=0) - 1, a_e[:, None], axis=1)[:, 0]
        p = jnp.where(valid, jnp.minimum(pos, cap - 1), cap)
        x_a = x[tok_id]
        buf = jnp.zeros((E, cap + 1, H), dtype=x.dtype).at[a_e, p].set(x_a)
        h = jax.nn.silu(jnp.einsum('ech,efh->ecf', buf, w1) + b1[:, None, :])
        y = jnp.einsum('ecf,egf->ecg', h, w2) + b2[:, None, :]
        contrib = y[a_e, p] * (a_w * valid.astype(x.dtype))[:, None]
        out = contrib.reshape(N, 2, H).sum(axis=1)
        return out.reshape(B, S, H)

    def _L1_attn_ref(x, Wq, Wk, Wv, Wo, bo, rel_emb):
        import jax, jax.numpy as jnp
        import numpy as np
        NUM_HEADS = 16
        CLIP = 16
        b, s, d_in = x.shape
        h, hd = (NUM_HEADS, x.shape[-1] // NUM_HEADS)
        q = (x @ Wq).reshape(b, s, h, hd).transpose(0, 2, 1, 3)
        k = (x @ Wk).reshape(b, s, h, hd).transpose(0, 2, 1, 3)
        v = (x @ Wv).reshape(b, s, h, hd).transpose(0, 2, 1, 3)
        r = jnp.arange(s)
        dist = jnp.clip(jnp.abs(r[None, :] - r[:, None]), 0, CLIP)
        a_k = rel_emb[dist]
        scores = jnp.einsum('bhqd,bhkd->bhqk', q, k) * a_k
        causal = jnp.triu(jnp.ones((s, s), dtype=bool), k=1)
        scores = jnp.where(causal, -jnp.inf, scores)
        attn = jax.nn.softmax(scores / np.sqrt(hd), axis=-1)
        ctx = jnp.einsum('bhqk,bhkd->bhqd', attn, v)
        ctx = ctx.transpose(0, 2, 1, 3).reshape(b, s, h * hd)
        return ctx @ Wo + bo

    def _L1_xattn_ref(query, key, value, Wq, bq, Wk, bk, Wv, bv, Wo, bo):
        import jax, jax.numpy as jnp
        import numpy as np
        B, T, E, H = (4, 1024, 128, 16)
        D = E // H
        SCALE = 1.0 / np.sqrt(D).astype(np.float32)
        EPS_FM = 1e-06
        EPS_Z = 1e-08

        def _heads(x):
            b, t, _ = x.shape
            return x.reshape(b, t, H, D).transpose(0, 2, 1, 3)

        def _feature_map(x):
            return jax.nn.relu(x) + EPS_FM
        b, tq, _ = query.shape
        Q = _feature_map(_heads(query @ Wq.T + bq) * SCALE)
        K = _feature_map(_heads(key @ Wk.T + bk) * SCALE)
        V = _heads(value @ Wv.T + bv)
        KV = jnp.einsum('bhnd,bhne->bhde', K, V)
        K_sum = K.sum(axis=2)
        Z = jnp.einsum('bhnd,bhd->bhn', Q, K_sum) + EPS_Z
        out = jnp.einsum('bhnd,bhde->bhne', Q, KV) / Z[..., None]
        out = out.transpose(0, 2, 1, 3).reshape(b, tq, E)
        return out @ Wo.T + bo

    def _L1_ffn_ref(hidden_states, conf_w, conf_b, gate_w, up_w, down_w, wealth):
        import jax, jax.numpy as jnp
        import numpy as np
        E, K = (8, 2)
        x = hidden_states
        confidences = jax.nn.sigmoid(jnp.einsum('bsh,eh->bse', x, conf_w) + conf_b)
        bids = confidences * wealth
        top_bids, selected_experts = jax.lax.top_k(bids, K)
        sorted_bids = -jnp.sort(-bids, axis=-1)
        payments = jnp.broadcast_to(sorted_bids[..., K:K + 1], top_bids.shape)
        routing_weights = jax.nn.softmax(top_bids, axis=-1)
        combine = jnp.sum(jax.nn.one_hot(selected_experts, E, dtype=x.dtype) * routing_weights[..., None], axis=2)

        def ffn(gw, uw, dw):
            g = jnp.einsum('bsh,ih->bsi', x, gw)
            u = jnp.einsum('bsh,ih->bsi', x, uw)
            return jnp.einsum('bsi,hi->bsh', jax.nn.silu(g) * u, dw)
        expert_out = jax.vmap(ffn)(gate_w, up_w, down_w)
        output = jnp.einsum('ebsh,bse->bsh', expert_out, combine)
        return output
    x = x + _L0_attn_ref(_layernorm(x, axis=-1), L0_attn_QK, L0_attn_VO)
    x = x + _L0_xattn_ref(_layernorm(x, axis=-1), ctx_1024, ctx_1024, L0_xattn_Wq, L0_xattn_bq, L0_xattn_Wk, L0_xattn_bk, L0_xattn_Wv, L0_xattn_bv, L0_xattn_Wo, L0_xattn_bo)
    x = x + _L0_ffn_ref(_layernorm(x, axis=-1), L0_ffn_gate_w, L0_ffn_w1, L0_ffn_b1, L0_ffn_w2, L0_ffn_b2)
    x = x + _L1_attn_ref(_layernorm(x, axis=-1), L1_attn_Wq, L1_attn_Wk, L1_attn_Wv, L1_attn_Wo, L1_attn_bo, L1_attn_rel_emb)
    x = x + _L1_xattn_ref(_layernorm(x, axis=-1), ctx_1024, ctx_1024, L1_xattn_Wq, L1_xattn_bq, L1_xattn_Wk, L1_xattn_bk, L1_xattn_Wv, L1_xattn_bv, L1_xattn_Wo, L1_xattn_bo)
    x = x + _L1_ffn_ref(_layernorm(x, axis=-1), L1_ffn_conf_w, L1_ffn_conf_b, L1_ffn_gate_w, L1_ffn_up_w, L1_ffn_down_w, L1_ffn_wealth)
    return x

_drawn_inputs = setup_inputs


def setup_inputs(seed=0):
    import zlib

    import numpy as np

    out = dict(_drawn_inputs(seed))
    spreads = {'L0_xattn_bq': (0.0, 0.1),
     'L0_xattn_bk': (0.0, 2.0),
     'L0_xattn_bv': (0.0, 0.1),
     'L0_xattn_bo': (0.0, 0.1),
     'L1_ffn_conf_b': (0.0, 0.1),
     'L1_ffn_wealth': (1.0, 0.2)}
    factors = {'L0_ffn_b1': 61.499,
     'L0_ffn_b2': 53.901,
     'L1_attn_bo': 3.46,
     'L1_xattn_bq': 8.0,
     'L1_xattn_bk': 24.562,
     'L1_xattn_bv': 4.52,
     'L1_xattn_bo': 4.58}
    for name, (base, spread) in spreads.items():
        noise = np.random.default_rng([zlib.crc32(name.encode()), seed]).standard_normal(out[name].shape)
        drawn = base * np.exp(spread * noise) if base else spread * noise
        out[name] = jnp.asarray(drawn.astype(out[name].dtype))
    for name, factor in factors.items():
        out[name] = (out[name] * factor).astype(out[name].dtype)
    return out
```

```python
from contextlib import ExitStack

import numpy as np
import concourse.bass as bass
from concourse import mybir

P = 128
D = 128
B, T = 2, 512
NC = T // P
H, HD = 16, 8
TK = 77
HS, HPB = 18, 6
E = 8
I1 = 512
NI = I1 // P
CAP = int(1.25 * B * T / E)
CLIP = 16
WL = P + CLIP
NP3 = 3
KR = 9 * HD
NEAR2 = WL + P
BIG = -1e30

F32 = mybir.dt.float32
F32R = mybir.dt.float32r
BF16 = mybir.dt.bfloat16
ALU = mybir.AluOpType
ACT = mybir.ActivationFunctionType
AX = mybir.AxisListType

WEIGHTS = ["aQK", "aVO", "cWq", "cWk", "cWv", "cWo", "mG", "sWq", "sWk", "sWv", "sWo", "lWq", "lWk", "lWv", "lWo", "fG"]
WIDTH = {"mG": E, "fG": E}
ROWS = ["cbv", "cbo", "sbo", "lbk", "lbv", "lbo", "fb", "fw", "rel"]
RWIDTH = {"fb": E, "fw": E, "rel": CLIP + 1}
COLS = ["cbq", "cbk", "lbq"]
CONSTS = ["ident", "block", "dist", "lower", "heads", "mask"]
CWIDTH = {"dist": NEAR2, "mask": NEAR2, "lower": E * E, "heads": H}


PE_STEPS = ["k_ps", "a_proj", "a_proj", "k_ps", "a_o", "c_qps", "g_ps", "m_ct", "m_b", "q_ps", "q_ps", "q_ps",
    "l_qps", "l_nps", "g_ps"]
DVE_STEPS = ["k_sb", "a_v", "k_sb", "c_q", "g_sub", "g_sel", "g_comb", "q_src", "q_v", "q_r", "q_l", "o_fin", "l_q",
    "o_fin", "f_z", "f_bs", "f_comb"]
ACT_STEPS = ["a_q", "g_e", "m_ctr", "q_k", "q_h", "q_m", "f_ez", "f_eb"]


def offsets(names, widths):
    at, out = 0, {}
    for n in names:
        out[n] = (at, at + widths.get(n, D))
        at = out[n][1]
    return out, at


W_AT, W_ALL = offsets(WEIGHTS, WIDTH)
R_AT, R_ALL = offsets(ROWS, RWIDTH)
C_AT, C_ALL = offsets(CONSTS, CWIDTH)


def build(nc, d, out, stages=6):
    with ExitStack() as ctx:
        def sb(name, shape, dt=F32):
            return ctx.enter_context(nc.sbuf_tensor(name, shape, dt))

        def sem(name):
            return ctx.enter_context(nc.semaphore(name))

        def sems(name):
            return [sem(f"{name}{b}") for b in range(B)]

        both = range(B)
        wts = sb("wts", [P, W_ALL])
        rows = sb("rows", [P, R_ALL])
        cols = sb("cols", [P, len(COLS) + E])
        cst = sb("cst", [P, C_ALL])
        b2 = sb("b2", [E, D])
        ctxT = sb("ctxT", [P, B, TK])
        x = sb("x", [P, B, NC, D])
        xb = sb("xb", [P, B, NC, D])
        xn = sb("xn", [P, B, NC, D])
        xnT = sb("xnT", [P, B, T])
        xnTh = sb("xnTh", [P, B, T], F32R)
        xnTl = sb("xnTl", [P, B, T], F32R)
        stats = sb("stats", [P, B, NC, 6])
        mv = sb("mv", [P, B, NC, 2])
        vare = sb("vare", [P, B, NC])
        rstd = sb("rstd", [P, B, NC])
        mhalf = sb("mhalf", [P, NC])
        ones = sb("ones", [P, P])
        ps = ctx.enter_context(nc.psum_tensor("ps", [P, 2 * NC, 512], F32))

        W = {n: wts[:, a:b] for n, (a, b) in W_AT.items()}
        R = {n: rows[:, a:b] for n, (a, b) in R_AT.items()}
        C = {n: cst[:, a:b] for n, (a, b) in C_AT.items()}
        ident = C["ident"]

        def bank(b, i):
            return ps[:, NC * b + i, :]

        probT = sb("probT", [P, B, NC, T])
        cqT = sb("cqT", [P, B, T])
        o = sb("o", [P, B, NC, D])
        oT = sb("oT", [P, B, T])
        lkv = sb("lkv", [P, B, D + H])
        rz = sb("rz", [P, B, NC, H])
        lg = sb("lg", [P, B, NC, E])
        pe_ = sb("pe_", [P, B, NC, E])
        gm = sb("gm", [P, B, NC])
        gs = sb("gs", [P, B, NC])
        cmpg = sb("cmpg", [P, B, NC, E, E])
        cmpe = sb("cmpe", [P, B, NC, E, E])
        rank = sb("rank", [P, B, NC, E])
        sel = sb("sel", [P, B, NC, E])
        comb = sb("comb", [P, B, NC, E])
        maskb = sb("maskb", [P, NEAR2 + P], BF16)
        identb = maskb[:, NEAR2:]
        near = sb("near", [P, NEAR2])
        hit = sb("hit", [P, NEAR2])
        sva = sb("sva", [P, B, NC, H, HD + 1])
        snm = sb("snm", [P, 2, 4])

        outer, phase = ctx, ExitStack()
        ctx = phase
        xqkT = sb("xqkT", [P, B, T])
        xvo = sb("xvo", [P, B, NC, D])
        negm = sb("negm", [P, B, NC])
        rsum = sb("rsum", [P, B, NC])
        rinv = sb("rinv", [P, B, NC])
        prob = sb("prob", [P, B, NC, T])
        ckT = sb("ckT", [P, B, TK])
        ckb = sb("ckb", [P, B, HS, TK])
        cva = sb("cva", [TK, B, H, HD + 1])
        cmax = sb("cmax", [P, B, HS])
        shifted = prob[:, :, 0:3, :].rearrange("p b c t -> p b (c t)")[:, :, 0:HS * TK]
        cprob = sb("cprob", [P, B, HS * TK])
        cprobT = probT[0:TK, :, :, :]
        rden = sb("rden", [P, B, H])
        lk = sb("lk", [TK, B, D])
        lv = sb("lv", [TK, B, D])
        valid = sb("valid", [P, E])
        combT = sb("combT", [E, B, T])
        w12 = sb("w12", [P, 2, E, D])
        w12h = sb("w12h", [P, 2, E, D], F32R)
        w12l = sb("w12l", [P, 2, E, D], F32R)
        hid = sb("hid", [P, B, 2, T])
        hidh = sb("hidh", [P, B, 2, T], F32R)
        hidl = sb("hidl", [P, B, 2, T], F32R)
        phase.close()

        QS, QA, KK = range(3)
        src = sb("src", [P, 3, T])
        rest = sb("rest", [P, 3, T])
        third = sb("third", [P, NP3, 3, T], BF16)
        stack = sb("stack", [KR, B, 3, H, T], BF16)
        scratch = nc.dram_tensor("qk_thirds", (B, 3, H, NP3, HD, T), BF16).ap()
        sprob = probT[:, 1].rearrange("p (a j) t -> p a j t", a=2)
        sprobT = probT[:, 0]
        so = sb("so", [P, NC, H, HD + 1])
        phase.close()

        fw = sb("fw", [P, 2, 3 * I1])
        fwh = sb("fwh", [P, 2, 3 * I1], F32R)
        fwl = sb("fwl", [P, 2, 3 * I1], F32R)
        sg = sb("sg", [P, 2, T])
        fa = probT
        fah = sb("fah", [P, 2, NI, T], F32R)
        fal = sb("fal", [P, 2, NI, T], F32R)
        outer.push(phase)
        ctx = outer

        d_x = sem("d_x"); d_w = sem("d_w"); d_w12 = sem("d_w12"); d_out = sem("d_out")
        mask_ready = sem("mask_ready"); d_sc = sems("d_sc"); d_st = sems("d_st"); d_f = sems("d_f")
        consts = sem("consts")
        v_ones = sem("v_ones")
        dve_done = sem("dve_done")
        pool_done = sem("pool_done")
        var_ready, rstd_ready, xn_ready = sems("var_ready"), sems("rstd_ready"), sems("xn_ready")
        xnt_ps, xnt_ready, xnl_ready = sems("xnt_ps"), sems("xnt_ready"), sems("xnl_ready")
        x_ready, xb_ready = sems("x_ready"), sems("xb_ready")
        ot_ps, ot_ready, y_ps = sems("ot_ps"), sems("ot_ready"), sems("y_ps")

        pe_step, dve_step, act_step = sems("pe_step"), sems("dve_step"), sems("act_step")
        order = {}
        for names in (PE_STEPS, DVE_STEPS, ACT_STEPS):
            for i, name in enumerate(names):
                order.setdefault(name, []).append(i + 1)

        def after(name, n=1):
            return order[name][n - 1]

        k_ps = a_proj = a_o = c_qps = g_ps = m_ct = m_b = q_ps = l_qps = l_nps = pe_step
        k_sb = a_v = c_q = g_sub = g_sel = g_comb = q_src = q_v = q_r = q_l = o_fin = l_q = f_z = f_bs = f_comb = dve_step
        a_q = g_e = m_ctr = q_k = q_h = q_m = f_ez = f_eb = act_step

        a_s, a_m, a_e, a_t, a_pt = (sems(n) for n in ("a_s", "a_m", "a_e", "a_t", "a_pt"))
        c_s, c_sub, c_e, c_t, c_pt, c_o, c_on = (sems(n) for n in ("c_s", "c_sub", "c_e", "c_t", "c_pt", "c_o", "c_on"))
        g_cnt = sem("g_cnt")
        w12_split = sem("w12_split")
        m_hps, m_h, m_hh, m_hl, m_y, m_x = (sems(n) for n in ("m_hps", "m_h", "m_hh", "m_hl", "m_y", "m_x"))
        s_s, s_m, s_e, s_t, s_o, s_on = (sems(n) for n in ("s_s", "s_m", "s_e", "s_t", "s_o", "s_on"))
        s_pt = [[sem(f"s_pt{b}_{i}") for i in range(3)] for b in both]
        f_wh = sem("f_wh"); f_wl = sem("f_wl")
        f_g, f_u, f_s, f_a, f_ah, f_al, f_y, f_x = (sem(n) for n in (
            "f_g", "f_u", "f_s", "f_a", "f_ah", "f_al", "f_y", "f_x"))

        block = ctx.enter_context(nc.Block())

        def mm3(pe, dst, lh, ll, rh, rl, start=True, stop=True):
            pe.matmul(dst, lh, rh, start=start, stop=False)
            pe.matmul(dst, lh, rl, start=False, stop=False)
            return pe.matmul(dst, ll, rh, start=False, stop=stop)

        @block.sync
        def _(sp):
            for b in both:
                sp.dma_start(x[:, b], d["x"][b].rearrange("(c p) d -> p c d", p=P)).then_inc(d_x, 16)
            sp.dma_start(cst[:, :], d["cst"]).then_inc(d_w, 16)
            sp.dma_start(wts[:, :], d["wts"]).then_inc(d_w, 16)
            sp.dma_start(rows[:, :], d["rows"].partition_broadcast(P)).then_inc(d_w, 16)
            sp.dma_start(cols[:, :], d["cols"]).then_inc(d_w, 16)
            sp.dma_start(ctxT[:, :, :], d["ctxT"]).then_inc(d_w, 16)
            sp.dma_start(b2[:, :], d["b2"]).then_inc(d_w, 16)
            sp.dma_start(w12[:, :, :, :], d["w12"]).then_inc(d_w12, 16)
            if stages > 3:
                for b in both:
                    sp.wait_ge(q_l[b], after("q_l"))
                    for i in range(3):
                        for t in range(NP3):
                            sp.dma_start(scratch[b, i, :, t], third[:, t, i]).then_inc(d_sc[b], 16)
                    sp.wait_ge(d_sc[b], 16 * 9)
                    for i in range(3):
                        for r in range(NP3):
                            for u in range(NP3):
                                t = r if i != KK else u
                                sp.dma_start(stack[(NP3 * r + u) * HD:(NP3 * r + u + 1) * HD, b, i],
                                             scratch[b, i, :, t].rearrange("h d t -> d h t")).then_inc(d_st[b], 16)
            if stages > 5:
                for e in range(E):
                    if e >= 2:
                        sp.wait_ge(f_wl, e - 1)
                    sp.dma_start(fw[:, e % 2, 0:2 * I1], d["fgu"][:, e]).then_inc(d_f[e % 2], 16)
                    sp.dma_start(fw[:, e % 2, 2 * I1:], d["fdn"][:, e]).then_inc(d_f[e % 2], 16)
            for b in both:
                sp.wait_ge(x_ready[b], stages)
                sp.dma_start(out[b].rearrange("(c p) d -> p c d", p=P), x[:, b]).then_inc(d_out, 16)
            sp.wait_ge(d_out, 16 * B)
        WALL = 16 * 6

        @block.gpsimd
        def _(pool):
            links = [0]

            def link(ins):
                links[0] += 1
                ins.then_inc(pool_done, 1)
                pool.wait_ge(pool_done, links[0])

            pool.memset(mhalf[:, :], -0.5).then_inc(consts, 1)
            pool.memset(ones[:, :], 1.0).then_inc(consts, 1)
            pool.memset(ckb[:, :, H:HS, :], 0.0).then_inc(consts, 1)
            pool.memset(cva[:, :, :, HD:HD + 1], 1.0).then_inc(consts, 1)
            pool.wait_ge(consts, 4)
            pool.memset(sva[:, :, :, :, HD:HD + 1], 1.0).then_inc(v_ones, 1)

            def rstds(k, b):
                pool.wait_ge(var_ready[b], k + 1)
                link(pool.tensor_scalar(vare[:, b, :], mv[:, b, :, 1], 1e-5, None, ALU.add))
                pool.tensor_tensor(rstd[:, b, :], vare[:, b, :], mhalf[:, :], ALU.pow).then_inc(rstd_ready[b], 1)

            def add_bias(k, b, row):
                if k:
                    pool.wait_ge(x_ready[b], k)
                pool.tensor_tensor(xb[:, b], x[:, b], R[row].unsqueeze(1).broadcast_to([P, NC, D]),
                                   ALU.add).then_inc(xb_ready[b], 1)

            for b in both:
                rstds(0, b)
            if stages > 3:
                pool.wait_ge(d_w, WALL)
                pool.tensor_copy(maskb[:, 0:NEAR2], C["mask"]).then_inc(mask_ready, 1)
                pool.tensor_copy(identb, ident).then_inc(mask_ready, 1)
                dist = C["dist"]
                link(pool.tensor_scalar(near[:, :], dist, -1.0, None, ALU.is_equal))
                for k in range(CLIP + 1):
                    link(pool.tensor_scalar(hit[:, :], dist, float(k), R["rel"][:, k:k + 1], ALU.is_equal, ALU.mult))
                    link(pool.tensor_tensor(near[:, :], near[:, :], hit[:, :], ALU.add))
            if stages > 1:
                for b in both:
                    rstds(1, b)
                    add_bias(1, b, "cbo")
                pool.wait_ge(d_w12, 16)
                link(pool.tensor_copy(w12h[:, :, :, :], w12[:, :, :, :]))
                pool.tensor_tensor(w12l[:, :, :, :], w12[:, :, :, :], w12h[:, :, :, :].bitcast(F32),
                                   ALU.subtract).then_inc(w12_split, 1)
            if stages > 2:
                for b in both:
                    rstds(2, b)
                for e in range(E):
                    for b in both:
                        pool.wait_ge(m_hh[b], e + 1)
                        if e >= 2:
                            pool.wait_ge(m_y[b], e - 1)
                        pool.tensor_tensor(hidl[:, b, e % 2], hid[:, b, e % 2], hidh[:, b, e % 2].bitcast(F32),
                                           ALU.subtract).then_inc(m_hl[b], 1)
            if stages > 3:
                for b in both:
                    rstds(3, b)
                    add_bias(3, b, "sbo")
            if stages > 4:
                for b in both:
                    rstds(4, b)
                    add_bias(4, b, "lbo")
            if stages > 5:
                for b in both:
                    rstds(5, b)
                for n_ in range(E * B * NI):
                    k, i = divmod(n_, NI)
                    pool.wait_ge(f_ah, n_ + 1)
                    if k >= 2:
                        pool.wait_ge(f_y, k - 1)
                    pool.tensor_tensor(fal[:, k % 2, i], fa[:, k % 2, i], fah[:, k % 2, i].bitcast(F32),
                                       ALU.subtract).then_inc(f_al, 1)

        @block.scalar
        def _(act):
            def xnt(k, b):
                act.wait_ge(xnt_ps[b], k + 1)
                act.activation(xnT[:, b], bank(b, 0), ACT.Copy).then_inc(xnt_ready[b], 1)

            def ot(n, b, i):
                act.wait_ge(ot_ps[b], n + 1)
                act.activation(oT[:, b], bank(b, i), ACT.Copy).then_inc(ot_ready[b], 1)

            for b in both:
                xnt(0, b)
            for b in both:
                act.wait_ge(a_proj[b], after("a_proj"))
                act.activation(xqkT[:, b], bank(b, 1), ACT.Copy, scale=float(D) ** -0.5).then_inc(a_q[b], 1)
            for b in both:
                for c in range(NC):
                    act.wait_ge(a_m[b], c + 1)
                    act.activation(prob[:, b, c], bank(b, SBANK[c]), ACT.Exp, bias=negm[:, b, c:c + 1],
                                   accum_out=rsum[:, b, c:c + 1]).then_inc(a_e[b], 1)
            for b in both:
                for u in (0, 2):
                    act.wait_ge(a_t[b], u + 1)
                    act.activation(probT[:, b, u], bank(b, SBANK[u]), ACT.Copy).then_inc(a_pt[b], 1)
            if stages > 1:
                for b in both:
                    xnt(1, b)
                for c in range(NC):
                    for b in both:
                        act.wait_ge(c_sub[b], c + 1)
                        act.activation(cprob[:, b], shifted[:, b], ACT.Exp).then_inc(c_e[b], 1)
                    for b in both:
                        for u in (0, 2):
                            act.wait_ge(c_t[b], NC * c + u + 1)
                            act.activation(cprobT[:, b, u], bank(b, TBANK[u])[0:TK, :], ACT.Copy).then_inc(c_pt[b], 1)
                for b in both:
                    ot(0, b, 0)
            if stages > 2:
                for b in both:
                    xnt(2, b)
                    act.activation(xnTh[:, b], bank(b, 0), ACT.Copy).then_inc(xnl_ready[b], 1)
                for b in both:
                    act.wait_ge(g_sub[b], after("g_sub"))
                    act.activation(pe_[:, b], lg[:, b], ACT.Exp).then_inc(g_e[b], 1)
                for e in range(E):
                    for b in both:
                        act.wait_ge(m_hps[b], e + 1)
                        if e >= 2:
                            act.wait_ge(m_hl[b], e - 1)
                            act.wait_ge(m_y[b], e - 1)
                        act.activation(hid[:, b, e % 2], bank(b, e % 2), ACT.Silu,
                                       bias=cols[:, len(COLS) + e:len(COLS) + e + 1]).then_inc(m_h[b], 1)
                        act.wait_ge(m_h[b], e + 1)
                        act.activation(hidh[:, b, e % 2], hid[:, b, e % 2], ACT.Copy).then_inc(m_hh[b], 1)
                for b in both:
                    act.wait_ge(m_ct[b], after("m_ct"))
                    act.activation(combT[:, b], bank(b, 0)[0:E, :], ACT.Copy).then_inc(m_ctr[b], 1)
            if stages > 3:
                for b in both:
                    xnt(3, b)
                for b in both:
                    act.wait_ge(q_ps[b], after("q_ps", 2))
                    if b:
                        act.wait_ge(q_l[b - 1], after("q_l"))
                    act.activation(src[:, KK], bank(b, 2), ACT.Copy).then_inc(q_k[b], 1)
                    act.wait_ge(q_k[b], after("q_k"))
                    act.wait_ge(q_src[b], after("q_src"))
                    if b:
                        act.wait_ge(d_sc[b - 1], 16 * 9)
                    act.activation(third[:, 0], src[:, :], ACT.Copy).then_inc(q_h[b], 1)
                    act.wait_ge(q_r[b], after("q_r"))
                    act.activation(third[:, 1], rest[:, :], ACT.Copy).then_inc(q_m[b], 1)
                for b in both:
                    def exps(n):
                        kind, par = n % 3, n % 2
                        act.wait_ge(s_m[b], n + 1)
                        if n >= 2:
                            act.wait_ge(s_t[b], 2 * (n - 1))
                        elif b:
                            act.wait_ge(s_t[b - 1], 2 * (GROUPS - 1 + n))
                        for j in range(2):
                            for at, w, m in GROUP[kind]:
                                last = act.activation(sprob[:, par, j, at:at + w], ps[:, 2 * par + j, at:at + w], ACT.Exp,
                                                      bias=snm[:, par, m + j:m + j + 1])
                        last.then_inc(s_e[b], 1)

                    def evac(m):
                        if m % 3 == 1:
                            return
                        act.wait_ge(s_t[b], m + 1)
                        if m >= 4:
                            act.wait_ge(s_o[b], m - 3)
                        w = UNIT[m // 2 % 3]
                        act.activation(sprobT[:, m % 4, 0:w], ps[:, 4 + m % 3, 0:w], ACT.Copy).then_inc(s_pt[b][m % 3], 1)

                    for n in range(GROUPS):
                        exps(n)
                        if n:
                            evac(2 * n - 2)
                            evac(2 * n - 1)
                    evac(2 * GROUPS - 2)
                    evac(2 * GROUPS - 1)
                for b in both:
                    ot(1, b, 0)
            if stages > 4:
                for b in both:
                    xnt(4, b)
                for b in both:
                    ot(2, b, 0)
            if stages > 5:
                for b in both:
                    xnt(5, b)
                    act.activation(xnTh[:, b], bank(b, 0), ACT.Copy).then_inc(xnl_ready[b], 1)
                for b in both:
                    act.wait_ge(f_z[b], after("f_z"))
                    act.activation(pe_[:, b], lg[:, b], ACT.Exp, scale=-1.0).then_inc(f_ez[b], 1)
                for b in both:
                    act.wait_ge(f_bs[b], after("f_bs"))
                    act.activation(pe_[:, b], lg[:, b], ACT.Exp).then_inc(f_eb[b], 1)

                def ah(n_):
                    k, i = divmod(n_, NI)
                    act.wait_ge(f_a, n_ + 1)
                    if k >= 2:
                        act.wait_ge(f_y, k - 1)
                    act.activation(fah[:, k % 2, i], fa[:, k % 2, i], ACT.Copy).then_inc(f_ah, 1)

                def wh(e):
                    act.wait_ge(d_f[e % 2], 32 * (e // 2 + 1))
                    if e >= 2:
                        act.wait_ge(f_y, B * (e - 1))
                    act.activation(fwh[:, e % 2], fw[:, e % 2], ACT.Copy).then_inc(f_wh, 1)

                wh(0)
                wh(1)
                for n_ in range(E * B * NI):
                    e, k = n_ // (B * NI), n_ // NI
                    if n_ % (B * NI) == NI + 1 and 1 <= e < E - 1:
                        wh(e + 1)
                    act.wait_ge(f_g, n_ + 1)
                    if n_ >= 2:
                        act.wait_ge(f_a, n_ - 1)
                    act.activation(sg[:, n_ % 2], ps[:, 2 * (n_ % 2)], ACT.Silu).then_inc(f_s, 1)
                    if n_:
                        ah(n_ - 1)
                ah(E * B * NI - 1)

        @block.vector
        def _(dve):
            links = [0]

            def link(ins):
                links[0] += 1
                ins.then_inc(dve_done, 1)
                dve.wait_ge(dve_done, links[0])

            def norm_stats(k, b):
                if k:
                    dve.wait_ge(x_ready[b], k)
                for c in range(NC):
                    last = dve.bn_stats(stats[:, b, c], x[:, b, c])
                link(last)
                for c in range(NC):
                    last = dve.bn_aggr(mv[:, b, c], stats[:, b, c])
                last.then_inc(var_ready[b], 1)

            def norm_apply(k, b):
                dve.wait_ge(rstd_ready[b], k + 1)
                for c in range(NC):
                    last = dve.tensor_scalar(xn[:, b, c], x[:, b, c], mv[:, b, c, 0:1], rstd[:, b, c:c + 1],
                                             ALU.subtract, ALU.mult)
                last.then_inc(xn_ready[b], 1)

            def tail(n_, b, i):
                dve.wait_ge(xb_ready[b], n_ + 1)
                dve.wait_ge(y_ps[b], n_ + 1)
                dve.tensor_tensor(x[:, b].rearrange("p c d -> p (c d)"), bank(b, i),
                                  xb[:, b].rearrange("p c d -> p (c d)"), ALU.add).then_inc(x_ready[b], 1)

            dve.wait_ge(d_x, 16 * B)
            for b in both:
                norm_stats(0, b)
            for b in both:
                norm_apply(0, b)
            dve.wait_ge(d_w, WALL)
            for b in both:
                dve.wait_ge(k_ps[b], after("k_ps"))
                link(dve.tensor_scalar(ckT[:, b], bank(b, 3)[:, 0:TK], cols[:, 1:2], None, ALU.add))
                dve.tensor_tensor(ckb[:, b, 0:H], ckT[:, b].unsqueeze(1).broadcast_to([P, H, TK]),
                                  C["heads"].unsqueeze(2).broadcast_to([P, H, TK]), ALU.mult)
                dve.tensor_tensor(cva[:, b, :, 0:HD], bank(b, 3)[0:TK, 128:256].rearrange("p (h e) -> p h e", e=HD),
                                  R["cbv"][0:TK, :].rearrange("p (h e) -> p h e", e=HD), ALU.add)
                link(dve.tensor_tensor(lk[:, b], bank(b, 3)[0:TK, 256:384], R["lbk"][0:TK, :], ALU.add))
                link(dve.tensor_scalar(lk[:, b], lk[:, b], float(HD) ** -0.5, 0.0, ALU.mult, ALU.max))
                dve.tensor_scalar(lk[:, b], lk[:, b], 1e-6, None, ALU.add)
                dve.tensor_tensor(lv[:, b], bank(b, 3)[0:TK, 384:512], R["lbv"][0:TK, :], ALU.add).then_inc(k_sb[b], 1)
            for b in both:
                dve.wait_ge(a_proj[b], after("a_proj", 2))
                dve.tensor_copy(xvo[:, b].rearrange("p c d -> p (c d)"), bank(b, 2)).then_inc(a_v[b], 1)
            for b in both:
                dve.wait_ge(k_ps[b], after("k_ps", 2))
                dve.tensor_tensor(lkv[:, b, 0:D], bank(b, 3)[:, 0:D], C["block"], ALU.mult)
                dve.tensor_tensor(lkv[:, b, D:D + H], bank(b, 3)[:, D:D + H], C["heads"], ALU.mult).then_inc(k_sb[b], 1)
            for b in both:
                for c in range(NC):
                    dve.wait_ge(a_s[b], c + 1)
                    dve.tensor_reduce(negm[:, b, c:c + 1], bank(b, SBANK[c]), AX.X, ALU.max, negate=True)\
                        .then_inc(a_m[b], 1)
            for b in both:
                dve.wait_ge(a_e[b], NC)
                link(dve.reciprocal(rinv[:, b], rsum[:, b]))
                for u in (1, 3):
                    dve.wait_ge(a_t[b], u + 1)
                    dve.tensor_copy(probT[:, b, u], bank(b, SBANK[u])).then_inc(a_pt[b], 1)
            for b in both:
                dve.wait_ge(a_o[b], after("a_o"))
                for c in range(NC):
                    last = dve.scalar_tensor_tensor(x[:, b, c], bank(b, 0)[:, c * D:(c + 1) * D], rinv[:, b, c:c + 1],
                                                    x[:, b, c], ALU.mult, ALU.add)
                last.then_inc(x_ready[b], 1)

            if stages > 1:
                for b in both:
                    norm_stats(1, b)
                for b in both:
                    norm_apply(1, b)
                for b in both:
                    dve.wait_ge(c_qps[b], after("c_qps"))
                    dve.tensor_scalar(cqT[:, b], bank(b, 1), cols[:, 0:1], float(HD) ** -0.5, ALU.add, ALU.mult)\
                        .then_inc(c_q[b], 1)
                for c in range(NC):
                    for b in both:
                        s3 = ps[:, NC * b:NC * b + 3, 0:HPB * TK].rearrange("p a (h k) -> p a h k", k=TK)
                        m3 = cmax[:, b].rearrange("p (a h) -> p a h", h=HPB)
                        dve.wait_ge(c_s[b], c + 1)
                        link(dve.tensor_reduce(m3, s3, AX.X, ALU.max))
                        dve.tensor_tensor(shifted[:, b].rearrange("p (a h k) -> p a h k", h=HPB, k=TK), s3,
                                          m3.unsqueeze(3).broadcast_to([P, 3, HPB, TK]), ALU.subtract)\
                            .then_inc(c_sub[b], 1)
                    for b in both:
                        for u in (1, 3):
                            dve.wait_ge(c_t[b], NC * c + u + 1)
                            dve.tensor_copy(cprobT[:, b, u], bank(b, TBANK[u])[0:TK, :]).then_inc(c_pt[b], 1)
                    for b in both:
                        dve.wait_ge(c_o[b], c + 1)
                        o9 = bank(b, 3)[:, 0:H * (HD + 1)].rearrange("p (h e) -> p h e", e=HD + 1)
                        link(dve.reciprocal(rden[:, b], o9[:, :, HD]))
                        dve.tensor_tensor(o[:, b, c].rearrange("p (h e) -> p h e", e=HD), o9[:, :, 0:HD],
                                          rden[:, b].unsqueeze(2).broadcast_to([P, H, HD]), ALU.mult)\
                            .then_inc(c_on[b], 1)
                for b in both:
                    tail(0, b, 1)

            def ranks(b, v):
                other = v.unsqueeze(2).broadcast_to([P, NC, E, E])
                mine = v.unsqueeze(3).broadcast_to([P, NC, E, E])
                low = C["lower"].rearrange("p (i j) -> p i j", j=E).unsqueeze(1).broadcast_to([P, NC, E, E])
                dve.tensor_tensor(cmpg[:, b], other, mine, ALU.is_gt)
                link(dve.tensor_tensor(cmpe[:, b], other, mine, ALU.is_equal))
                link(dve.tensor_tensor(cmpe[:, b], cmpe[:, b], low, ALU.mult))
                link(dve.tensor_tensor(cmpg[:, b], cmpg[:, b], cmpe[:, b], ALU.add))
                link(dve.tensor_reduce(rank[:, b], cmpg[:, b], AX.X, ALU.add))
                return dve.tensor_scalar(sel[:, b], rank[:, b], 1.5, None, ALU.is_lt)

            def per_chunk(v):
                return v.unsqueeze(2).broadcast_to([P, NC, E])

            if stages > 2:
                for b in both:
                    norm_stats(2, b)
                for b in both:
                    norm_apply(2, b)
                for b in both:
                    dve.wait_ge(xnl_ready[b], 1)
                    dve.tensor_tensor(xnTl[:, b], xnT[:, b], xnTh[:, b].bitcast(F32), ALU.subtract).then_inc(xnl_ready[b], 1)
                for b in both:
                    g = bank(b, 3)[:, 0:NC * E].rearrange("p (c e) -> p c e", e=E)
                    dve.wait_ge(g_ps[b], after("g_ps"))
                    link(dve.tensor_reduce(gm[:, b], g, AX.X, ALU.max))
                    dve.tensor_tensor(lg[:, b], g, per_chunk(gm[:, b]), ALU.subtract).then_inc(g_sub[b], 1)
                for b in both:
                    dve.wait_ge(g_e[b], after("g_e"))
                    link(dve.tensor_reduce(gs[:, b], pe_[:, b], AX.X, ALU.add))
                    link(dve.reciprocal(gm[:, b], gs[:, b]))
                    link(dve.tensor_tensor(pe_[:, b], pe_[:, b], per_chunk(gm[:, b]), ALU.mult))
                    ranks(b, pe_[:, b]).then_inc(g_sel[b], 1)
                dve.wait_ge(g_cnt, 1)
                link(dve.tensor_scalar(valid[:, :], bank(0, 3)[:, 64:64 + E], CAP + 0.5, None, ALU.is_lt))
                for b in both:
                    link(dve.tensor_tensor(comb[:, b], pe_[:, b], sel[:, b], ALU.mult))
                    dve.tensor_tensor(comb[:, b], comb[:, b], valid[:, :].unsqueeze(1).broadcast_to([P, NC, E]),
                                      ALU.mult).then_inc(g_comb[b], 1)
                for b in both:
                    dve.wait_ge(g_comb[b], after("g_comb"))
                for e in range(E):
                    for b in both:
                        dve.wait_ge(m_y[b], e + 1)
                        if e:
                            dve.wait_ge(m_x[b], e)
                        for c in range(NC):
                            last = dve.scalar_tensor_tensor(x[:, b, c], bank(b, 2 + e % 2)[:, c * D:(c + 1) * D],
                                                            comb[:, b, c, e:e + 1], x[:, b, c], ALU.mult, ALU.add)
                        last.then_inc(m_x[b], 1)
                for b in both:
                    dve.wait_ge(m_b[b], after("m_b"))
                    dve.wait_ge(m_x[b], E)
                    dve.tensor_tensor(x[:, b].rearrange("p c d -> p (c d)"), bank(b, 1),
                                      x[:, b].rearrange("p c d -> p (c d)"), ALU.add).then_inc(x_ready[b], 1)
            if stages > 3:
                for b in both:
                    norm_stats(3, b)
                for b in both:
                    norm_apply(3, b)
                dve.wait_ge(v_ones, 1)
                for b in both:
                    dve.wait_ge(q_ps[b], after("q_ps"))
                    if b:
                        dve.wait_ge(q_l[b - 1], after("q_l"))
                    link(dve.tensor_scalar(src[:, QS], bank(b, 1), float(HD) ** -0.5, None, ALU.mult))
                    dve.tensor_scalar(src[:, QA], src[:, QS], R["rel"][:, CLIP:CLIP + 1], None, ALU.mult).then_inc(q_src[b], 1)
                    dve.wait_ge(q_ps[b], after("q_ps", 3))
                    dve.tensor_copy(sva[:, b, :, :, 0:HD], bank(b, 3).rearrange("p (c h e) -> p c h e", h=H, e=HD))\
                        .then_inc(q_v[b], 1)
                    dve.wait_ge(q_h[b], after("q_h"))
                    dve.tensor_tensor(rest[:, :], src[:, :], third[:, 0], ALU.subtract).then_inc(q_r[b], 1)
                    dve.wait_ge(q_m[b], after("q_m"))
                    dve.tensor_tensor(third[:, 2], rest[:, :], third[:, 1], ALU.subtract).then_inc(q_l[b], 1)
                dve.wait_ge(pool_done, NEAR_LINKS)
                for b in both:
                    def maxes(n):
                        kind, par = n % 3, n % 2
                        dve.wait_ge(s_s[b], n + 1)
                        at, w = NEARCOLS[kind]
                        two = ps[:, 2 * par:2 * par + 2, :]
                        link(dve.tensor_tensor(two[:, :, at:at + w], two[:, :, at:at + w],
                                               near[:, 0:w].unsqueeze(1).broadcast_to([P, 2, w]), ALU.mult))
                        for at, w, m in GROUP[kind]:
                            last = dve.tensor_reduce(snm[:, par, m:m + 2], two[:, :, at:at + w], AX.X, ALU.max, negate=True)
                        last.then_inc(s_m[b], 1)

                    def evac(m):
                        if m % 3 != 1:
                            return
                        dve.wait_ge(s_t[b], m + 1)
                        if m >= 4:
                            dve.wait_ge(s_o[b], m - 3)
                        w = UNIT[m // 2 % 3]
                        dve.tensor_copy(sprobT[:, m % 4, 0:w], ps[:, 4 + m % 3, 0:w]).then_inc(s_pt[b][m % 3], 1)

                    def outputs(q):
                        dve.wait_ge(s_o[b], 12 * (q + 1))
                        dve.tensor_copy(so[:, :, 4 * q:4 * q + 4, :],
                                        ps[:, 7, 0:16 * 9].rearrange("p (h c e) -> p c h e", c=NC, e=9)).then_inc(s_on[b], 1)

                    for n in range(GROUPS):
                        maxes(n)
                        if n:
                            evac(2 * n - 2)
                            evac(2 * n - 1)
                        if n > 6 and n % 6 == 1:
                            outputs(n // 6 - 1)
                    evac(2 * GROUPS - 2)
                    evac(2 * GROUPS - 1)
                    outputs(3)
                    dve.wait_ge(s_on[b], 4)
                    link(dve.reciprocal(rz[:, b], so[:, :, :, HD]))
                    for c in range(NC):
                        last = dve.tensor_tensor(o[:, b, c].rearrange("p (h e) -> p h e", e=HD), so[:, c, :, 0:HD],
                                                 rz[:, b, c].unsqueeze(2).broadcast_to([P, H, HD]), ALU.mult)
                    last.then_inc(o_fin[b], 1)
                for b in both:
                    tail(1, b, 1)
            if stages > 4:
                for b in both:
                    norm_stats(4, b)
                for b in both:
                    norm_apply(4, b)
                for b in both:
                    dve.wait_ge(l_qps[b], after("l_qps"))
                    link(dve.tensor_scalar(cqT[:, b], bank(b, 1), cols[:, 2:3], float(HD) ** -0.5, ALU.add, ALU.mult))
                    dve.tensor_scalar(cqT[:, b], cqT[:, b], 0.0, 1e-6, ALU.max, ALU.add).then_inc(l_q[b], 1)
                for b in both:
                    dve.wait_ge(l_nps[b], after("l_nps"))
                    two = ps[:, NC * b + 2:NC * b + 4, 0:2 * (D + H)].rearrange("p a (c n) -> p a c n", n=D + H)
                    link(dve.tensor_scalar(rz[:, b].rearrange("p (a c) h -> p a c h", c=2), two[:, :, :, D:], 1e-8, None, ALU.add))
                    link(dve.reciprocal(rz[:, b], rz[:, b]))
                    for c in range(NC):
                        last = dve.tensor_tensor(o[:, b, c].rearrange("p (h e) -> p h e", e=HD),
                                                 two[:, c // 2, c % 2, 0:D].rearrange("p (h e) -> p h e", e=HD),
                                                 rz[:, b, c].unsqueeze(2).broadcast_to([P, H, HD]), ALU.mult)
                    last.then_inc(o_fin[b], 1)
                for b in both:
                    tail(2, b, 1)
            if stages > 5:
                for b in both:
                    norm_stats(5, b)
                for b in both:
                    norm_apply(5, b)
                for b in both:
                    dve.wait_ge(xnl_ready[b], 3)
                    dve.tensor_tensor(xnTl[:, b], xnT[:, b], xnTh[:, b].bitcast(F32), ALU.subtract).then_inc(xnl_ready[b], 1)

                def each(v):
                    return v.unsqueeze(1).broadcast_to([P, NC, E])

                for b in both:
                    dve.wait_ge(g_ps[b], after("g_ps", 2))
                    dve.tensor_tensor(lg[:, b], bank(b, 3)[:, 0:NC * E].rearrange("p (c e) -> p c e", e=E), each(R["fb"]),
                                      ALU.add).then_inc(f_z[b], 1)
                for b in both:
                    dve.wait_ge(f_ez[b], after("f_ez"))
                    link(dve.tensor_scalar(lg[:, b], pe_[:, b], 1.0, None, ALU.add))
                    link(dve.reciprocal(lg[:, b], lg[:, b]))
                    link(dve.tensor_tensor(lg[:, b], lg[:, b], each(R["fw"]), ALU.mult))
                    link(ranks(b, lg[:, b]))
                    link(dve.tensor_reduce(gm[:, b], lg[:, b], AX.X, ALU.max))
                    dve.tensor_tensor(lg[:, b], lg[:, b], per_chunk(gm[:, b]), ALU.subtract).then_inc(f_bs[b], 1)
                for b in both:
                    dve.wait_ge(f_eb[b], after("f_eb"))
                    link(dve.tensor_tensor(comb[:, b], pe_[:, b], sel[:, b], ALU.mult))
                    link(dve.tensor_reduce(gs[:, b], comb[:, b], AX.X, ALU.add))
                    link(dve.reciprocal(gs[:, b], gs[:, b]))
                    dve.tensor_tensor(comb[:, b], comb[:, b], per_chunk(gs[:, b]), ALU.mult).then_inc(f_comb[b], 1)
                    dve.wait_ge(f_comb[b], after("f_comb"))

                def wl(e):
                    dve.wait_ge(f_wh, e + 1)
                    if e >= 2:
                        dve.wait_ge(f_y, B * (e - 1))
                    dve.tensor_tensor(fwl[:, e % 2], fw[:, e % 2], fwh[:, e % 2].bitcast(F32), ALU.subtract).then_inc(f_wl, 1)

                def add_expert(k):
                    e, b = divmod(k, B)
                    dve.wait_ge(f_y, k + 1)
                    if k >= 2:
                        dve.wait_ge(f_x, k - 1)
                    for c in range(NC):
                        last = dve.scalar_tensor_tensor(x[:, b, c], ps[:, 4 + k % 4, c * D:(c + 1) * D],
                                                        comb[:, b, c, e:e + 1], x[:, b, c], ALU.mult, ALU.add)
                    last.then_inc(f_x, 1)

                wl(0)
                wl(1)
                for n_ in range(E * B * NI):
                    k, i = divmod(n_, NI)
                    e = k // B
                    if n_ % (B * NI) == NI + 1 and 1 <= e < E - 1:
                        wl(e + 1)
                    dve.wait_ge(f_u, n_ + 1)
                    dve.wait_ge(f_s, n_ + 1)
                    if k >= 2:
                        dve.wait_ge(f_al, n_ - 2 * NI + 1)
                    dve.tensor_tensor(fa[:, k % 2, i], sg[:, n_ % 2], ps[:, 2 * (n_ % 2) + 1], ALU.mult).then_inc(f_a, 1)
                    if i == 2 and k >= 2:
                        add_expert(k - 2)
                add_expert(E * B - 2)
                add_expert(E * B - 1)
                dve.wait_ge(f_x, E * B)
                for b in both:
                    dve.engine_nop().then_inc(x_ready[b], 1)

        @block.tensor
        def _(pe):
            def xnt(k, b):
                pe.wait_ge(xn_ready[b], k + 1)
                for c in range(NC):
                    last = pe.transpose(bank(b, 0)[:, c * P:(c + 1) * P], xn[:, b, c], ident)
                last.then_inc(xnt_ps[b], 1)

            def ot(n_, b, i):
                for c in range(NC):
                    last = pe.transpose(bank(b, i)[:, c * P:(c + 1) * P], o[:, b, c], ident)
                last.then_inc(ot_ps[b], 1)

            def wo(n_, b, i, w):
                pe.wait_ge(ot_ready[b], n_ + 1)
                for c in range(NC):
                    last = pe.matmul(bank(b, i)[:, c * D:(c + 1) * D], oT[:, b, c * P:(c + 1) * P], W[w],
                                     start=True, stop=True)
                last.then_inc(y_ps[b], 1)

            pe.wait_ge(consts, 4)
            pe.wait_ge(d_w, WALL)
            for b in both:
                xnt(0, b)
            for b in both:
                pe.matmul(bank(b, 3)[:, 0:TK], W["cWk"], ctxT[:, b], start=True, stop=True)
                for i, w in enumerate(("cWv", "lWk", "lWv")):
                    last = pe.matmul(bank(b, 3)[0:TK, (i + 1) * 128:(i + 2) * 128], ctxT[:, b], W[w], start=True, stop=True)
                last.then_inc(k_ps[b], 1)
            for b in both:
                pe.wait_ge(xnt_ready[b], 1)
                pe.matmul(bank(b, 1), W["aQK"], xnT[:, b], start=True, stop=True).then_inc(a_proj[b], 1)
                for c in range(NC):
                    last = pe.matmul(bank(b, 2)[:, c * D:(c + 1) * D], xnT[:, b, c * P:(c + 1) * P], W["aVO"],
                                     start=True, stop=True)
                last.then_inc(a_proj[b], 1)
            for b in both:
                pe.wait_ge(k_sb[b], after("k_sb"))
                pe.matmul(bank(b, 3)[:, 0:D], lk[:, b], lv[:, b], start=True, stop=True)
                pe.matmul(bank(b, 3)[:, D:D + H], lk[:, b], ones[0:TK, 0:H], start=True, stop=True).then_inc(k_ps[b], 1)
            for b in both:
                pe.wait_ge(a_q[b], after("a_q"))
                for c in range(NC):
                    if SBANK[c] == 2:
                        pe.wait_ge(a_v[b], after("a_v"))
                    if SBANK[c] == 3:
                        pe.wait_ge(k_sb[b], after("k_sb", 2))
                    pe.matmul(bank(b, SBANK[c]), xqkT[:, b, c * P:(c + 1) * P], xnT[:, b], start=True, stop=True)\
                        .then_inc(a_s[b], 1)
            for b in both:
                pe.wait_ge(a_e[b], NC)
                for u in range(NC):
                    for c in range(NC):
                        last = pe.transpose(bank(b, SBANK[u])[:, c * P:(c + 1) * P], prob[:, b, c, u * P:(u + 1) * P], ident)
                    last.then_inc(a_t[b], 1)
            for b in both:
                pe.wait_ge(a_pt[b], NC)
                for c in range(NC):
                    for u in range(NC):
                        last = pe.matmul(bank(b, 0)[:, c * D:(c + 1) * D], probT[:, b, u, c * P:(c + 1) * P], xvo[:, b, u],
                                         start=(u == 0), stop=(u == NC - 1))
                last.then_inc(a_o[b], 1)

            if stages > 1:
                for b in both:
                    xnt(1, b)
                for b in both:
                    pe.wait_ge(xnt_ready[b], 2)
                    pe.matmul(bank(b, 1), W["cWq"], xnT[:, b], start=True, stop=True).then_inc(c_qps[b], 1)
                for c in range(NC):
                    for b in both:
                        if c == 0:
                            pe.wait_ge(c_q[b], after("c_q"))
                        else:
                            pe.wait_ge(c_pt[b], NC * c)
                        for a in range(3):
                            last = pe.matmul(bank(b, a)[:, 0:HPB * TK], cqT[:, b, c * P:(c + 1) * P],
                                             ckb[:, b, a * HPB:(a + 1) * HPB].rearrange("p h k -> p (h k)"),
                                             start=True, stop=True)
                        last.then_inc(c_s[b], 1)
                    for b in both:
                        pe.wait_ge(c_e[b], c + 1)
                        if c:
                            pe.wait_ge(c_on[b], c)
                        for u in range(NC):
                            for j in range(NC):
                                h = NC * u + j
                                last = pe.transpose(bank(b, TBANK[u])[0:TK, j * P:(j + 1) * P],
                                                    cprob[:, b, h * TK:(h + 1) * TK], ident)
                            last.then_inc(c_t[b], 1)
                    for b in both:
                        pe.wait_ge(c_pt[b], NC * (c + 1))
                        for h in range(H):
                            last = pe.matmul(bank(b, 3)[:, h * 9:h * 9 + 9], cprobT[:, b, h // NC, (h % NC) * P:(h % NC + 1) * P],
                                             cva[:, b, h], start=True, stop=True)
                        last.then_inc(c_o[b], 1)
                for b in both:
                    pe.wait_ge(c_on[b], NC)
                    ot(0, b, 0)
                for b in both:
                    wo(0, b, 1, "cWo")

            if stages > 2:
                pe.wait_ge(w12_split, 1)
                for b in both:
                    xnt(2, b)
                for b in both:
                    pe.wait_ge(xnt_ready[b], 3)
                    for c in range(NC):
                        last = pe.matmul(bank(b, 3)[:, c * E:(c + 1) * E], xnT[:, b, c * P:(c + 1) * P], W["mG"],
                                         start=True, stop=True)
                    last.then_inc(g_ps[b], 1)

                def hidden(e, b):
                    if e == 0:
                        pe.wait_ge(xnl_ready[b], 2)
                    if e >= 2:
                        pe.wait_ge(m_h[b], e - 1)
                    mm3(pe, bank(b, e % 2), w12h[:, 0, e], w12l[:, 0, e], xnTh[:, b], xnTl[:, b]).then_inc(m_hps[b], 1)

                for b in both:
                    hidden(0, b)
                for b in both:
                    pe.wait_ge(g_sel[b], after("g_sel"))
                for b in both:
                    for c in range(NC):
                        last = pe.matmul(bank(0, 3)[:, 64:64 + E], ones[:, :], sel[:, b, c],
                                         start=(b == 0 and c == 0), stop=(b == B - 1 and c == NC - 1))
                last.then_inc(g_cnt, 1)
                for e in range(E):
                    if e + 1 < E:
                        for b in both:
                            hidden(e + 1, b)
                    for b in both:
                        pe.wait_ge(m_hl[b], e + 1)
                        if e == 1:
                            pe.wait_ge(g_comb[b], after("g_comb"))
                        if e >= 2:
                            pe.wait_ge(m_x[b], e - 1)
                        for c in range(NC):
                            cc = slice(c * P, (c + 1) * P)
                            last = mm3(pe, bank(b, 2 + e % 2)[:, cc], hidh[:, b, e % 2, cc], hidl[:, b, e % 2, cc],
                                       w12h[:, 1, e], w12l[:, 1, e])
                        last.then_inc(m_y[b], 1)
                for b in both:
                    pe.wait_ge(g_comb[b], after("g_comb"))
                    pe.wait_ge(m_h[b], E)
                    for c in range(NC):
                        last = pe.transpose(bank(b, 0)[0:E, c * P:(c + 1) * P], comb[:, b, c], ident)
                    last.then_inc(m_ct[b], 1)
                for b in both:
                    pe.wait_ge(m_ctr[b], after("m_ctr"))
                    for c in range(NC):
                        last = pe.matmul(bank(b, 1)[:, c * D:(c + 1) * D], combT[:, b, c * P:(c + 1) * P], b2[:, :],
                                         start=True, stop=True)
                    last.then_inc(m_b[b], 1)

            if stages > 3:
                pe.wait_ge(mask_ready, 2)
                for b in both:
                    xnt(3, b)
                for b in both:
                    pe.wait_ge(xnt_ready[b], 4)
                    pe.matmul(bank(b, 1), W["sWq"], xnT[:, b], start=True, stop=True).then_inc(q_ps[b], 1)
                    pe.matmul(bank(b, 2), W["sWk"], xnT[:, b], start=True, stop=True).then_inc(q_ps[b], 1)
                    for c in range(NC):
                        last = pe.matmul(bank(b, 3)[:, c * D:(c + 1) * D], xnT[:, b, c * P:(c + 1) * P], W["sWv"],
                                         start=True, stop=True)
                    last.then_inc(q_ps[b], 1)
                for b in both:
                    pe.wait_ge(q_v[b], after("q_v"))
                    pe.wait_ge(q_k[b], after("q_k"))
                    pe.wait_ge(q_src[b], after("q_src"))
                for b in both:
                    pe.wait_ge(d_st[b], 16 * 27)

                    def scores(n):
                        kind, par = n % 3, n % 2
                        if n >= 2:
                            pe.wait_ge(s_e[b], n - 1)
                        elif b:
                            pe.wait_ge(s_e[b - 1], GROUPS - 1 + n)
                        at, w = NEARCOLS[kind]
                        for j in range(2):
                            h = 2 * (n // 3) + j
                            dst = ps[:, 2 * par + j]

                            def qk(i, c, k0, k1, to, **flags):
                                return pe.matmul(dst[:, to:to + k1 - k0], stack[:, b, i, h, c * P:(c + 1) * P],
                                                 stack[:, b, KK, h, k0:k1], **flags)

                            c = NC - 1 - kind
                            qk(QA, c, 0, c * P - CLIP, 0, start=True, stop=True)
                            pe.matmul(dst[:, at:at + w], identb, maskb[:, 0:w], start=True, stop=False)
                            last = qk(QS, c, c * P - CLIP, (c + 1) * P, at, start=False, stop=(kind < 2))
                            if kind == 2:
                                last = qk(QS, 0, 0, P, at + WL, start=False, stop=True)
                        last.then_inc(s_s[b], 1)

                    def turns(n):
                        kind, par = n % 3, n % 2
                        pe.wait_ge(s_e[b], n + 1)
                        for j in range(2):
                            m = 2 * n + j
                            if m >= 3:
                                pe.wait_ge(s_pt[b][m % 3], m // 3)
                            elif b:
                                pe.wait_ge(s_pt[b - 1][m % 3], 2 * GROUPS // 3)
                            for i in range(UNIT[kind] // P):
                                last = pe.transpose(ps[:, 4 + m % 3, i * P:(i + 1) * P], sprob[:, par, j, i * P:(i + 1) * P], ident)
                            last.then_inc(s_t[b], 1)

                    def values(m):
                        n, j = divmod(m, 2)
                        kind, h = n % 3, 2 * (n // 3) + j
                        pe.wait_ge(s_pt[b][m % 3], m // 3 + 1)
                        if m % 12 == 0:
                            if m:
                                pe.wait_ge(s_on[b], m // 12)
                            elif b:
                                pe.wait_ge(s_on[b - 1], 4)
                        c = NC - 1 - kind
                        at = ((h % 4) * NC + c) * 9
                        for u in range(c + 1):
                            last = pe.matmul(ps[:, 7, at:at + 9], sprobT[:, m % 4, u * P:(u + 1) * P], sva[:, b, u, h],
                                             start=(u == 0), stop=(u == c))
                        if kind == 2:
                            last = pe.matmul(ps[:, 7, at - 9:at], sprobT[:, m % 4, 2 * P:3 * P], sva[:, b, 0, h],
                                             start=True, stop=True)
                        last.then_inc(s_o[b], 1)

                    scores(0)
                    for n in range(GROUPS):
                        if n + 1 < GROUPS:
                            scores(n + 1)
                        turns(n)
                        if n:
                            values(2 * n - 2)
                            values(2 * n - 1)
                    values(2 * GROUPS - 2)
                    values(2 * GROUPS - 1)
                for b in both:
                    pe.wait_ge(o_fin[b], after("o_fin"))
                    ot(1, b, 0)
                for b in both:
                    wo(1, b, 1, "sWo")
            if stages > 4:
                for b in both:
                    xnt(4, b)
                for b in both:
                    pe.wait_ge(xnt_ready[b], 5)
                    pe.matmul(bank(b, 1), W["lWq"], xnT[:, b], start=True, stop=True).then_inc(l_qps[b], 1)
                for b in both:
                    pe.wait_ge(l_q[b], after("l_q"))
                    for c in range(NC):
                        at = (c % 2) * (D + H)
                        last = pe.matmul(bank(b, 2 + c // 2)[:, at:at + D + H], cqT[:, b, c * P:(c + 1) * P], lkv[:, b],
                                         start=True, stop=True)
                    last.then_inc(l_nps[b], 1)
                for b in both:
                    pe.wait_ge(o_fin[b], after("o_fin", 2))
                    ot(2, b, 0)
                for b in both:
                    wo(2, b, 1, "lWo")
            if stages > 5:
                for b in both:
                    xnt(5, b)
                for b in both:
                    pe.wait_ge(xnt_ready[b], 6)
                    for c in range(NC):
                        last = pe.matmul(bank(b, 3)[:, c * E:(c + 1) * E], xnT[:, b, c * P:(c + 1) * P], W["fG"],
                                         start=True, stop=True)
                    last.then_inc(g_ps[b], 1)
                for b in both:
                    pe.wait_ge(f_z[b], after("f_z"))
                    pe.wait_ge(xnl_ready[b], 4)

                def gate_up(n_):
                    k, i = divmod(n_, NI)
                    e, b = divmod(k, B)
                    if k % B == 0 and i == 0:
                        pe.wait_ge(f_wl, e + 1)
                    if n_ >= 2:
                        pe.wait_ge(f_a, n_ - 1)
                    for half, done in ((0, f_g), (1, f_u)):
                        at = slice(half * I1 + i * P, half * I1 + (i + 1) * P)
                        mm3(pe, ps[:, 2 * (n_ % 2) + half], fwh[:, e % 2, at], fwl[:, e % 2, at], xnTh[:, b], xnTl[:, b])\
                            .then_inc(done, 1)

                def down(k):
                    e = k // B
                    pe.wait_ge(f_al, NI * (k + 1))
                    if k >= 4:
                        pe.wait_ge(f_x, k - 3)
                    for c in range(NC):
                        cc = slice(c * P, (c + 1) * P)
                        for i in range(NI):
                            at = slice(2 * I1 + i * P, 2 * I1 + (i + 1) * P)
                            last = mm3(pe, ps[:, 4 + k % 4, cc], fah[:, k % 2, i, cc], fal[:, k % 2, i, cc],
                                       fwh[:, e % 2, at], fwl[:, e % 2, at], start=(i == 0), stop=(i == NI - 1))
                    last.then_inc(f_y, 1)

                for n_ in range(E * B * NI):
                    gate_up(n_)
                    if n_ % NI == 1 and n_ > NI:
                        down(n_ // NI - 1)
                down(E * B - 1)


GROUPS = 3 * H // 2
GROUP = [[(0, 4 * P, 0)], [(0, 3 * P, 0)], [(0, 2 * P, 0), (2 * P, P, 2)]]
NEARCOLS = [(3 * P - CLIP, WL), (2 * P - CLIP, WL), (P - CLIP, NEAR2)]
UNIT = [4 * P, 3 * P, 3 * P]
NEAR_LINKS = 2 + 1 + 2 * (CLIP + 1)
SBANK = [0, 3, 1, 2]
TBANK = [3, 0, 1, 2]


def constants():
    p = np.arange(P)
    heads = (p[:, None] // HD == np.arange(H)).astype(np.float32)
    blockd = (p[:, None] // HD == p // HD).astype(np.float32)
    away = p[:, None] + CLIP - np.arange(WL)
    dist = np.where(away < 0, -1, np.minimum(away, CLIP)).astype(np.float32)
    dist = np.concatenate([dist, dist[:, CLIP:]], 1)
    mask = np.where(dist < 0, BIG, 0.0).astype(np.float32)
    low = (np.arange(E)[None, :] < np.arange(E)[:, None]).astype(np.float32).reshape(1, E * E)
    return np.ascontiguousarray(np.concatenate(
        [np.eye(P, dtype=np.float32), blockd, dist, np.repeat(low, P, 0), heads, mask], 1))


STAGES = 6


def kernel(**a):
    import concourse.bacc as bacc
    from concourse.bass_utils import run_bass_kernel_spmd

    a = {k: np.asarray(v) for k, v in a.items()}
    w = {"aQK": a["L0_attn_QK"], "aVO": a["L0_attn_VO"],
         "cWq": a["L0_xattn_Wq"].T, "cWk": a["L0_xattn_Wk"].T, "cWv": a["L0_xattn_Wv"].T, "cWo": a["L0_xattn_Wo"].T,
         "mG": a["L0_ffn_gate_w"].T,
         "sWq": a["L1_attn_Wq"], "sWk": a["L1_attn_Wk"], "sWv": a["L1_attn_Wv"], "sWo": a["L1_attn_Wo"],
         "lWq": a["L1_xattn_Wq"].T, "lWk": a["L1_xattn_Wk"].T, "lWv": a["L1_xattn_Wv"].T, "lWo": a["L1_xattn_Wo"].T,
         "fG": a["L1_ffn_conf_w"].T}
    r = {"cbv": "L0_xattn_bv", "cbo": "L0_xattn_bo", "sbo": "L1_attn_bo", "lbk": "L1_xattn_bk", "lbv": "L1_xattn_bv",
         "lbo": "L1_xattn_bo", "fb": "L1_ffn_conf_b", "fw": "L1_ffn_wealth", "rel": "L1_attn_rel_emb"}
    c = {"cbq": "L0_xattn_bq", "cbk": "L0_xattn_bk", "lbq": "L1_xattn_bq"}
    cc = np.ascontiguousarray
    arrays = {
        "x": cc(a["x"]),
        "cst": constants(),
        "wts": cc(np.concatenate([w[n] for n in WEIGHTS], 1)),
        "rows": cc(np.concatenate([a[r[n]] for n in ROWS])),
        "cols": cc(np.concatenate([a[c[n]][:, None] for n in COLS] + [a["L0_ffn_b1"].T], 1)),
        "ctxT": cc(a["ctx_1024"].transpose(2, 0, 1)),
        "b2": cc(a["L0_ffn_b2"]),
        "w12": cc(np.stack([a["L0_ffn_w1"].transpose(2, 0, 1), a["L0_ffn_w2"].transpose(2, 0, 1)], 1)),
        "fgu": cc(np.stack([a["L1_ffn_gate_w"].transpose(2, 0, 1), a["L1_ffn_up_w"].transpose(2, 0, 1)], 2)),
        "fdn": cc(a["L1_ffn_down_w"].reshape(E, D, NI, P).transpose(3, 0, 2, 1)),
    }
    nc = bacc.Bacc("TRN2", target_bir_lowering=False, num_devices=1)
    d = {n: nc.dram_tensor(f"in_{n}", v.shape, mybir.dt.from_np(v.dtype), kind="ExternalInput").ap()
         for n, v in arrays.items()}
    out = nc.dram_tensor("out_x", (B, T, D), F32, kind="ExternalOutput").ap()
    build(nc, d, out, STAGES)
    got = run_bass_kernel_spmd(nc, [{f"in_{n}": v for n, v in arrays.items()}], core_ids=[0])
    return got.results[0]["out_x"]
```

```python
from contextlib import ExitStack

import numpy as np
import concourse.bass as bass
from concourse import mybir

P = 128
D = 128
B, T = 2, 512
NC = T // P
H, HD = 16, 8
QH, QC = 4, 32
TK = 77
HS, HPB = 18, 6
E = 8
I1 = 512
NI = I1 // P
CAP = int(1.25 * B * T / E)
CLIP = 16
WL = P + CLIP
NP3 = 3
KR = 9 * HD
NEAR2 = WL + P
BIG = -1e30

F32 = mybir.dt.float32
F32R = mybir.dt.float32r
BF16 = mybir.dt.bfloat16
ALU = mybir.AluOpType
ACT = mybir.ActivationFunctionType
AX = mybir.AxisListType

WEIGHTS = ["aQK", "aVO", "cWq", "cWk", "cWv", "cWo", "mG", "sWq", "sWk", "sWv", "sWo", "lWq", "lWk", "lWv", "lWo", "fG"]
WIDTH = {"mG": E, "fG": E}
ROWS = ["cbv", "cbo", "sbo", "lbk", "lbv", "lbo", "fb", "fw", "rel"]
RWIDTH = {"fb": E, "fw": E, "rel": CLIP + 1}
COLS = ["cbq", "cbk", "lbq"]
CONSTS = ["ident", "block", "dist", "lower", "heads", "mask"]
CWIDTH = {"dist": NEAR2, "mask": NEAR2, "lower": E * E, "heads": H}


PE_STEPS = ["k_ps", "a_proj", "a_proj", "k_ps", "a_o", "c_qps", "g_ps", "m_ct", "m_b", "m_yp", "q_ps", "q_ps",
            "q_ps", "l_qps", "l_nps", "g_ps", "m_ct", "m_b", "m_yp"]
DVE_STEPS = ["k_sb", "a_v", "k_sb", "c_q", "o_fin", "g_sub", "g_sel", "g_comb", "m_cl", "q_src", "q_v", "q_r", "q_l",
             "o_fin", "l_q", "o_fin", "f_z", "f_bs", "f_comb", "m_cl"]
ACT_STEPS = ["a_q", "g_e", "m_ctr", "m_yt", "q_k", "q_h", "q_m", "f_ez", "f_eb", "m_ctr", "m_yt"]


def offsets(names, widths):
    at, out = 0, {}
    for n in names:
        out[n] = (at, at + widths.get(n, D))
        at = out[n][1]
    return out, at


W_AT, W_ALL = offsets(WEIGHTS, WIDTH)
R_AT, R_ALL = offsets(ROWS, RWIDTH)
C_AT, C_ALL = offsets(CONSTS, CWIDTH)


def build(nc, d, out, stages=6):
    with ExitStack() as ctx:
        def sb(name, shape, dt=F32):
            return ctx.enter_context(nc.sbuf_tensor(name, shape, dt))

        def sem(name):
            return ctx.enter_context(nc.semaphore(name))

        def sems(name):
            return [sem(f"{name}{b}") for b in range(B)]

        both = range(B)
        wts = sb("wts", [P, W_ALL])
        rows = sb("rows", [P, R_ALL])
        cols = sb("cols", [P, len(COLS) + E])
        cst = sb("cst", [P, C_ALL])
        b2 = sb("b2", [P, D])
        ctxT = sb("ctxT", [P, B, TK])
        x = sb("x", [P, B, NC, D])
        xb = sb("xb", [P, B, NC, D])
        xn = sb("xn", [P, B, NC, D])
        xnT = sb("xnT", [P, B, T])
        xnTh = sb("xnTh", [P, B, T], F32R)
        xnTl = sb("xnTl", [P, B, T], F32R)
        stats = sb("stats", [P, B, NC, 6])
        mv = sb("mv", [P, B, NC, 2])
        vare = sb("vare", [P, B, NC])
        rstd = sb("rstd", [P, B, NC])
        mhalf = sb("mhalf", [P, NC])
        ones = sb("ones", [P, P])
        ps = ctx.enter_context(nc.psum_tensor("ps", [P, 2 * NC, 512], F32))

        W = {n: wts[:, a:b] for n, (a, b) in W_AT.items()}
        R = {n: rows[:, a:b] for n, (a, b) in R_AT.items()}
        C = {n: cst[:, a:b] for n, (a, b) in C_AT.items()}
        ident = C["ident"]

        def bank(b, i):
            return ps[:, NC * b + i, :]

        def route_bank(l, b):
            return ps[:, 6 + b, :] if l else bank(b, 3)

        probT = sb("probT", [P, B, NC, T])
        cqT = sb("cqT", [P, B, T])
        oacc = sb("oacc", [P, B, T])
        o = sb("o", [P, B, NC, D])
        oT = sb("oT", [P, B, T])
        lkv = sb("lkv", [P, B, D + H])
        rz = sb("rz", [P, B, NC, H])
        lg = sb("lg", [P, B, NC, E])
        pe_ = sb("pe_", [P, B, NC, E])
        gm = sb("gm", [P, B, NC])
        gs = sb("gs", [P, B, NC])
        cmpg = sb("cmpg", [P, B, NC, E, E])
        cmpe = sb("cmpe", [P, B, NC, E, E])
        rank = sb("rank", [P, B, NC, E])
        sel = sb("sel", [P, B, NC, E])
        comb = sb("comb", [P, B, NC, P])
        maskb = sb("maskb", [P, NEAR2 + P], BF16)
        identb = maskb[:, NEAR2:]
        near = sb("near", [P, NEAR2])
        hit = sb("hit", [P, NEAR2])
        svp = sb("svp", [P, B, NC, H, QC])
        snm = sb("snm", [P, 2, 4])

        outer, phase = ctx, ExitStack()
        ctx = phase
        xqkT = sb("xqkT", [P, B, T])
        xvo = sb("xvo", [P, B, NC, D])
        negm = sb("negm", [P, B, NC])
        rsum = sb("rsum", [P, B, NC])
        rinv = sb("rinv", [P, B, NC])
        prob = sb("prob", [P, B, NC, T])
        ckT = sb("ckT", [P, B, TK])
        ckb = sb("ckb", [P, B, HS, TK])
        cvp = sb("cvp", [TK, B, H, QC])
        cmax = sb("cmax", [P, B, HS])
        shifted = prob[:, :, 0:3, :].rearrange("p b c t -> p b (c t)")[:, :, 0:HS * TK]
        cprob = shifted
        cprobT = probT[0:TK, :, :, :]
        lk = sb("lk", [TK, B, D])
        lv = sb("lv", [TK, B, D])
        valid = sb("valid", [P, E])
        w12 = sb("w12", [P, 2, E, D])
        w12h = sb("w12h", [P, 2, E, D], F32R)
        w12l = sb("w12l", [P, 2, E, D], F32R)
        hid = sb("hid", [P, B, 2, T])
        hidh = sb("hidh", [P, B, 2, T], F32R)
        hidl = sb("hidl", [P, B, 2, T], F32R)
        combT0, combTh0, combTl0 = (sb(n, [P, B, T], t) for n, t in (("combT0", F32), ("combTh0", F32R), ("combTl0", F32R)))
        pick0 = sb("pick0", [P, E, P], F32R)
        phase.close()

        QS, QA, KK = range(3)
        flat = probT[:, :, :, :].rearrange("p b c t -> p (b c) t")
        src, rest = flat[:, 0:3], flat[:, 3:6]
        third = sb("third", [P, NP3, 3, T], BF16)
        stack = sb("stack", [KR, B, 3, H, T], BF16)
        scratch = nc.dram_tensor("qk_thirds", (B, 3, H, NP3, HD, T), BF16).ap()
        sprob = probT[:, 1].rearrange("p (a j) t -> p a j t", a=2)
        sprobT = probT[:, 0]
        phase.close()

        fw = sb("fw", [P, 2, 3 * I1])
        fwh = sb("fwh", [P, 2, 3 * I1], F32R)
        fwl = sb("fwl", [P, 2, 3 * I1], F32R)
        sg = sb("sg", [P, 2, T])
        fa = probT
        fah = sb("fah", [P, 2, NI, T], F32R)
        fal = sb("fal", [P, 2, NI, T], F32R)
        combT1, combTh1, combTl1 = (sb(n, [P, B, T], t) for n, t in (("combT1", F32), ("combTh1", F32R), ("combTl1", F32R)))
        pick1 = sb("pick1", [P, E, P], F32R)
        combT, combTh, combTl, pick = (combT0, combT1), (combTh0, combTh1), (combTl0, combTl1), (pick0, pick1)
        outer.push(phase)
        ctx = outer

        d_x = sem("d_x"); d_w = sem("d_w"); d_w12 = sem("d_w12"); d_out = sem("d_out")
        mask_ready = sem("mask_ready"); d_sc = sems("d_sc"); d_st = sems("d_st"); d_f = sems("d_f")
        consts = sem("consts")
        v_ones = sem("v_ones")
        dve_done = sem("dve_done")
        pool_done = sem("pool_done")
        var_ready, rstd_ready, xn_ready = sems("var_ready"), sems("rstd_ready"), sems("xn_ready")
        xnt_ps, xnt_ready, xnl_ready = sems("xnt_ps"), sems("xnt_ready"), sems("xnl_ready")
        x_ready, xb_ready = sems("x_ready"), sems("xb_ready")
        ot_ps, ot_ready, y_ps = sems("ot_ps"), sems("ot_ready"), sems("y_ps")

        pe_step, dve_step, act_step = sems("pe_step"), sems("dve_step"), sems("act_step")
        order = {}
        for names in (PE_STEPS, DVE_STEPS, ACT_STEPS):
            for i, name in enumerate(names):
                order.setdefault(name, []).append(i + 1)

        def after(name, n=1):
            return order[name][n - 1]

        k_ps = a_proj = a_o = c_qps = g_ps = m_ct = m_b = m_yp = q_ps = l_qps = l_nps = pe_step
        k_sb = a_v = c_q = g_sub = g_sel = g_comb = m_cl = q_src = q_v = q_r = q_l = o_fin = l_q = f_z = f_bs = f_comb = dve_step
        a_q = g_e = m_ctr = m_yt = q_k = q_h = q_m = f_ez = f_eb = act_step

        a_s, a_m, a_e, a_t, a_pt = (sems(n) for n in ("a_s", "a_m", "a_e", "a_t", "a_pt"))
        c_s, c_sub, c_e, c_sum, c_t, c_pt, c_o, c_on = (sems(n) for n in (
            "c_s", "c_sub", "c_e", "c_sum", "c_t", "c_pt", "c_o", "c_on"))
        g_cnt = sem("g_cnt")
        w12_split = sem("w12_split")
        m_hps, m_h, m_cb, m_hc, m_hh, m_hl, m_y = (sems(n) for n in ("m_hps", "m_h", "m_cb", "m_hc", "m_hh", "m_hl", "m_y"))
        s_s, s_m, s_e, s_t, s_o, s_on = (sems(n) for n in ("s_s", "s_m", "s_e", "s_t", "s_o", "s_on"))
        s_pt = [[sem(f"s_pt{b}_{i}") for i in range(3)] for b in both]
        f_wh = sem("f_wh"); f_wl = sem("f_wl")
        f_g, f_u, f_s, f_cb, f_a, f_ah, f_al, f_y = (sem(n) for n in (
            "f_g", "f_u", "f_s", "f_cb", "f_a", "f_ah", "f_al", "f_y"))

        block = ctx.enter_context(nc.Block())

        def mm3(pe, dst, lh, ll, rh, rl, start=True, stop=True):
            pe.matmul(dst, lh, rh, start=start, stop=False)
            pe.matmul(dst, lh, rl, start=False, stop=False)
            return pe.matmul(dst, ll, rh, start=False, stop=stop)

        @block.sync
        def _(sp):
            for b in both:
                sp.dma_start(x[:, b], d["x"][b].rearrange("(c p) d -> p c d", p=P)).then_inc(d_x, 16)
            sp.dma_start(cst[:, :], d["cst"]).then_inc(d_w, 16)
            sp.dma_start(wts[:, :], d["wts"]).then_inc(d_w, 16)
            sp.dma_start(rows[:, :], d["rows"].partition_broadcast(P)).then_inc(d_w, 16)
            sp.dma_start(cols[:, :], d["cols"]).then_inc(d_w, 16)
            sp.dma_start(ctxT[:, :, :], d["ctxT"]).then_inc(d_w, 16)
            sp.dma_start(b2[:, :], d["b2"]).then_inc(d_w, 16)
            sp.dma_start(w12[:, :, :, :], d["w12"]).then_inc(d_w12, 16)
            if stages > 3:
                for b in both:
                    sp.wait_ge(q_l[b], after("q_l"))
                    for i in range(3):
                        for t in range(NP3):
                            sp.dma_start(scratch[b, i, :, t], third[:, t, i]).then_inc(d_sc[b], 16)
                    sp.wait_ge(d_sc[b], 16 * 9)
                    for i in range(3):
                        for r in range(NP3):
                            for u in range(NP3):
                                t = r if i != KK else u
                                sp.dma_start(stack[(NP3 * r + u) * HD:(NP3 * r + u + 1) * HD, b, i],
                                             scratch[b, i, :, t].rearrange("h d t -> d h t")).then_inc(d_st[b], 16)
            if stages > 5:
                for b in both:
                    sp.wait_ge(x_ready[b], 4)
                for e in range(E):
                    if e >= 2:
                        sp.wait_ge(f_wl, 3 * (e - 1))
                    sp.dma_start(fw[:, e % 2, 0:2 * I1], d["fgu"][:, e]).then_inc(d_f[e % 2], 16)
                    sp.dma_start(fw[:, e % 2, 2 * I1:], d["fdn"][:, e]).then_inc(d_f[e % 2], 16)
            for b in both:
                sp.wait_ge(x_ready[b], stages)
                sp.dma_start(out[b].rearrange("(c p) d -> p c d", p=P), x[:, b]).then_inc(d_out, 16)
            sp.wait_ge(d_out, 16 * B)
        WALL = 16 * 6

        @block.gpsimd
        def _(pool):
            links = [0]

            def link(ins):
                links[0] += 1
                ins.then_inc(pool_done, 1)
                pool.wait_ge(pool_done, links[0])

            pool.memset(mhalf[:, :], -0.5).then_inc(consts, 1)
            pool.memset(ones[:, :], 1.0).then_inc(consts, 1)
            pool.memset(ckb[:, :, H:HS, :], 0.0).then_inc(consts, 1)
            pool.memset(cvp[:, :, :, :], 0.0).then_inc(consts, 1)
            pool.wait_ge(consts, 4)
            pool.memset(svp[:, :, :, :, :], 0.0).then_inc(v_ones, 1)
            pool.memset(comb[:, :, :, :], 0.0).then_inc(v_ones, 1)
            pool.wait_ge(d_w, WALL)
            pool.tensor_copy(pick0[:, :, :], ident[:, 0:E].unsqueeze(2).broadcast_to([P, E, P])).then_inc(v_ones, 1)

            def rstds(k, b):
                pool.wait_ge(var_ready[b], k + 1)
                link(pool.tensor_scalar(vare[:, b, :], mv[:, b, :, 1], 1e-5, None, ALU.add))
                pool.tensor_tensor(rstd[:, b, :], vare[:, b, :], mhalf[:, :], ALU.pow).then_inc(rstd_ready[b], 1)

            def add_bias(k, b, row):
                if k:
                    pool.wait_ge(x_ready[b], k)
                pool.tensor_tensor(xb[:, b], x[:, b], R[row].unsqueeze(1).broadcast_to([P, NC, D]),
                                   ALU.add).then_inc(xb_ready[b], 1)

            for b in both:
                rstds(0, b)
            if stages > 1:
                for b in both:
                    rstds(1, b)
                    add_bias(1, b, "cbo")
                pool.wait_ge(d_w12, 16)
                link(pool.tensor_copy(w12h[:, :, :, :], w12[:, :, :, :]))
                pool.tensor_tensor(w12l[:, :, :, :], w12[:, :, :, :], w12h[:, :, :, :].bitcast(F32),
                                   ALU.subtract).then_inc(w12_split, 1)
            if stages > 3:
                pool.wait_ge(d_w, WALL)
                pool.tensor_copy(maskb[:, 0:NEAR2], C["mask"]).then_inc(mask_ready, 1)
                pool.tensor_copy(identb, ident).then_inc(mask_ready, 1)
                dist = C["dist"]
                link(pool.tensor_scalar(near[:, :], dist, -1.0, None, ALU.is_equal))
                for k in range(CLIP + 1):
                    link(pool.tensor_scalar(hit[:, :], dist, float(k), R["rel"][:, k:k + 1], ALU.is_equal, ALU.mult))
                    link(pool.tensor_tensor(near[:, :], near[:, :], hit[:, :], ALU.add))
            if stages > 2:
                for b in both:
                    rstds(2, b)
                for e in range(E):
                    for b in both:
                        pool.wait_ge(m_hh[b], e + 1)
                        if e >= 2:
                            pool.wait_ge(m_y[b], e - 1)
                        pool.tensor_tensor(hidl[:, b, e % 2], hid[:, b, e % 2], hidh[:, b, e % 2].bitcast(F32),
                                           ALU.subtract).then_inc(m_hl[b], 1)
            if stages > 3:
                for b in both:
                    rstds(3, b)
                    add_bias(3, b, "sbo")
            if stages > 4:
                for b in both:
                    rstds(4, b)
                    add_bias(4, b, "lbo")
            if stages > 5:
                for b in both:
                    pool.wait_ge(s_on[b], 1)
                pool.tensor_copy(pick1[:, :, :], ident[:, 0:E].unsqueeze(2).broadcast_to([P, E, P])).then_inc(v_ones, 1)
            if stages > 5:
                for b in both:
                    rstds(5, b)
                for n_ in range(E * B * NI):
                    k, i = divmod(n_, NI)
                    pool.wait_ge(f_ah, n_ + 1)
                    if k >= 2:
                        pool.wait_ge(f_y, k - 1)
                    pool.tensor_tensor(fal[:, k % 2, i], fa[:, k % 2, i], fah[:, k % 2, i].bitcast(F32),
                                       ALU.subtract).then_inc(f_al, 1)

        @block.scalar
        def _(act):
            def xnt(k, b):
                act.wait_ge(xnt_ps[b], k + 1)
                act.activation(xnT[:, b], bank(b, 0), ACT.Copy).then_inc(xnt_ready[b], 1)

            def ot(n, b, i):
                act.wait_ge(ot_ps[b], n + 1)
                act.activation(oT[:, b], bank(b, i), ACT.Copy).then_inc(ot_ready[b], 1)

            def comb_rows(n_, b):
                act.wait_ge(m_ct[b], after("m_ct", n_))
                act.activation(combT[n_ - 1][:, b], route_bank(n_ - 1, b), ACT.Copy)
                act.activation(combTh[n_ - 1][:, b], route_bank(n_ - 1, b), ACT.Copy).then_inc(m_ctr[b], 1)

            def moe_out(n_, b, acc):
                act.wait_ge(m_b[b], after("m_b", n_))
                act.activation(oT[:, b], acc, ACT.Copy).then_inc(m_yt[b], 1)

            def wh(e, part):
                if part == 0:
                    act.wait_ge(d_f[e % 2], 32 * (e // 2 + 1))
                    if e >= 2:
                        act.wait_ge(f_y, B * (e - 1))
                at = slice(part * I1, (part + 1) * I1)
                act.activation(fwh[:, e % 2, at], fw[:, e % 2, at], ACT.Copy).then_inc(f_wh, 1)

            for b in both:
                xnt(0, b)
            for b in both:
                act.wait_ge(a_proj[b], after("a_proj"))
                act.activation(xqkT[:, b], bank(b, 1), ACT.Copy, scale=float(D) ** -0.5).then_inc(a_q[b], 1)
            for b in both:
                for c in range(NC):
                    act.wait_ge(a_m[b], c + 1)
                    act.activation(prob[:, b, c], bank(b, SBANK[c]), ACT.Exp, bias=negm[:, b, c:c + 1],
                                   accum_out=rsum[:, b, c:c + 1]).then_inc(a_e[b], 1)
            for b in both:
                for u in (0, 2):
                    act.wait_ge(a_t[b], u + 1)
                    act.activation(probT[:, b, u], bank(b, SBANK[u]), ACT.Copy).then_inc(a_pt[b], 1)
            if stages > 1:
                for b in both:
                    xnt(1, b)
                for c in range(NC):
                    for b in both:
                        act.wait_ge(c_sub[b], c + 1)
                        act.activation(cprob[:, b], shifted[:, b], ACT.Exp).then_inc(c_e[b], 1)
                        for u in range(NC):
                            act.wait_ge(c_t[b], NC * c + u + 1)
                            act.activation(cprobT[:, b, u], bank(b, TBANK[u])[0:TK, :], ACT.Copy).then_inc(c_pt[b], 1)
            if stages > 2:
                for b in both:
                    xnt(2, b)
                    act.activation(xnTh[:, b], bank(b, 0), ACT.Copy).then_inc(xnl_ready[b], 1)
                for b in both:
                    act.wait_ge(g_sub[b], after("g_sub"))
                    act.activation(pe_[:, b], lg[:, b], ACT.Exp).then_inc(g_e[b], 1)
                for b in both:
                    comb_rows(1, b)
                for e in range(E):
                    for b in both:
                        act.wait_ge(m_hps[b], e + 1)
                        if e >= 2:
                            act.wait_ge(m_hl[b], e - 1)
                        act.activation(hid[:, b, e % 2], bank(b, e % 2), ACT.Silu,
                                       bias=cols[:, len(COLS) + e:len(COLS) + e + 1]).then_inc(m_h[b], 1)
                    for b in both:
                        act.wait_ge(m_hc[b], e + 1)
                        if e >= 2:
                            act.wait_ge(m_y[b], e - 1)
                        act.activation(hidh[:, b, e % 2], hid[:, b, e % 2], ACT.Copy).then_inc(m_hh[b], 1)
                for b in both:
                    moe_out(1, b, bank(b, 2))
            if stages > 3:
                for b in both:
                    xnt(3, b)
                for b in both:
                    act.wait_ge(q_ps[b], after("q_ps", 2))
                    if b:
                        act.wait_ge(q_l[b - 1], after("q_l"))
                    act.activation(src[:, KK], bank(b, 2), ACT.Copy).then_inc(q_k[b], 1)
                    act.wait_ge(q_k[b], after("q_k"))
                    act.wait_ge(q_src[b], after("q_src"))
                    if b:
                        act.wait_ge(d_sc[b - 1], 16 * 9)
                    act.activation(third[:, 0], src[:, :], ACT.Copy).then_inc(q_h[b], 1)
                    act.wait_ge(q_r[b], after("q_r"))
                    act.activation(third[:, 1], rest[:, :], ACT.Copy).then_inc(q_m[b], 1)
                act.wait_ge(q_l[1], after("q_l"))
                for b in both:
                    def exps(n):
                        kind, par = n % 3, n % 2
                        act.wait_ge(s_m[b], n + 1)
                        if n >= 2:
                            act.wait_ge(s_t[b], 2 * (n - 1))
                        elif b:
                            act.wait_ge(s_t[b - 1], 2 * (GROUPS - 1 + n))
                        for j in range(2):
                            for i, (at, w, m) in enumerate(GROUP[kind]):
                                c, h = NC - 1 - kind - i, head(n // 3, j)
                                last = act.activation(sprob[:, par, j, at:at + w], ps[:, 2 * par + j, at:at + w], ACT.Exp,
                                                      bias=snm[:, par, m + j:m + j + 1], accum_out=rz[:, b, c, h:h + 1])
                        last.then_inc(s_e[b], 1)

                    def evac(m):
                        if m % 3 == 1:
                            return
                        act.wait_ge(s_t[b], m + 1)
                        if m >= 4:
                            act.wait_ge(s_o[b], m - 3)
                        w = UNIT[m // 2 % 3]
                        act.activation(sprobT[:, m % 4, 0:w], ps[:, 4 + m % 3, 0:w], ACT.Copy).then_inc(s_pt[b][m % 3], 1)

                    for n in range(GROUPS):
                        exps(n)
                        if n:
                            evac(2 * n - 2)
                            evac(2 * n - 1)
                    evac(2 * GROUPS - 2)
                    evac(2 * GROUPS - 1)
            if stages > 4:
                for b in both:
                    xnt(4, b)
                if stages > 5:
                    for part in range(3):
                        wh(0, part)
                for b in both:
                    ot(2, b, 0)
            if stages > 5:
                for b in both:
                    xnt(5, b)
                    act.activation(xnTh[:, b], bank(b, 0), ACT.Copy).then_inc(xnl_ready[b], 1)
                for b in both:
                    act.wait_ge(f_z[b], after("f_z"))
                    act.activation(pe_[:, b], lg[:, b], ACT.Exp, scale=-1.0).then_inc(f_ez[b], 1)
                for b in both:
                    act.wait_ge(f_bs[b], after("f_bs"))
                    act.activation(pe_[:, b], lg[:, b], ACT.Exp).then_inc(f_eb[b], 1)

                def ah(n_):
                    k, i = divmod(n_, NI)
                    act.wait_ge(f_a, n_ + 1)
                    if k >= 2:
                        act.wait_ge(f_y, k - 1)
                    act.activation(fah[:, k % 2, i], fa[:, k % 2, i], ACT.Copy).then_inc(f_ah, 1)

                for b in both:
                    comb_rows(2, b)
                for n_ in range(E * B * NI):
                    e, k = n_ // (B * NI), n_ // NI
                    part = n_ % (B * NI) - NI + 1
                    if 0 <= part < 3 and e < E - 1:
                        wh(e + 1, part)
                    act.wait_ge(f_g, n_ + 1)
                    if n_ >= 2:
                        act.wait_ge(f_a, n_ - 1)
                    act.activation(sg[:, n_ % 2], ps[:, 2 * (n_ % 2)], ACT.Silu).then_inc(f_s, 1)
                    if n_:
                        ah(n_ - 1)
                ah(E * B * NI - 1)
                for b in both:
                    moe_out(2, b, ps[:, 4 + b])

        @block.vector
        def _(dve):
            links = [0]

            def link(ins):
                links[0] += 1
                ins.then_inc(dve_done, 1)
                dve.wait_ge(dve_done, links[0])

            def norm_stats(k, b):
                if k:
                    dve.wait_ge(x_ready[b], k)
                for c in range(NC):
                    last = dve.bn_stats(stats[:, b, c], x[:, b, c])
                link(last)
                for c in range(NC):
                    last = dve.bn_aggr(mv[:, b, c], stats[:, b, c])
                last.then_inc(var_ready[b], 1)

            def norm_apply(k, b):
                dve.wait_ge(rstd_ready[b], k + 1)
                for c in range(NC):
                    last = dve.tensor_scalar(xn[:, b, c], x[:, b, c], mv[:, b, c, 0:1], rstd[:, b, c:c + 1],
                                             ALU.subtract, ALU.mult)
                last.then_inc(xn_ready[b], 1)

            def tail(n_, b, i):
                dve.wait_ge(xb_ready[b], n_ + 1)
                dve.wait_ge(y_ps[b], n_ + 1)
                dve.tensor_tensor(x[:, b].rearrange("p c d -> p (c d)"), bank(b, i),
                                  xb[:, b].rearrange("p c d -> p (c d)"), ALU.add).then_inc(x_ready[b], 1)

            dve.wait_ge(d_x, 16 * B)
            for b in both:
                norm_stats(0, b)
            for b in both:
                norm_apply(0, b)
            dve.wait_ge(d_w, WALL)
            dve.wait_ge(consts, 4)
            for b in both:
                dve.wait_ge(k_ps[b], after("k_ps"))
                link(dve.tensor_scalar(ckT[:, b], bank(b, 3)[:, 0:TK], cols[:, 1:2], None, ALU.add))
                dve.tensor_tensor(ckb[:, b, 0:H], ckT[:, b].unsqueeze(1).broadcast_to([P, H, TK]),
                                  C["heads"].unsqueeze(2).broadcast_to([P, H, TK]), ALU.mult)
                for j in range(QH):
                    def slot(v):
                        return v.rearrange("p (g j e) -> p g j e", j=QH, e=HD)[:, :, j]
                    dve.tensor_tensor(cvp[:, b].rearrange("p (g j) q -> p g j q", j=QH)[:, :, j, j * HD:(j + 1) * HD],
                                      slot(bank(b, 3)[0:TK, 128:256]), slot(R["cbv"][0:TK, :]), ALU.add)
                link(dve.tensor_tensor(lk[:, b], bank(b, 3)[0:TK, 256:384], R["lbk"][0:TK, :], ALU.add))
                link(dve.tensor_scalar(lk[:, b], lk[:, b], float(HD) ** -0.5, 0.0, ALU.mult, ALU.max))
                dve.tensor_scalar(lk[:, b], lk[:, b], 1e-6, None, ALU.add)
                dve.tensor_tensor(lv[:, b], bank(b, 3)[0:TK, 384:512], R["lbv"][0:TK, :], ALU.add).then_inc(k_sb[b], 1)
            for b in both:
                dve.wait_ge(a_proj[b], after("a_proj", 2))
                dve.tensor_copy(xvo[:, b].rearrange("p c d -> p (c d)"), bank(b, 2)).then_inc(a_v[b], 1)
            for b in both:
                dve.wait_ge(k_ps[b], after("k_ps", 2))
                dve.tensor_tensor(lkv[:, b, 0:D], bank(b, 3)[:, 0:D], C["block"], ALU.mult)
                dve.tensor_tensor(lkv[:, b, D:D + H], bank(b, 3)[:, D:D + H], C["heads"], ALU.mult).then_inc(k_sb[b], 1)
            for b in both:
                for c in range(NC):
                    dve.wait_ge(a_s[b], c + 1)
                    dve.tensor_reduce(negm[:, b, c:c + 1], bank(b, SBANK[c]), AX.X, ALU.max, negate=True)\
                        .then_inc(a_m[b], 1)
            for b in both:
                dve.wait_ge(a_e[b], NC)
                link(dve.reciprocal(rinv[:, b], rsum[:, b]))
                for u in (1, 3):
                    dve.wait_ge(a_t[b], u + 1)
                    dve.tensor_copy(probT[:, b, u], bank(b, SBANK[u])).then_inc(a_pt[b], 1)
            for b in both:
                dve.wait_ge(a_o[b], after("a_o"))
                for c in range(NC):
                    last = dve.scalar_tensor_tensor(x[:, b, c], bank(b, 0)[:, c * D:(c + 1) * D], rinv[:, b, c:c + 1],
                                                    x[:, b, c], ALU.mult, ALU.add)
                last.then_inc(x_ready[b], 1)

            def spread_inverse(b):
                link(dve.reciprocal(rz[:, b], rz[:, b]))
                for c in range(NC):
                    last = dve.tensor_copy(o[:, b, c].rearrange("p (h e) -> p h e", e=HD),
                                           rz[:, b, c].unsqueeze(2).broadcast_to([P, H, HD]))
                last.then_inc(o_fin[b], 1)

            def scale_outputs(n_, b):
                dve.wait_ge(ot_ps[b], n_)
                dve.tensor_tensor(oT[:, b], bank(b, 0), oacc[:, b], ALU.mult).then_inc(ot_ready[b], 1)

            if stages > 1:
                for b in both:
                    norm_stats(1, b)
                for b in both:
                    norm_apply(1, b)
                for b in both:
                    dve.wait_ge(c_qps[b], after("c_qps"))
                    dve.tensor_scalar(cqT[:, b], bank(b, 1), cols[:, 0:1], float(HD) ** -0.5, ALU.add, ALU.mult)\
                        .then_inc(c_q[b], 1)
                def shift(c, b):
                    s3 = ps[:, NC * b:NC * b + 3, 0:HPB * TK].rearrange("p a (h k) -> p a h k", k=TK)
                    m3 = cmax[:, b].rearrange("p (a h) -> p a h", h=HPB)
                    dve.wait_ge(c_s[b], c + 1)
                    link(dve.tensor_reduce(m3, s3, AX.X, ALU.max))
                    dve.tensor_tensor(shifted[:, b].rearrange("p (a h k) -> p a h k", h=HPB, k=TK), s3,
                                      m3.unsqueeze(3).broadcast_to([P, 3, HPB, TK]), ALU.subtract).then_inc(c_sub[b], 1)

                def sums(c, b):
                    dve.wait_ge(c_e[b], c + 1)
                    dve.tensor_reduce(rz[:, b, c], cprob[:, b, 0:H * TK].rearrange("p (h k) -> p h k", k=TK), AX.X, ALU.add)\
                        .then_inc(c_sum[b], 1)

                def outputs(c, b):
                    dve.wait_ge(c_o[b], c + 1)
                    dve.tensor_copy(oacc[:, b, c * P:(c + 1) * P], bank(b, 3)[:, c * P:(c + 1) * P]).then_inc(c_on[b], 1)

                for b in both:
                    shift(0, b)
                for c in range(NC):
                    for b in both:
                        sums(c, b)
                        if c + 1 < NC:
                            shift(c + 1, b)
                        outputs(c, b)
                for b in both:
                    dve.wait_ge(c_sum[b], NC)
                    spread_inverse(b)
                for b in both:
                    scale_outputs(1, b)
                for b in both:
                    tail(0, b, 1)

            def ranks(b, v):
                other = v.unsqueeze(2).broadcast_to([P, NC, E, E])
                mine = v.unsqueeze(3).broadcast_to([P, NC, E, E])
                low = C["lower"].rearrange("p (i j) -> p i j", j=E).unsqueeze(1).broadcast_to([P, NC, E, E])
                dve.tensor_tensor(cmpg[:, b], other, mine, ALU.is_gt)
                link(dve.tensor_tensor(cmpe[:, b], other, mine, ALU.is_equal))
                link(dve.tensor_tensor(cmpe[:, b], cmpe[:, b], low, ALU.mult))
                link(dve.tensor_tensor(cmpg[:, b], cmpg[:, b], cmpe[:, b], ALU.add))
                link(dve.tensor_reduce(rank[:, b], cmpg[:, b], AX.X, ALU.add))
                return dve.tensor_scalar(sel[:, b], rank[:, b], 1.5, None, ALU.is_lt)

            def per_chunk(v):
                return v.unsqueeze(2).broadcast_to([P, NC, E])

            def comb_low(n_, b):
                dve.wait_ge(m_ctr[b], after("m_ctr", n_))
                dve.tensor_tensor(combTl[n_ - 1][:, b], combT[n_ - 1][:, b], combTh[n_ - 1][:, b].bitcast(F32), ALU.subtract).then_inc(m_cl[b], 1)

            def moe_add(n_, b, turned):
                dve.wait_ge(m_yp[b], after("m_yp", n_))
                dve.tensor_tensor(x[:, b].rearrange("p c d -> p (c d)"), turned,
                                  x[:, b].rearrange("p c d -> p (c d)"), ALU.add).then_inc(x_ready[b], 1)

            if stages > 2:
                for b in both:
                    norm_stats(2, b)
                for b in both:
                    norm_apply(2, b)
                for b in both:
                    dve.wait_ge(xnl_ready[b], 1)
                    dve.tensor_tensor(xnTl[:, b], xnT[:, b], xnTh[:, b].bitcast(F32), ALU.subtract).then_inc(xnl_ready[b], 1)
                for b in both:
                    g = bank(b, 3)[:, 0:NC * E].rearrange("p (c e) -> p c e", e=E)
                    dve.wait_ge(g_ps[b], after("g_ps"))
                    link(dve.tensor_reduce(gm[:, b], g, AX.X, ALU.max))
                    dve.tensor_tensor(lg[:, b], g, per_chunk(gm[:, b]), ALU.subtract).then_inc(g_sub[b], 1)
                for b in both:
                    dve.wait_ge(g_e[b], after("g_e"))
                    link(dve.tensor_reduce(gs[:, b], pe_[:, b], AX.X, ALU.add))
                    link(dve.reciprocal(gm[:, b], gs[:, b]))
                    link(dve.tensor_tensor(pe_[:, b], pe_[:, b], per_chunk(gm[:, b]), ALU.mult))
                    ranks(b, pe_[:, b]).then_inc(g_sel[b], 1)
                dve.wait_ge(g_cnt, 1)
                dve.wait_ge(v_ones, 3)
                link(dve.tensor_scalar(valid[:, :], bank(0, 3)[:, 64:64 + E], CAP + 0.5, None, ALU.is_lt))
                for b in both:
                    link(dve.tensor_tensor(pe_[:, b], pe_[:, b], sel[:, b], ALU.mult))
                    dve.tensor_tensor(comb[:, b, :, 0:E], pe_[:, b], valid[:, :].unsqueeze(1).broadcast_to([P, NC, E]),
                                      ALU.mult).then_inc(g_comb[b], 1)
                for b in both:
                    comb_low(1, b)
                for e in range(E):
                    for b in both:
                        dve.wait_ge(m_h[b], e + 1)
                        dve.wait_ge(m_cb[b], e + 1)
                        dve.tensor_tensor(hid[:, b, e % 2], hid[:, b, e % 2], bank(b, 3), ALU.mult).then_inc(m_hc[b], 1)
                for b in both:
                    moe_add(1, b, bank(b, 1))
            if stages > 3:
                for b in both:
                    norm_stats(3, b)
                for b in both:
                    norm_apply(3, b)
                dve.wait_ge(v_ones, 1)
                for b in both:
                    dve.wait_ge(q_ps[b], after("q_ps"))
                    if b:
                        dve.wait_ge(q_l[b - 1], after("q_l"))
                    link(dve.tensor_scalar(src[:, QS], bank(b, 1), float(HD) ** -0.5, None, ALU.mult))
                    dve.tensor_scalar(src[:, QA], src[:, QS], R["rel"][:, CLIP:CLIP + 1], None, ALU.mult).then_inc(q_src[b], 1)
                    dve.wait_ge(q_ps[b], after("q_ps", 3))
                    v4 = bank(b, 3).rearrange("p (c g j e) -> p c g j e", c=NC, j=QH, e=HD)
                    p4 = svp[:, b].rearrange("p c (g j) q -> p c g j q", j=QH)
                    for j in range(QH):
                        last = dve.tensor_copy(p4[:, :, :, j, j * HD:(j + 1) * HD], v4[:, :, :, j])
                    last.then_inc(q_v[b], 1)
                    dve.wait_ge(q_h[b], after("q_h"))
                    dve.tensor_tensor(rest[:, :], src[:, :], third[:, 0], ALU.subtract).then_inc(q_r[b], 1)
                    dve.wait_ge(q_m[b], after("q_m"))
                    dve.tensor_tensor(third[:, 2], rest[:, :], third[:, 1], ALU.subtract).then_inc(q_l[b], 1)
                dve.wait_ge(pool_done, NEAR_LINKS)
                for b in both:
                    def maxes(n):
                        kind, par = n % 3, n % 2
                        dve.wait_ge(s_s[b], n + 1)
                        at, w = NEARCOLS[kind]
                        two = ps[:, 2 * par:2 * par + 2, :]
                        link(dve.tensor_tensor(two[:, :, at:at + w], two[:, :, at:at + w],
                                               near[:, 0:w].unsqueeze(1).broadcast_to([P, 2, w]), ALU.mult))
                        for at, w, m in GROUP[kind]:
                            last = dve.tensor_reduce(snm[:, par, m:m + 2], two[:, :, at:at + w], AX.X, ALU.max, negate=True)
                        last.then_inc(s_m[b], 1)

                    def evac(m):
                        if m % 3 != 1:
                            return
                        dve.wait_ge(s_t[b], m + 1)
                        if m >= 4:
                            dve.wait_ge(s_o[b], m - 3)
                        w = UNIT[m // 2 % 3]
                        dve.tensor_copy(sprobT[:, m % 4, 0:w], ps[:, 4 + m % 3, 0:w]).then_inc(s_pt[b][m % 3], 1)

                    for n in range(GROUPS):
                        maxes(n)
                        if n >= 2:
                            evac(2 * n - 4)
                            evac(2 * n - 3)
                    evac(2 * GROUPS - 4)
                    evac(2 * GROUPS - 3)
                    evac(2 * GROUPS - 2)
                    evac(2 * GROUPS - 1)
                    dve.wait_ge(s_e[b], GROUPS)
                    spread_inverse(b)
                    dve.wait_ge(s_o[b], 2 * GROUPS)
                    dve.tensor_copy(oacc[:, b], ps[:, 7]).then_inc(s_on[b], 1)
                for b in both:
                    dve.wait_ge(s_on[b], 1)
                    scale_outputs(2, b)
                for b in both:
                    tail(1, b, 1)
            if stages > 4:
                for b in both:
                    norm_stats(4, b)
                for b in both:
                    norm_apply(4, b)
                for b in both:
                    dve.wait_ge(l_qps[b], after("l_qps"))
                    link(dve.tensor_scalar(cqT[:, b], bank(b, 1), cols[:, 2:3], float(HD) ** -0.5, ALU.add, ALU.mult))
                    dve.tensor_scalar(cqT[:, b], cqT[:, b], 0.0, 1e-6, ALU.max, ALU.add).then_inc(l_q[b], 1)
                for b in both:
                    dve.wait_ge(l_nps[b], after("l_nps"))
                    two = ps[:, NC * b + 2:NC * b + 4, 0:2 * (D + H)].rearrange("p a (c n) -> p a c n", n=D + H)
                    link(dve.tensor_scalar(rz[:, b].rearrange("p (a c) h -> p a c h", c=2), two[:, :, :, D:], 1e-8, None, ALU.add))
                    link(dve.reciprocal(rz[:, b], rz[:, b]))
                    for c in range(NC):
                        last = dve.tensor_tensor(o[:, b, c].rearrange("p (h e) -> p h e", e=HD),
                                                 two[:, c // 2, c % 2, 0:D].rearrange("p (h e) -> p h e", e=HD),
                                                 rz[:, b, c].unsqueeze(2).broadcast_to([P, H, HD]), ALU.mult)
                    last.then_inc(o_fin[b], 1)
                for b in both:
                    tail(2, b, 1)
            if stages > 5:
                for b in both:
                    norm_stats(5, b)
                for b in both:
                    norm_apply(5, b)
                for b in both:
                    dve.wait_ge(xnl_ready[b], 3)
                    dve.tensor_tensor(xnTl[:, b], xnT[:, b], xnTh[:, b].bitcast(F32), ALU.subtract).then_inc(xnl_ready[b], 1)

                def wl(e, part):
                    dve.wait_ge(f_wh, 3 * e + part + 1)
                    if e >= 2:
                        dve.wait_ge(f_y, B * (e - 1))
                    at = slice(part * I1, (part + 1) * I1)
                    dve.tensor_tensor(fwl[:, e % 2, at], fw[:, e % 2, at], fwh[:, e % 2, at].bitcast(F32),
                                      ALU.subtract).then_inc(f_wl, 1)

                for part in range(3):
                    wl(0, part)

                def each(v):
                    return v.unsqueeze(1).broadcast_to([P, NC, E])

                for b in both:
                    dve.wait_ge(g_ps[b], after("g_ps", 2))
                    dve.tensor_tensor(lg[:, b], route_bank(1, b)[:, 0:NC * E].rearrange("p (c e) -> p c e", e=E), each(R["fb"]),
                                      ALU.add).then_inc(f_z[b], 1)
                for b in both:
                    dve.wait_ge(f_ez[b], after("f_ez"))
                    link(dve.tensor_scalar(lg[:, b], pe_[:, b], 1.0, None, ALU.add))
                    link(dve.reciprocal(lg[:, b], lg[:, b]))
                    link(dve.tensor_tensor(lg[:, b], lg[:, b], each(R["fw"]), ALU.mult))
                    link(ranks(b, lg[:, b]))
                    link(dve.tensor_reduce(gm[:, b], lg[:, b], AX.X, ALU.max))
                    dve.tensor_tensor(lg[:, b], lg[:, b], per_chunk(gm[:, b]), ALU.subtract).then_inc(f_bs[b], 1)
                for b in both:
                    dve.wait_ge(f_eb[b], after("f_eb"))
                    link(dve.tensor_tensor(pe_[:, b], pe_[:, b], sel[:, b], ALU.mult))
                    link(dve.tensor_reduce(gs[:, b], pe_[:, b], AX.X, ALU.add))
                    link(dve.reciprocal(gs[:, b], gs[:, b]))
                    dve.tensor_tensor(comb[:, b, :, 0:E], pe_[:, b], per_chunk(gs[:, b]), ALU.mult).then_inc(f_comb[b], 1)

                for b in both:
                    comb_low(2, b)
                for n_ in range(E * B * NI):
                    k, i = divmod(n_, NI)
                    e, part = k // B, n_ % (B * NI) - NI
                    if 0 <= part < 3 and e < E - 1:
                        wl(e + 1, part)
                    dve.wait_ge(f_s, n_ + 1)
                    dve.wait_ge(f_cb, k + 1)
                    if k >= 2:
                        dve.wait_ge(f_al, n_ - 2 * NI + 1)
                    link(dve.tensor_tensor(fa[:, k % 2, i], sg[:, n_ % 2], ps[:, 6 + k % 2], ALU.mult))
                    dve.wait_ge(f_u, n_ + 1)
                    dve.tensor_tensor(fa[:, k % 2, i], fa[:, k % 2, i], ps[:, 2 * (n_ % 2) + 1], ALU.mult).then_inc(f_a, 1)
                for b in both:
                    moe_add(2, b, ps[:, 6 + b])

        @block.tensor
        def _(pe):
            def xnt(k, b):
                pe.wait_ge(xn_ready[b], k + 1)
                for c in range(NC):
                    last = pe.transpose(bank(b, 0)[:, c * P:(c + 1) * P], xn[:, b, c], ident)
                last.then_inc(xnt_ps[b], 1)

            def ot(n_, b, i):
                for c in range(NC):
                    last = pe.transpose(bank(b, i)[:, c * P:(c + 1) * P], o[:, b, c], ident)
                last.then_inc(ot_ps[b], 1)

            def wo(n_, b, i, w):
                pe.wait_ge(ot_ready[b], n_ + 1)
                for c in range(NC):
                    last = pe.matmul(bank(b, i)[:, c * D:(c + 1) * D], oT[:, b, c * P:(c + 1) * P], W[w],
                                     start=True, stop=True)
                last.then_inc(y_ps[b], 1)

            def comb_rows(l, b, made):
                pe.wait_ge(dve_step[b], after(made))
                for c in range(NC):
                    last = pe.transpose(route_bank(l, b)[:, c * P:(c + 1) * P], comb[:, b, c], ident)
                last.then_inc(m_ct[b], 1)

            def spread(dst, l, e, b):
                pe.matmul(dst, pick[l][:, e], combTh[l][:, b], start=True, stop=False)
                return pe.matmul(dst, pick[l][:, e], combTl[l][:, b], start=False, stop=True)

            def moe_turn(n_, b, dst):
                pe.wait_ge(m_yt[b], after("m_yt", n_))
                for c in range(NC):
                    last = pe.transpose(dst[:, c * P:(c + 1) * P], oT[:, b, c * P:(c + 1) * P], ident)
                last.then_inc(m_yp[b], 1)

            pe.wait_ge(consts, 4)
            pe.wait_ge(d_w, WALL)
            for b in both:
                xnt(0, b)
            for b in both:
                pe.matmul(bank(b, 3)[:, 0:TK], W["cWk"], ctxT[:, b], start=True, stop=True)
                for i, w in enumerate(("cWv", "lWk", "lWv")):
                    last = pe.matmul(bank(b, 3)[0:TK, (i + 1) * 128:(i + 2) * 128], ctxT[:, b], W[w], start=True, stop=True)
                last.then_inc(k_ps[b], 1)
            for b in both:
                pe.wait_ge(xnt_ready[b], 1)
                pe.matmul(bank(b, 1), W["aQK"], xnT[:, b], start=True, stop=True).then_inc(a_proj[b], 1)
                for c in range(NC):
                    last = pe.matmul(bank(b, 2)[:, c * D:(c + 1) * D], xnT[:, b, c * P:(c + 1) * P], W["aVO"],
                                     start=True, stop=True)
                last.then_inc(a_proj[b], 1)
            for b in both:
                pe.wait_ge(k_sb[b], after("k_sb"))
                pe.matmul(bank(b, 3)[:, 0:D], lk[:, b], lv[:, b], start=True, stop=True)
                pe.matmul(bank(b, 3)[:, D:D + H], lk[:, b], ones[0:TK, 0:H], start=True, stop=True).then_inc(k_ps[b], 1)
            for b in both:
                pe.wait_ge(a_q[b], after("a_q"))
                for c in range(NC):
                    if SBANK[c] == 2:
                        pe.wait_ge(a_v[b], after("a_v"))
                    if SBANK[c] == 3:
                        pe.wait_ge(k_sb[b], after("k_sb", 2))
                    pe.matmul(bank(b, SBANK[c]), xqkT[:, b, c * P:(c + 1) * P], xnT[:, b], start=True, stop=True)\
                        .then_inc(a_s[b], 1)
            for b in both:
                pe.wait_ge(a_e[b], NC)
                for u in range(NC):
                    for c in range(NC):
                        last = pe.transpose(bank(b, SBANK[u])[:, c * P:(c + 1) * P], prob[:, b, c, u * P:(u + 1) * P], ident)
                    last.then_inc(a_t[b], 1)
            for b in both:
                pe.wait_ge(a_pt[b], NC)
                for c in range(NC):
                    for u in range(NC):
                        last = pe.matmul(bank(b, 0)[:, c * D:(c + 1) * D], probT[:, b, u, c * P:(c + 1) * P], xvo[:, b, u],
                                         start=(u == 0), stop=(u == NC - 1))
                last.then_inc(a_o[b], 1)

            if stages > 1:
                for b in both:
                    xnt(1, b)
                for b in both:
                    pe.wait_ge(xnt_ready[b], 2)
                    pe.matmul(bank(b, 1), W["cWq"], xnT[:, b], start=True, stop=True).then_inc(c_qps[b], 1)
                def scores(c, b):
                    if c == 0:
                        pe.wait_ge(c_q[b], after("c_q"))
                    else:
                        pe.wait_ge(c_pt[b], NC * c)
                    for a in range(3):
                        last = pe.matmul(bank(b, a)[:, 0:HPB * TK], cqT[:, b, c * P:(c + 1) * P],
                                         ckb[:, b, a * HPB:(a + 1) * HPB].rearrange("p h k -> p (h k)"),
                                         start=True, stop=True)
                    last.then_inc(c_s[b], 1)

                def turns(c, b):
                    pe.wait_ge(c_e[b], c + 1)
                    if c:
                        pe.wait_ge(c_on[b], c)
                    for j in range(QH):
                        for g in range(H // QH):
                            h = QH * g + j
                            last = pe.transpose(bank(b, TBANK[j])[0:TK, g * P:(g + 1) * P],
                                                cprob[:, b, h * TK:(h + 1) * TK], ident)
                        last.then_inc(c_t[b], 1)

                def values(c, b):
                    pe.wait_ge(c_pt[b], NC * (c + 1))
                    for j in range(QH):
                        for g in range(H // QH):
                            last = pe.matmul(bank(b, 3)[g * QC:(g + 1) * QC, c * P:(c + 1) * P], cvp[:, b, QH * g + j],
                                             cprobT[:, b, j, g * P:(g + 1) * P], start=(j == 0), stop=(j == QH - 1))
                    last.then_inc(c_o[b], 1)

                for b in both:
                    scores(0, b)
                for c in range(NC):
                    for b in both:
                        turns(c, b)
                        if c + 1 < NC:
                            scores(c + 1, b)
                        values(c, b)
                for b in both:
                    pe.wait_ge(o_fin[b], after("o_fin"))
                    ot(0, b, 0)
                for b in both:
                    wo(0, b, 1, "cWo")

            if stages > 2:
                pe.wait_ge(w12_split, 1)
                for b in both:
                    xnt(2, b)
                for b in both:
                    pe.wait_ge(xnt_ready[b], 3)
                    for c in range(NC):
                        last = pe.matmul(bank(b, 3)[:, c * E:(c + 1) * E], xnT[:, b, c * P:(c + 1) * P], W["mG"],
                                         start=True, stop=True)
                    last.then_inc(g_ps[b], 1)

                def hidden(e, b):
                    if e == 0:
                        pe.wait_ge(xnl_ready[b], 2)
                    if e >= 2:
                        pe.wait_ge(m_h[b], e - 1)
                    mm3(pe, bank(b, e % 2), w12h[:, 0, e], w12l[:, 0, e], xnTh[:, b], xnTl[:, b]).then_inc(m_hps[b], 1)

                for b in both:
                    hidden(0, b)
                for b in both:
                    pe.wait_ge(g_sel[b], after("g_sel"))
                for b in both:
                    for c in range(NC):
                        last = pe.matmul(bank(0, 3)[:, 64:64 + E], ones[:, :], sel[:, b, c],
                                         start=(b == 0 and c == 0), stop=(b == B - 1 and c == NC - 1))
                last.then_inc(g_cnt, 1)
                for b in both:
                    comb_rows(0, b, "g_comb")

                def weights(e, b):
                    if e == 0:
                        pe.wait_ge(m_cl[b], after("m_cl"))
                    else:
                        pe.wait_ge(m_hc[b], e)
                    spread(bank(b, 3), 0, e, b).then_inc(m_cb[b], 1)

                for b in both:
                    weights(0, b)
                for e in range(E):
                    if e + 1 < E:
                        for b in both:
                            hidden(e + 1, b)
                        for b in both:
                            weights(e + 1, b)
                    for b in both:
                        pe.wait_ge(m_hl[b], e + 1)
                        mm3(pe, bank(b, 2), w12h[:, 1, e], w12l[:, 1, e], hidh[:, b, e % 2], hidl[:, b, e % 2],
                            start=(e == 0), stop=False).then_inc(m_y[b], 1)
                for b in both:
                    pe.matmul(bank(b, 2), b2[:, :], combT0[:, b], start=False, stop=True).then_inc(m_b[b], 1)
                for b in both:
                    moe_turn(1, b, bank(b, 1))

            if stages > 3:
                pe.wait_ge(mask_ready, 2)
                for b in both:
                    xnt(3, b)
                for b in both:
                    pe.wait_ge(xnt_ready[b], 4)
                    pe.matmul(bank(b, 1), W["sWq"], xnT[:, b], start=True, stop=True).then_inc(q_ps[b], 1)
                    pe.matmul(bank(b, 2), W["sWk"], xnT[:, b], start=True, stop=True).then_inc(q_ps[b], 1)
                    for c in range(NC):
                        last = pe.matmul(bank(b, 3)[:, c * D:(c + 1) * D], xnT[:, b, c * P:(c + 1) * P], W["sWv"],
                                         start=True, stop=True)
                    last.then_inc(q_ps[b], 1)
                for b in both:
                    pe.wait_ge(q_v[b], after("q_v"))
                    pe.wait_ge(q_k[b], after("q_k"))
                    pe.wait_ge(q_src[b], after("q_src"))
                for b in both:
                    pe.wait_ge(d_st[b], 16 * 27)

                    def scores(n):
                        kind, par = n % 3, n % 2
                        if n >= 2:
                            pe.wait_ge(s_e[b], n - 1)
                        elif b:
                            pe.wait_ge(s_e[b - 1], GROUPS - 1 + n)
                        at, w = NEARCOLS[kind]
                        for j in range(2):
                            h = head(n // 3, j)
                            dst = ps[:, 2 * par + j]

                            def qk(i, c, k0, k1, to, **flags):
                                return pe.matmul(dst[:, to:to + k1 - k0], stack[:, b, i, h, c * P:(c + 1) * P],
                                                 stack[:, b, KK, h, k0:k1], **flags)

                            c = NC - 1 - kind
                            qk(QA, c, 0, c * P - CLIP, 0, start=True, stop=True)
                            pe.matmul(dst[:, at:at + w], identb, maskb[:, 0:w], start=True, stop=False)
                            last = qk(QS, c, c * P - CLIP, (c + 1) * P, at, start=False, stop=(kind < 2))
                            if kind == 2:
                                last = qk(QS, 0, 0, P, at + WL, start=False, stop=True)
                        last.then_inc(s_s[b], 1)

                    def turns(n):
                        kind, par = n % 3, n % 2
                        pe.wait_ge(s_e[b], n + 1)
                        for j in range(2):
                            m = 2 * n + j
                            if m >= 3:
                                pe.wait_ge(s_pt[b][m % 3], m // 3)
                            elif b:
                                pe.wait_ge(s_pt[b - 1][m % 3], 2 * GROUPS // 3)
                            for i in range(UNIT[kind] // P):
                                last = pe.transpose(ps[:, 4 + m % 3, i * P:(i + 1) * P], sprob[:, par, j, i * P:(i + 1) * P], ident)
                            last.then_inc(s_t[b], 1)

                    def values(n):
                        kind, pair = n % 3, n // 3
                        for j in range(2):
                            m = 2 * n + j
                            pe.wait_ge(s_pt[b][m % 3], m // 3 + 1)
                        if n == 0 and b:
                            pe.wait_ge(s_on[b - 1], 1)
                        c = NC - 1 - kind
                        blocks = [(c, u, u) for u in range(c + 1)] + ([(0, 2, 0)] if kind == 2 else [])
                        for c, i, u in blocks:
                            for j in range(2):
                                h = head(pair, j)
                                tile = slice(h // QH * QC, (h // QH + 1) * QC)
                                last = pe.matmul(ps[tile, 7, c * P:(c + 1) * P], svp[:, b, u, h],
                                                 sprobT[:, (2 * n + j) % 4, i * P:(i + 1) * P],
                                                 start=(pair < 2 and kind == 0 and u == 0),
                                                 stop=(pair >= 2 * QH - 2 and (c, u) == (0, 0)))
                        last.then_inc(s_o[b], 2)

                    scores(0)
                    scores(1)
                    for n in range(GROUPS):
                        if n + 2 < GROUPS:
                            scores(n + 2)
                        turns(n)
                        if n:
                            values(n - 1)
                    values(GROUPS - 1)
                for b in both:
                    pe.wait_ge(o_fin[b], after("o_fin", 2))
                    ot(1, b, 0)
                for b in both:
                    wo(1, b, 1, "sWo")
            if stages > 4:
                for b in both:
                    xnt(4, b)
                for b in both:
                    pe.wait_ge(xnt_ready[b], 5)
                    pe.matmul(bank(b, 1), W["lWq"], xnT[:, b], start=True, stop=True).then_inc(l_qps[b], 1)
                for b in both:
                    pe.wait_ge(l_q[b], after("l_q"))
                    for c in range(NC):
                        at = (c % 2) * (D + H)
                        last = pe.matmul(bank(b, 2 + c // 2)[:, at:at + D + H], cqT[:, b, c * P:(c + 1) * P], lkv[:, b],
                                         start=True, stop=True)
                    last.then_inc(l_nps[b], 1)
                for b in both:
                    pe.wait_ge(o_fin[b], after("o_fin", 3))
                    ot(2, b, 0)
                for b in both:
                    wo(2, b, 1, "lWo")
            if stages > 5:
                for b in both:
                    xnt(5, b)
                for b in both:
                    pe.wait_ge(xnt_ready[b], 6)
                    for c in range(NC):
                        last = pe.matmul(route_bank(1, b)[:, c * E:(c + 1) * E], xnT[:, b, c * P:(c + 1) * P], W["fG"],
                                         start=True, stop=True)
                    last.then_inc(g_ps[b], 1)

                def gate_up(n_):
                    k, i = divmod(n_, NI)
                    e, b = divmod(k, B)
                    if k % B == 0 and i == 0:
                        pe.wait_ge(f_wl, 3 * (e + 1))
                    if n_ in (0, NI):
                        pe.wait_ge(xnl_ready[b], 4)
                    if n_ >= 2:
                        pe.wait_ge(f_a, n_ - 1)
                    for half, done in ((0, f_g), (1, f_u)):
                        at = slice(half * I1 + i * P, half * I1 + (i + 1) * P)
                        mm3(pe, ps[:, 2 * (n_ % 2) + half], fwh[:, e % 2, at], fwl[:, e % 2, at], xnTh[:, b], xnTl[:, b])\
                            .then_inc(done, 1)

                def weights(k):
                    e, b = divmod(k, B)
                    if k >= 2:
                        pe.wait_ge(f_a, NI * (k - 1))
                    spread(ps[:, 6 + k % 2], 1, e, b).then_inc(f_cb, 1)

                def down(k):
                    e, b = divmod(k, B)
                    pe.wait_ge(f_al, NI * (k + 1))
                    for i in range(NI):
                        at = slice(2 * I1 + i * P, 2 * I1 + (i + 1) * P)
                        last = mm3(pe, ps[:, 4 + b], fwh[:, e % 2, at], fwl[:, e % 2, at], fah[:, k % 2, i], fal[:, k % 2, i],
                                   start=(e == 0 and i == 0), stop=(e == E - 1 and i == NI - 1))
                    last.then_inc(f_y if e < E - 1 else m_b[b], 1)

                gate_up(0)
                gate_up(1)
                for b in both:
                    comb_rows(1, b, "f_comb")
                pe.wait_ge(v_ones, 4)
                for b in both:
                    pe.wait_ge(m_cl[b], after("m_cl", 2))
                for n_ in range(E * B * NI):
                    if n_ % NI == 0:
                        weights(n_ // NI)
                    if n_ >= 2:
                        gate_up(n_)
                    if n_ % NI == 2 and n_ > NI:
                        down(n_ // NI - 1)
                pe.wait_ge(f_a, NI * (E * B - 1))
                moe_turn(2, 0, ps[:, 6])
                down(E * B - 1)
                pe.wait_ge(f_a, NI * E * B)
                moe_turn(2, 1, ps[:, 7])


def head(pair, j):
    i = 2 * pair + j
    return i % (H // QH) * QH + i // (H // QH)


GROUPS = 3 * H // 2
GROUP = [[(0, 4 * P, 0)], [(0, 3 * P, 0)], [(0, 2 * P, 0), (2 * P, P, 2)]]
NEARCOLS = [(3 * P - CLIP, WL), (2 * P - CLIP, WL), (P - CLIP, NEAR2)]
UNIT = [4 * P, 3 * P, 3 * P]
NEAR_LINKS = 2 + 1 + 2 * (CLIP + 1)
SBANK = [0, 3, 1, 2]
TBANK = [3, 0, 1, 2]


def constants():
    p = np.arange(P)
    heads = (p[:, None] // HD == np.arange(H)).astype(np.float32)
    blockd = (p[:, None] // HD == p // HD).astype(np.float32)
    away = p[:, None] + CLIP - np.arange(WL)
    dist = np.where(away < 0, -1, np.minimum(away, CLIP)).astype(np.float32)
    dist = np.concatenate([dist, dist[:, CLIP:]], 1)
    mask = np.where(dist < 0, BIG, 0.0).astype(np.float32)
    low = (np.arange(E)[None, :] < np.arange(E)[:, None]).astype(np.float32).reshape(1, E * E)
    return np.ascontiguousarray(np.concatenate(
        [np.eye(P, dtype=np.float32), blockd, dist, np.repeat(low, P, 0), heads, mask], 1))


STAGES = 6


def kernel(**a):
    import concourse.bacc as bacc
    from concourse.bass_utils import run_bass_kernel_spmd

    a = {k: np.asarray(v) for k, v in a.items()}
    w = {"aQK": a["L0_attn_QK"], "aVO": a["L0_attn_VO"],
         "cWq": a["L0_xattn_Wq"].T, "cWk": a["L0_xattn_Wk"].T, "cWv": a["L0_xattn_Wv"].T, "cWo": a["L0_xattn_Wo"].T,
         "mG": a["L0_ffn_gate_w"].T,
         "sWq": a["L1_attn_Wq"], "sWk": a["L1_attn_Wk"], "sWv": a["L1_attn_Wv"], "sWo": a["L1_attn_Wo"],
         "lWq": a["L1_xattn_Wq"].T, "lWk": a["L1_xattn_Wk"].T, "lWv": a["L1_xattn_Wv"].T, "lWo": a["L1_xattn_Wo"].T,
         "fG": a["L1_ffn_conf_w"].T}
    r = {"cbv": "L0_xattn_bv", "cbo": "L0_xattn_bo", "sbo": "L1_attn_bo", "lbk": "L1_xattn_bk", "lbv": "L1_xattn_bv",
         "lbo": "L1_xattn_bo", "fb": "L1_ffn_conf_b", "fw": "L1_ffn_wealth", "rel": "L1_attn_rel_emb"}
    c = {"cbq": "L0_xattn_bq", "cbk": "L0_xattn_bk", "lbq": "L1_xattn_bq"}
    cc = np.ascontiguousarray
    arrays = {
        "x": cc(a["x"]),
        "cst": constants(),
        "wts": cc(np.concatenate([w[n] for n in WEIGHTS], 1)),
        "rows": cc(np.concatenate([a[r[n]] for n in ROWS])),
        "cols": cc(np.concatenate([a[c[n]][:, None] for n in COLS] + [a["L0_ffn_b1"].T], 1)),
        "ctxT": cc(a["ctx_1024"].transpose(2, 0, 1)),
        "b2": cc(np.concatenate([a["L0_ffn_b2"], np.zeros((P - E, D), np.float32)])),
        "w12": cc(np.stack([a["L0_ffn_w1"].transpose(2, 0, 1), a["L0_ffn_w2"].transpose(2, 0, 1)], 1)),
        "fgu": cc(np.stack([a["L1_ffn_gate_w"].transpose(2, 0, 1), a["L1_ffn_up_w"].transpose(2, 0, 1)], 2)),
        "fdn": cc(a["L1_ffn_down_w"].reshape(E, D, NI, P).transpose(3, 0, 2, 1)),
    }
    nc = bacc.Bacc("TRN2", target_bir_lowering=False, num_devices=1)
    d = {n: nc.dram_tensor(f"in_{n}", v.shape, mybir.dt.from_np(v.dtype), kind="ExternalInput").ap()
         for n, v in arrays.items()}
    out = nc.dram_tensor("out_x", (B, T, D), F32, kind="ExternalOutput").ap()
    build(nc, d, out, STAGES)
    got = run_bass_kernel_spmd(nc, [{f"in_{n}": v for n, v in arrays.items()}], core_ids=[0])
    return got.results[0]["out_x"]
```

```python
from contextlib import ExitStack

import numpy as np
import concourse.bass as bass
from concourse import mybir

P = 128
D = 128
B, T = 2, 512
NC = T // P
H, HD = 16, 8
QH, QC = 4, 32
TK = 77
HS, HPB = 18, 6
E = 8
I1 = 512
NI = I1 // P
CAP = int(1.25 * B * T / E)
CLIP = 16
WL = P + CLIP
SLOTS = H // QH
KR = QH * 3 * HD
NEAR2 = WL + P
BIG = -1e30

F32 = mybir.dt.float32
F32R = mybir.dt.float32r
BF16 = mybir.dt.bfloat16
ALU = mybir.AluOpType
ACT = mybir.ActivationFunctionType
AX = mybir.AxisListType

WEIGHTS = ["aQK", "aVO", "cWq", "cWk", "cWv", "cWo", "mG", "sWq", "sWk", "sWv", "sWo", "lWq", "lWk", "lWv", "lWo", "fG"]
WIDTH = {"mG": E, "fG": E, "sWq": SLOTS * KR, "sWk": SLOTS * KR}
ROWS = ["cbv", "cbo", "sbo", "lbk", "lbv", "lbo", "fb", "fw", "rel"]
RWIDTH = {"fb": E, "fw": E, "rel": CLIP + 1}
COLS = ["cbq", "cbk", "lbq"]
CONSTS = ["ident", "block", "dist", "lower", "heads", "mask", "signs", "rowhead"]
CWIDTH = {"signs": 4, "rowhead": QH, "dist": NEAR2, "mask": NEAR2, "lower": E * E, "heads": H}


PE_STEPS = ["k_ps", "a_proj", "a_proj", "k_ps", "a_o", "c_qps", "g_ps", "m_ct", "m_b", "m_yp", "q_vps",
            "l_qps", "l_nps", "g_ps", "m_ct", "m_b", "m_yp"]
DVE_STEPS = ["k_sb", "a_v", "k_sb", "c_q", "o_fin", "g_sub", "g_sel", "g_comb", "m_cl", "q_v",
             "o_fin", "l_q", "o_fin", "f_z", "f_bs", "f_comb", "m_cl"]
ACT_STEPS = ["a_q", "g_e", "m_ctr", "m_yt", "f_ez", "f_eb", "m_ctr", "m_yt"]


def offsets(names, widths):
    at, out = 0, {}
    for n in names:
        out[n] = (at, at + widths.get(n, D))
        at = out[n][1]
    return out, at


W_AT, W_ALL = offsets(WEIGHTS, WIDTH)
R_AT, R_ALL = offsets(ROWS, RWIDTH)
C_AT, C_ALL = offsets(CONSTS, CWIDTH)


def build(nc, d, out, stages=6):
    with ExitStack() as ctx:
        def sb(name, shape, dt=F32):
            return ctx.enter_context(nc.sbuf_tensor(name, shape, dt))

        def sem(name):
            return ctx.enter_context(nc.semaphore(name))

        def sems(name):
            return [sem(f"{name}{b}") for b in range(B)]

        both = range(B)
        wts = sb("wts", [P, W_ALL])
        rows = sb("rows", [P, R_ALL])
        cols = sb("cols", [P, len(COLS) + E])
        cst = sb("cst", [P, C_ALL])
        b2 = sb("b2", [P, D])
        ctxT = sb("ctxT", [P, B, TK])
        x = sb("x", [P, B, NC, D])
        xb = sb("xb", [P, B, NC, D])
        xn = sb("xn", [P, B, NC, D])
        xnT = sb("xnT", [P, B, T])
        xnTh = sb("xnTh", [P, B, T], F32R)
        xnTl = sb("xnTl", [P, B, T], F32R)
        stats = sb("stats", [P, B, NC, 6])
        mv = sb("mv", [P, B, NC, 2])
        vare = sb("vare", [P, B, NC])
        rstd = sb("rstd", [P, B, NC])
        mhalf = sb("mhalf", [P, NC])
        ones = sb("ones", [P, P])
        ps = ctx.enter_context(nc.psum_tensor("ps", [P, 2 * NC, 512], F32))

        W = {n: wts[:, a:b] for n, (a, b) in W_AT.items()}
        R = {n: rows[:, a:b] for n, (a, b) in R_AT.items()}
        C = {n: cst[:, a:b] for n, (a, b) in C_AT.items()}
        ident = C["ident"]

        def bank(b, i):
            return ps[:, NC * b + i, :]

        def route_bank(l, b):
            return ps[:, 6 + b, :] if l else bank(b, 3)

        probT = sb("probT", [P, B, NC, T])
        cqT = sb("cqT", [P, B, T])
        oacc = sb("oacc", [P, B, T])
        o = sb("o", [P, B, NC, D])
        oT = sb("oT", [P, B, T])
        lkv = sb("lkv", [P, B, D + H])
        rz = sb("rz", [P, B, NC, H])
        lg = sb("lg", [P, B, NC, E])
        pe_ = sb("pe_", [P, B, NC, E])
        gm = sb("gm", [P, B, NC])
        gs = sb("gs", [P, B, NC])
        cmpg = sb("cmpg", [P, B, NC, E, E])
        cmpe = sb("cmpe", [P, B, NC, E, E])
        rank = sb("rank", [P, B, NC, E])
        sel = sb("sel", [P, B, NC, E])
        comb = sb("comb", [P, B, NC, P])
        maskb = sb("maskb", [P, NEAR2 + P], BF16)
        identb = maskb[:, NEAR2:]
        near = sb("near", [P, NEAR2])
        hit = sb("hit", [P, NEAR2])
        svp = sb("svp", [P, B, NC, H, QC])
        snm = sb("snm", [P, 2, 4])
        scale = sb("scale", [P, 4])

        outer, phase = ctx, ExitStack()
        ctx = phase
        xqkT = sb("xqkT", [P, B, T])
        xvo = oacc[:, :, :].rearrange("p b (c d) -> p b c d", c=NC)
        negm = sb("negm", [P, B, NC])
        rsum = sb("rsum", [P, B, NC])
        rinv = sb("rinv", [P, B, NC])
        prob = sb("prob", [P, B, NC, T])
        ckT = sb("ckT", [P, B, TK])
        ckb = sb("ckb", [P, B, HS, TK])
        cvp = sb("cvp", [TK, B, H, QC])
        cmax = sb("cmax", [P, B, HS])
        shifted = prob[:, :, 0:3, :].rearrange("p b c t -> p b (c t)")[:, :, 0:HS * TK]
        cprob = shifted
        cprobT = probT[0:TK, :, :, :]
        lk = sb("lk", [TK, B, D])
        lv = sb("lv", [TK, B, D])
        valid = sb("valid", [P, E])
        w12 = sb("w12", [P, 2, E, D])
        w12h = sb("w12h", [P, 2, E, D], F32R)
        w12l = sb("w12l", [P, 2, E, D], F32R)
        hid = sb("hid", [P, B, 2, T])
        hidh = sb("hidh", [P, B, 2, T], F32R)
        hidl = sb("hidl", [P, B, 2, T], F32R)
        combTh0, combTl0 = (sb(n, [P, B, T], F32R) for n in ("combTh0", "combTl0"))
        b2h, b2l = (sb(n, [P, D], F32R) for n in ("b2h", "b2l"))
        pick0 = sb("pick0", [P, E, P], F32R)
        phase.close()

        QS, QA, KK = range(3)
        reps = sb("reps", [KR, B, 3, SLOTS, T], F32R)
        high = sb("high", [KR, 2, 3, T], F32R)
        khead = sb("khead", [KR, H, T], F32R)
        sprob = probT[:, 1].rearrange("p (a j) t -> p a j t", a=2)
        sprobT = probT[:, 0]
        phase.close()

        fw = sb("fw", [P, 2, 3 * I1])
        fwh = sb("fwh", [P, 2, 3 * I1], F32R)
        fwl = sb("fwl", [P, 2, 3 * I1], F32R)
        sg = sb("sg", [P, 2, T])
        fa = probT
        fah = sb("fah", [P, 2, NI, T], F32R)
        fal = sb("fal", [P, 2, NI, T], F32R)
        combTh1, combTl1 = (sb(n, [P, B, T], F32R) for n in ("combTh1", "combTl1"))
        pick1 = sb("pick1", [P, E, P], F32R)
        combTh, combTl, pick = (combTh0, combTh1), (combTl0, combTl1), (pick0, pick1)
        outer.push(phase)
        ctx = outer

        d_x = sem("d_x"); d_cst = sem("d_cst"); d_w = sem("d_w"); d_r = sem("d_r"); d_w12 = sem("d_w12"); d_out = sem("d_out")
        mask_ready = sem("mask_ready"); d_f = sems("d_f")
        consts = sem("consts")
        v_ones = sem("v_ones")
        near_ready = sem("near_ready")
        dve_done = sem("dve_done")
        pool_done = sem("pool_done")
        var_ready, rstd_ready, xn_ready = sems("var_ready"), sems("rstd_ready"), sems("xn_ready")
        xnt_ps, xnt_ready, xnl_ready = sems("xnt_ps"), sems("xnt_ready"), sems("xnl_ready")
        x_ready, xb_ready = sems("x_ready"), sems("xb_ready")
        ot_ps, ot_ready, y_ps = sems("ot_ps"), sems("ot_ready"), sems("y_ps")

        pe_step, dve_step, act_step = sems("pe_step"), sems("dve_step"), sems("act_step")
        order = {}
        for names in (PE_STEPS, DVE_STEPS, ACT_STEPS):
            for i, name in enumerate(names):
                order.setdefault(name, []).append(i + 1)

        def after(name, n=1):
            return order[name][n - 1]

        k_ps = a_proj = a_o = c_qps = g_ps = m_ct = m_b = m_yp = q_vps = l_qps = l_nps = pe_step
        k_sb = a_v = c_q = g_sub = g_sel = g_comb = m_cl = q_v = o_fin = l_q = f_z = f_bs = f_comb = dve_step
        a_q = g_e = m_ctr = m_yt = f_ez = f_eb = act_step

        a_s, a_m, a_e, a_t, a_pt = (sems(n) for n in ("a_s", "a_m", "a_e", "a_t", "a_pt"))
        c_s, c_sub, c_e, c_sum, c_t, c_pt, c_o, c_on = (sems(n) for n in (
            "c_s", "c_sub", "c_e", "c_sum", "c_t", "c_pt", "c_o", "c_on"))
        g_cnt = sem("g_cnt")
        w12_split = sem("w12_split")
        m_hps, m_h, m_cb, m_hc, m_hh, m_hl, m_y = (sems(n) for n in ("m_hps", "m_h", "m_cb", "m_hc", "m_hh", "m_hl", "m_y"))
        s_s, s_m, s_e, s_t, s_o, s_on = (sems(n) for n in ("s_s", "s_m", "s_e", "s_t", "s_o", "s_on"))
        p_ps, p_high, p_done, p_head = (sems(n) for n in ("p_ps", "p_high", "p_done", "p_head"))
        s_pt = [[sem(f"s_pt{b}_{i}") for i in range(3)] for b in both]
        f_wh = sem("f_wh"); f_wl = sem("f_wl")
        f_g, f_u, f_s, f_cb, f_a, f_ah, f_al, f_y = (sem(n) for n in (
            "f_g", "f_u", "f_s", "f_cb", "f_a", "f_ah", "f_al", "f_y"))

        block = ctx.enter_context(nc.Block())

        def mm3(pe, dst, lh, ll, rh, rl, start=True, stop=True):
            pe.matmul(dst, lh, rh, start=start, stop=False)
            pe.matmul(dst, lh, rl, start=False, stop=False)
            return pe.matmul(dst, ll, rh, start=False, stop=stop)

        @block.sync
        def _(sp):
            for b in both:
                sp.dma_start(x[:, b], d["x"][b].rearrange("(c p) d -> p c d", p=P)).then_inc(d_x, 16)
            sp.dma_start(cst[:, :], d["cst"]).then_inc(d_cst, 16)
            sp.dma_start(ctxT[:, :, :], d["ctxT"]).then_inc(d_w, 16)
            sp.dma_start(wts[:, :], d["wts"]).then_inc(d_w, 16)
            sp.dma_start(cols[:, :], d["cols"]).then_inc(d_r, 16)
            sp.dma_start(rows[:, :], d["rows"].partition_broadcast(P)).then_inc(d_r, 16)
            sp.dma_start(b2[:, :], d["b2"]).then_inc(d_r, 16)
            sp.dma_start(w12[:, :, :, :], d["w12"]).then_inc(d_w12, 16)
            if stages > 5:
                for b in both:
                    sp.wait_ge(x_ready[b], 4)
                for e in range(E):
                    if e >= 2:
                        sp.wait_ge(f_wl, 3 * (e - 1))
                    sp.dma_start(fw[:, e % 2, 0:2 * I1], d["fgu"][:, e]).then_inc(d_f[e % 2], 16)
                    sp.dma_start(fw[:, e % 2, 2 * I1:], d["fdn"][:, e]).then_inc(d_f[e % 2], 16)
            for b in both:
                sp.wait_ge(x_ready[b], stages)
                sp.dma_start(out[b].rearrange("(c p) d -> p c d", p=P), x[:, b]).then_inc(d_out, 16)
            sp.wait_ge(d_out, 16 * B)

        @block.gpsimd
        def _(pool):
            links = [0]

            def link(ins):
                links[0] += 1
                ins.then_inc(pool_done, 1)
                pool.wait_ge(pool_done, links[0])

            def rstds(k, b):
                pool.wait_ge(var_ready[b], k + 1)
                link(pool.tensor_scalar(vare[:, b, :], mv[:, b, :, 1], 1e-5, None, ALU.add))
                pool.tensor_tensor(rstd[:, b, :], vare[:, b, :], mhalf[:, :], ALU.pow).then_inc(rstd_ready[b], 1)

            def add_bias(k, b, row):
                if k:
                    pool.wait_ge(x_ready[b], k)
                pool.tensor_tensor(xb[:, b], x[:, b], R[row].unsqueeze(1).broadcast_to([P, NC, D]),
                                   ALU.add).then_inc(xb_ready[b], 1)

            link(pool.memset(mhalf[:, :], -0.5))
            for b in both:
                rstds(0, b)
            pool.memset(cvp[:, :, :, :], 0.0).then_inc(consts, 1)
            pool.memset(ones[:, :], 1.0).then_inc(consts, 1)
            pool.memset(ckb[:, :, H:HS, :], 0.0).then_inc(consts, 1)
            pool.memset(comb[:, :, :, :], 0.0).then_inc(v_ones, 1)
            pool.wait_ge(d_cst, 16)
            for b in both:
                pool.wait_ge(k_sb[b], after("k_sb"))
                pool.tensor_tensor(ckb[:, b, 0:H], ckT[:, b].unsqueeze(1).broadcast_to([P, H, TK]),
                                   C["heads"].unsqueeze(2).broadcast_to([P, H, TK]), ALU.mult).then_inc(consts, 1)
            pool.tensor_copy(pick0[:, :, :], ident[:, 0:E].unsqueeze(2).broadcast_to([P, E, P])).then_inc(v_ones, 1)
            if stages > 1:
                for b in both:
                    rstds(1, b)
                pool.wait_ge(d_r, 16 * 3)
                for b in both:
                    add_bias(1, b, "cbo")
                pool.wait_ge(d_w12, 16)
                pool.tensor_copy(b2h[:, :], b2[:, :])
                link(pool.tensor_copy(w12h[:, :, :, :], w12[:, :, :, :]))
                pool.tensor_tensor(b2l[:, :], b2[:, :], b2h[:, :].bitcast(F32), ALU.subtract)
                pool.tensor_tensor(w12l[:, :, :, :], w12[:, :, :, :], w12h[:, :, :, :].bitcast(F32),
                                   ALU.subtract).then_inc(w12_split, 1)
            if stages > 3:
                pool.wait_ge(d_r, 16 * 3)
                pool.memset(svp[:, :, :, :, :], 0.0).then_inc(v_ones, 1)
                pool.tensor_copy(maskb[:, 0:NEAR2], C["mask"]).then_inc(mask_ready, 1)
                pool.tensor_copy(identb, ident).then_inc(mask_ready, 1)
                dist = C["dist"]
                link(pool.tensor_scalar(near[:, :], dist, -1.0, None, ALU.is_equal))
                for k in range(CLIP + 1):
                    link(pool.tensor_scalar(hit[:, :], dist, float(k), R["rel"][:, k:k + 1], ALU.is_equal, ALU.mult))
                    last = pool.tensor_tensor(near[:, :], near[:, :], hit[:, :], ALU.add)
                    if k < CLIP:
                        link(last)
                link(last)
                for i, col in enumerate((0, 1)):
                    pool.tensor_copy(scale[:, i:i + 1], C["signs"][:, col:col + 1])
                    last = pool.tensor_tensor(scale[:, 2 + i:3 + i], C["signs"][:, col:col + 1], R["rel"][:, CLIP:CLIP + 1],
                                              ALU.mult)
                last.then_inc(near_ready, 1)
            if stages > 2:
                for b in both:
                    rstds(2, b)
                for e in range(E):
                    for b in both:
                        pool.wait_ge(m_hh[b], e + 1)
                        if e >= 2:
                            pool.wait_ge(m_y[b], e - 1)
                        pool.tensor_tensor(hidl[:, b, e % 2], hid[:, b, e % 2], hidh[:, b, e % 2].bitcast(F32),
                                           ALU.subtract).then_inc(m_hl[b], 1)
            if stages > 3:
                for b in both:
                    rstds(3, b)
                for b in both:
                    for i in range(H):
                        if i % QH == 0:
                            pool.wait_ge(p_done[b], 2 * (i // QH) + 2)
                        if b and i % 2 == 0:
                            pool.wait_ge(s_s[0], 3 * (i // 2) + 3)
                        pool.tensor_tensor(khead[:, i], reps[:, b, KK, i // QH].bitcast(F32),
                                           C["rowhead"][0:KR, i % QH:i % QH + 1].broadcast_to([KR, T]), ALU.mult)\
                            .then_inc(p_head[b], 1)
                    add_bias(3, b, "sbo")
            if stages > 4:
                for b in both:
                    rstds(4, b)
                    add_bias(4, b, "lbo")
            if stages > 5:
                for b in both:
                    pool.wait_ge(s_on[b], 1)
                for part in range(3):
                    pool.wait_ge(f_wh, part + 1)
                    at = slice(part * I1, (part + 1) * I1)
                    pool.tensor_tensor(fwl[:, 0, at], fw[:, 0, at], fwh[:, 0, at].bitcast(F32), ALU.subtract).then_inc(f_wl, 1)
                pool.tensor_copy(pick1[:, :, :], ident[:, 0:E].unsqueeze(2).broadcast_to([P, E, P])).then_inc(v_ones, 1)
            if stages > 5:
                for b in both:
                    rstds(5, b)
                for n_ in range(E * B * NI):
                    k, i = divmod(n_, NI)
                    pool.wait_ge(f_ah, n_ + 1)
                    if k >= 2:
                        pool.wait_ge(f_y, k - 1)
                    pool.tensor_tensor(fal[:, k % 2, i], fa[:, k % 2, i], fah[:, k % 2, i].bitcast(F32),
                                       ALU.subtract).then_inc(f_al, 1)

        @block.scalar
        def _(act):
            def xnt(k, b):
                act.wait_ge(xnt_ps[b], k + 1)
                act.activation(xnT[:, b], bank(b, 0), ACT.Copy).then_inc(xnt_ready[b], 1)

            def ot(n, b, i):
                act.wait_ge(ot_ps[b], n + 1)
                act.activation(oT[:, b], bank(b, i), ACT.Copy).then_inc(ot_ready[b], 1)

            def comb_rows(n_, b):
                act.wait_ge(m_ct[b], after("m_ct", n_))
                act.activation(combTh[n_ - 1][:, b], route_bank(n_ - 1, b), ACT.Copy).then_inc(m_ctr[b], 1)

            def moe_out(n_, b, acc):
                act.wait_ge(m_b[b], after("m_b", n_))
                act.activation(oT[:, b], acc, ACT.Copy).then_inc(m_yt[b], 1)

            def wh(e, part):
                if part == 0:
                    act.wait_ge(d_f[e % 2], 32 * (e // 2 + 1))
                    if e >= 2:
                        act.wait_ge(f_y, B * (e - 1))
                at = slice(part * I1, (part + 1) * I1)
                act.activation(fwh[:, e % 2, at], fw[:, e % 2, at], ACT.Copy).then_inc(f_wh, 1)

            for b in both:
                xnt(0, b)
            for b in both:
                act.wait_ge(a_proj[b], after("a_proj"))
                act.activation(xqkT[:, b], bank(b, 1), ACT.Copy, scale=float(D) ** -0.5).then_inc(a_q[b], 1)
            for b in both:
                for c in range(NC):
                    act.wait_ge(a_m[b], c + 1)
                    act.activation(prob[:, b, c], bank(b, SBANK[c]), ACT.Exp, bias=negm[:, b, c:c + 1],
                                   accum_out=rsum[:, b, c:c + 1]).then_inc(a_e[b], 1)
            for b in both:
                for u in (0, 2):
                    act.wait_ge(a_t[b], u + 1)
                    act.activation(probT[:, b, u], bank(b, SBANK[u]), ACT.Copy).then_inc(a_pt[b], 1)
            if stages > 1:
                for b in both:
                    xnt(1, b)
                for c in range(NC):
                    for b in both:
                        act.wait_ge(c_sub[b], c + 1)
                        act.activation(cprob[:, b], shifted[:, b], ACT.Exp).then_inc(c_e[b], 1)
                        for u in range(NC):
                            act.wait_ge(c_t[b], NC * c + u + 1)
                            act.activation(cprobT[:, b, u], bank(b, TBANK[u])[0:TK, :], ACT.Copy).then_inc(c_pt[b], 1)
            if stages > 2:
                for b in both:
                    xnt(2, b)
                    act.activation(xnTh[:, b], bank(b, 0), ACT.Copy).then_inc(xnl_ready[b], 1)
                for b in both:
                    act.wait_ge(g_sub[b], after("g_sub"))
                    act.activation(pe_[:, b], lg[:, b], ACT.Exp).then_inc(g_e[b], 1)
                for b in both:
                    comb_rows(1, b)
                for e in range(E):
                    for b in both:
                        act.wait_ge(m_hps[b], e + 1)
                        if e >= 2:
                            act.wait_ge(m_hl[b], e - 1)
                        act.activation(hid[:, b, e % 2], bank(b, e % 2), ACT.Silu,
                                       bias=cols[:, len(COLS) + e:len(COLS) + e + 1]).then_inc(m_h[b], 1)
                    for b in both:
                        act.wait_ge(m_hc[b], e + 1)
                        if e >= 2:
                            act.wait_ge(m_y[b], e - 1)
                        act.activation(hidh[:, b, e % 2], hid[:, b, e % 2], ACT.Copy).then_inc(m_hh[b], 1)
                for b in both:
                    moe_out(1, b, bank(b, 2))
            if stages > 3:
                for b in both:
                    xnt(3, b)
                act.wait_ge(near_ready, 1)

                def highs(b, u):
                    act.wait_ge(p_ps[b], u + 1)
                    if u >= 4:
                        act.wait_ge(p_done[b], u - 3)
                    elif b:
                        act.wait_ge(p_done[b - 1], 2 * SLOTS - 3 + u)
                    half = high[:, u // 2 % 2]
                    if u % 2:
                        last = act.activation(half[:, KK], ps[0:KR, PBANK[u]], ACT.Copy, scale=C["signs"][0:KR, 2:3])
                    else:
                        act.activation(half[:, QS], ps[0:KR, PBANK[u]], ACT.Copy, scale=scale[0:KR, 0:1])
                        last = act.activation(half[:, QA], ps[0:KR, PBANK[u]], ACT.Copy, scale=scale[0:KR, 2:3])
                    last.then_inc(p_high[b], 1)

                for b in both:
                    for u in range(2 * SLOTS):
                        highs(b, u)

                    def exps(n):
                        kind, par = n % 3, n % 2
                        act.wait_ge(s_m[b], n + 1)
                        if n >= 2:
                            act.wait_ge(s_t[b], 2 * (n - 1))
                        elif b:
                            act.wait_ge(s_t[b - 1], 2 * (GROUPS - 1 + n))
                        for j in range(2):
                            for i, (at, w, m) in enumerate(GROUP[kind]):
                                c, h = NC - 1 - kind - i, head(n // 3, j)
                                last = act.activation(sprob[:, par, j, at:at + w], ps[:, 2 * par + j, at:at + w], ACT.Exp,
                                                      bias=snm[:, par, m + j:m + j + 1], accum_out=rz[:, b, c, h:h + 1])
                            last.then_inc(s_e[b], 1)

                    def evac(m):
                        if m % 3 == 1:
                            return
                        act.wait_ge(s_t[b], m + 1)
                        if m >= 4:
                            act.wait_ge(s_o[b], m - 3)
                        w = UNIT[m // 2 % 3]
                        act.activation(sprobT[:, m % 4, 0:w], ps[:, 4 + m % 3, 0:w], ACT.Copy).then_inc(s_pt[b][m % 3], 1)

                    for n in range(GROUPS):
                        exps(n)
                        if n:
                            evac(2 * n - 2)
                            evac(2 * n - 1)
                    evac(2 * GROUPS - 2)
                    evac(2 * GROUPS - 1)
            if stages > 4:
                for b in both:
                    xnt(4, b)
                if stages > 5:
                    for part in range(3):
                        wh(0, part)
                for b in both:
                    ot(2, b, 0)
            if stages > 5:
                for b in both:
                    xnt(5, b)
                    act.activation(xnTh[:, b], bank(b, 0), ACT.Copy).then_inc(xnl_ready[b], 1)
                for b in both:
                    act.wait_ge(f_z[b], after("f_z"))
                    act.activation(pe_[:, b], lg[:, b], ACT.Exp, scale=-1.0).then_inc(f_ez[b], 1)
                for b in both:
                    act.wait_ge(f_bs[b], after("f_bs"))
                    act.activation(pe_[:, b], lg[:, b], ACT.Exp).then_inc(f_eb[b], 1)
                    if b == 0:
                        comb_rows(2, 0)

                def ah(n_):
                    k, i = divmod(n_, NI)
                    act.wait_ge(f_a, n_ + 1)
                    if k >= 2:
                        act.wait_ge(f_y, k - 1)
                    act.activation(fah[:, k % 2, i], fa[:, k % 2, i], ACT.Copy).then_inc(f_ah, 1)

                for n_ in range(E * B * NI):
                    e, k = n_ // (B * NI), n_ // NI
                    if n_ == 3:
                        comb_rows(2, 1)
                    act.wait_ge(f_g, n_ + 1)
                    if n_ >= 2:
                        act.wait_ge(f_a, n_ - 1)
                    act.activation(sg[:, n_ % 2], ps[:, 2 * (n_ % 2)], ACT.Silu).then_inc(f_s, 1)
                    if n_:
                        ah(n_ - 1)
                    part = n_ % (B * NI) - NI + 1
                    if 0 <= part < 3 and e < E - 1:
                        wh(e + 1, part)
                moe_out(2, 0, ps[:, 4])
                ah(E * B * NI - 1)
                moe_out(2, 1, ps[:, 5])

        @block.vector
        def _(dve):
            links = [0]

            def link(ins):
                links[0] += 1
                ins.then_inc(dve_done, 1)
                dve.wait_ge(dve_done, links[0])

            def norm_stats(k, b):
                if k:
                    dve.wait_ge(x_ready[b], k)
                for c in range(NC):
                    last = dve.bn_stats(stats[:, b, c], x[:, b, c])
                link(last)
                for c in range(NC):
                    last = dve.bn_aggr(mv[:, b, c], stats[:, b, c])
                last.then_inc(var_ready[b], 1)

            def norm_apply(k, b):
                dve.wait_ge(rstd_ready[b], k + 1)
                for c in range(NC):
                    dve.tensor_scalar(xn[:, b, c], x[:, b, c], mv[:, b, c, 0:1], rstd[:, b, c:c + 1],
                                      ALU.subtract, ALU.mult).then_inc(xn_ready[b], 1)

            def tail(n_, b, i):
                dve.wait_ge(xb_ready[b], n_ + 1)
                dve.wait_ge(y_ps[b], n_ + 1)
                dve.tensor_tensor(x[:, b].rearrange("p c d -> p (c d)"), bank(b, i),
                                  xb[:, b].rearrange("p c d -> p (c d)"), ALU.add).then_inc(x_ready[b], 1)

            dve.wait_ge(d_x, 16 * B)
            for b in both:
                norm_stats(0, b)
            for b in both:
                norm_apply(0, b)
            dve.wait_ge(d_r, 16 * 3)
            dve.wait_ge(consts, 3)
            for b in both:
                dve.wait_ge(k_ps[b], after("k_ps"))
                dve.tensor_scalar(ckT[:, b], bank(b, 3)[:, 0:TK], cols[:, 1:2], None, ALU.add)
                for j in range(QH):
                    def slot(v):
                        return v.rearrange("p (g j e) -> p g j e", j=QH, e=HD)[:, :, j]
                    dve.tensor_tensor(cvp[:, b].rearrange("p (g j) q -> p g j q", j=QH)[:, :, j, j * HD:(j + 1) * HD],
                                      slot(bank(b, 3)[0:TK, 128:256]), slot(R["cbv"][0:TK, :]), ALU.add)
                link(dve.tensor_tensor(lk[:, b], bank(b, 3)[0:TK, 256:384], R["lbk"][0:TK, :], ALU.add))
                link(dve.tensor_scalar(lk[:, b], lk[:, b], float(HD) ** -0.5, 0.0, ALU.mult, ALU.max))
                dve.tensor_scalar(lk[:, b], lk[:, b], 1e-6, None, ALU.add)
                dve.tensor_tensor(lv[:, b], bank(b, 3)[0:TK, 384:512], R["lbv"][0:TK, :], ALU.add).then_inc(k_sb[b], 1)
            for b in both:
                dve.wait_ge(a_proj[b], after("a_proj", 2))
                dve.tensor_copy(xvo[:, b].rearrange("p c d -> p (c d)"), bank(b, 2)).then_inc(a_v[b], 1)
            for b in both:
                dve.wait_ge(k_ps[b], after("k_ps", 2))
                dve.tensor_tensor(lkv[:, b, 0:D], bank(b, 3)[:, 0:D], C["block"], ALU.mult)
                dve.tensor_tensor(lkv[:, b, D:D + H], bank(b, 3)[:, D:D + H], C["heads"], ALU.mult).then_inc(k_sb[b], 1)
            for b in both:
                for c in range(NC):
                    dve.wait_ge(a_s[b], c + 1)
                    dve.tensor_reduce(negm[:, b, c:c + 1], bank(b, SBANK[c]), AX.X, ALU.max, negate=True)\
                        .then_inc(a_m[b], 1)
            for b in both:
                dve.wait_ge(a_e[b], NC)
                link(dve.reciprocal(rinv[:, b], rsum[:, b]))
                for u in (1, 3):
                    dve.wait_ge(a_t[b], u + 1)
                    dve.tensor_copy(probT[:, b, u], bank(b, SBANK[u])).then_inc(a_pt[b], 1)
            for b in both:
                dve.wait_ge(a_o[b], after("a_o"))
                for c in range(NC):
                    last = dve.scalar_tensor_tensor(x[:, b, c], bank(b, 0)[:, c * D:(c + 1) * D], rinv[:, b, c:c + 1],
                                                    x[:, b, c], ALU.mult, ALU.add)
                last.then_inc(x_ready[b], 1)
                if stages > 1:
                    norm_stats(1, b)

            def spread_inverse(b):
                link(dve.reciprocal(rz[:, b], rz[:, b]))
                for c in range(NC):
                    last = dve.tensor_copy(o[:, b, c].rearrange("p (h e) -> p h e", e=HD),
                                           rz[:, b, c].unsqueeze(2).broadcast_to([P, H, HD]))
                last.then_inc(o_fin[b], 1)

            def scale_outputs(n_, b):
                dve.wait_ge(ot_ps[b], n_)
                dve.tensor_tensor(oT[:, b], bank(b, 0), oacc[:, b], ALU.mult).then_inc(ot_ready[b], 1)

            if stages > 1:
                for b in both:
                    norm_apply(1, b)
                for b in both:
                    dve.wait_ge(c_qps[b], after("c_qps"))
                    dve.tensor_scalar(cqT[:, b], bank(b, 1), cols[:, 0:1], float(HD) ** -0.5, ALU.add, ALU.mult)\
                        .then_inc(c_q[b], 1)
                def shift(c, b):
                    s3 = ps[:, NC * b:NC * b + 3, 0:HPB * TK].rearrange("p a (h k) -> p a h k", k=TK)
                    m3 = cmax[:, b].rearrange("p (a h) -> p a h", h=HPB)
                    dve.wait_ge(c_s[b], c + 1)
                    link(dve.tensor_reduce(m3, s3, AX.X, ALU.max))
                    dve.tensor_tensor(shifted[:, b].rearrange("p (a h k) -> p a h k", h=HPB, k=TK), s3,
                                      m3.unsqueeze(3).broadcast_to([P, 3, HPB, TK]), ALU.subtract).then_inc(c_sub[b], 1)

                def sums(c, b):
                    dve.wait_ge(c_e[b], c + 1)
                    dve.tensor_reduce(rz[:, b, c], cprob[:, b, 0:H * TK].rearrange("p (h k) -> p h k", k=TK), AX.X, ALU.add)\
                        .then_inc(c_sum[b], 1)

                def outputs(c, b):
                    dve.wait_ge(c_o[b], c + 1)
                    dve.tensor_copy(oacc[:, b, c * P:(c + 1) * P], bank(b, 3)[:, c * P:(c + 1) * P]).then_inc(c_on[b], 1)

                for b in both:
                    shift(0, b)
                for c in range(NC):
                    for b in both:
                        sums(c, b)
                        if c + 1 < NC:
                            shift(c + 1, b)
                        outputs(c, b)
                for b in both:
                    dve.wait_ge(c_sum[b], NC)
                    spread_inverse(b)
                for b in both:
                    scale_outputs(1, b)
                for b in both:
                    tail(0, b, 1)
                    if stages > 2:
                        norm_stats(2, b)

            def ranks(b, v):
                other = v.unsqueeze(2).broadcast_to([P, NC, E, E])
                mine = v.unsqueeze(3).broadcast_to([P, NC, E, E])
                low = C["lower"].rearrange("p (i j) -> p i j", j=E).unsqueeze(1).broadcast_to([P, NC, E, E])
                dve.tensor_tensor(cmpg[:, b], other, mine, ALU.is_gt)
                link(dve.tensor_tensor(cmpe[:, b], other, mine, ALU.is_equal))
                link(dve.tensor_tensor(cmpe[:, b], cmpe[:, b], low, ALU.mult))
                link(dve.tensor_tensor(cmpg[:, b], cmpg[:, b], cmpe[:, b], ALU.add))
                link(dve.tensor_reduce(rank[:, b], cmpg[:, b], AX.X, ALU.add))
                return dve.tensor_scalar(sel[:, b], rank[:, b], 1.5, None, ALU.is_lt)

            def per_chunk(v):
                return v.unsqueeze(2).broadcast_to([P, NC, E])

            def comb_low(n_, b):
                dve.wait_ge(m_ctr[b], after("m_ctr", n_))
                dve.tensor_tensor(combTl[n_ - 1][:, b], route_bank(n_ - 1, b), combTh[n_ - 1][:, b].bitcast(F32), ALU.subtract).then_inc(m_cl[b], 1)

            def moe_add(n_, b, turned):
                dve.wait_ge(m_yp[b], after("m_yp", n_))
                dve.tensor_tensor(x[:, b].rearrange("p c d -> p (c d)"), turned,
                                  x[:, b].rearrange("p c d -> p (c d)"), ALU.add).then_inc(x_ready[b], 1)

            if stages > 2:
                for b in both:
                    norm_apply(2, b)
                for b in both:
                    dve.wait_ge(xnl_ready[b], 1)
                    dve.tensor_tensor(xnTl[:, b], xnT[:, b], xnTh[:, b].bitcast(F32), ALU.subtract).then_inc(xnl_ready[b], 1)
                for b in both:
                    g = bank(b, 3)[:, 0:NC * E].rearrange("p (c e) -> p c e", e=E)
                    dve.wait_ge(g_ps[b], after("g_ps"))
                    link(dve.tensor_reduce(gm[:, b], g, AX.X, ALU.max))
                    dve.tensor_tensor(lg[:, b], g, per_chunk(gm[:, b]), ALU.subtract).then_inc(g_sub[b], 1)
                for b in both:
                    dve.wait_ge(g_e[b], after("g_e"))
                    link(dve.tensor_reduce(gs[:, b], pe_[:, b], AX.X, ALU.add))
                    link(dve.reciprocal(gm[:, b], gs[:, b]))
                    link(dve.tensor_tensor(pe_[:, b], pe_[:, b], per_chunk(gm[:, b]), ALU.mult))
                    ranks(b, pe_[:, b]).then_inc(g_sel[b], 1)
                dve.wait_ge(g_cnt, 1)
                dve.wait_ge(v_ones, 2)
                link(dve.tensor_reduce(valid[:, :], bank(0, 3)[:, 64:64 + NC * E].rearrange("p (c e) -> p e c", e=E),
                                       AX.X, ALU.add))
                link(dve.tensor_scalar(valid[:, :], valid[:, :], CAP + 0.5, None, ALU.is_lt))
                for b in both:
                    link(dve.tensor_tensor(pe_[:, b], pe_[:, b], sel[:, b], ALU.mult))
                    dve.tensor_tensor(comb[:, b, :, 0:E], pe_[:, b], valid[:, :].unsqueeze(1).broadcast_to([P, NC, E]),
                                      ALU.mult).then_inc(g_comb[b], 1)
                for b in both:
                    comb_low(1, b)
                for e in range(E):
                    for b in both:
                        dve.wait_ge(m_h[b], e + 1)
                        dve.wait_ge(m_cb[b], e + 1)
                        dve.tensor_tensor(hid[:, b, e % 2], hid[:, b, e % 2], bank(b, 3), ALU.mult).then_inc(m_hc[b], 1)
                for b in both:
                    moe_add(1, b, bank(b, 1))
                    if stages > 3:
                        norm_stats(3, b)
            if stages > 3:
                for b in both:
                    norm_apply(3, b)
                dve.wait_ge(v_ones, 3)
                dve.wait_ge(near_ready, 1)

                def place_values(b):
                    dve.wait_ge(q_vps[b], after("q_vps"))
                    v4 = ps[:, VBANK].rearrange("p (c g j e) -> p c g j e", c=NC, j=QH, e=HD)
                    p4 = svp[:, b].rearrange("p c (g j) q -> p c g j q", j=QH)
                    for j in range(QH):
                        last = dve.tensor_copy(p4[:, :, :, j, j * HD:(j + 1) * HD], v4[:, :, :, j])
                    last.then_inc(q_v[b], 1)

                def lows(b, u):
                    dve.wait_ge(p_high[b], u + 1)
                    s_, whole, half = u // 2, ps[0:KR, PBANK[u]], high[:, u // 2 % 2]
                    if u % 2:
                        last = dve.scalar_tensor_tensor(reps[:, b, KK, s_], whole, C["signs"][0:KR, 3:4],
                                                        half[:, KK].bitcast(F32), ALU.mult, ALU.add)
                    else:
                        dve.scalar_tensor_tensor(reps[:, b, QS, s_], whole, scale[0:KR, 1:2],
                                                 half[:, QS].bitcast(F32), ALU.mult, ALU.add)
                        last = dve.scalar_tensor_tensor(reps[:, b, QA, s_], whole, scale[0:KR, 3:4],
                                                        half[:, QA].bitcast(F32), ALU.mult, ALU.add)
                    last.then_inc(p_done[b], 1)

                for b in both:
                    place_values(b)
                    for u in range(4):
                        lows(b, u)

                    def maxes(n):
                        kind, par = n % 3, n % 2
                        dve.wait_ge(s_s[b], n + 1)
                        at, w = NEARCOLS[kind]
                        two = ps[:, 2 * par:2 * par + 2, :]
                        link(dve.tensor_tensor(two[:, :, at:at + w], two[:, :, at:at + w],
                                               near[:, 0:w].unsqueeze(1).broadcast_to([P, 2, w]), ALU.mult))
                        for at, w, m in GROUP[kind]:
                            last = dve.tensor_reduce(snm[:, par, m:m + 2], two[:, :, at:at + w], AX.X, ALU.max, negate=True)
                        last.then_inc(s_m[b], 1)

                    def evac(m):
                        if m % 3 != 1:
                            return
                        dve.wait_ge(s_t[b], m + 1)
                        if m >= 4:
                            dve.wait_ge(s_o[b], m - 3)
                        w = UNIT[m // 2 % 3]
                        dve.tensor_copy(sprobT[:, m % 4, 0:w], ps[:, 4 + m % 3, 0:w]).then_inc(s_pt[b][m % 3], 1)

                    for n in range(GROUPS):
                        maxes(n)
                        if n in (1, 2):
                            lows(b, 2 * n + 2)
                            lows(b, 2 * n + 3)
                        if n >= 2:
                            evac(2 * n - 4)
                            evac(2 * n - 3)
                    evac(2 * GROUPS - 4)
                    evac(2 * GROUPS - 3)
                    evac(2 * GROUPS - 2)
                    evac(2 * GROUPS - 1)
                    dve.wait_ge(s_e[b], 2 * GROUPS)
                    spread_inverse(b)
                    dve.wait_ge(s_o[b], 2 * GROUPS)
                    dve.tensor_copy(oacc[:, b], ps[:, 7]).then_inc(s_on[b], 1)
                for b in both:
                    dve.wait_ge(s_on[b], 1)
                    scale_outputs(2, b)
                for b in both:
                    tail(1, b, 1)
                    if stages > 4:
                        norm_stats(4, b)
            if stages > 4:
                for b in both:
                    norm_apply(4, b)
                for b in both:
                    dve.wait_ge(l_qps[b], after("l_qps"))
                    link(dve.tensor_scalar(cqT[:, b], bank(b, 1), cols[:, 2:3], float(HD) ** -0.5, ALU.add, ALU.mult))
                    dve.tensor_scalar(cqT[:, b], cqT[:, b], 0.0, 1e-6, ALU.max, ALU.add).then_inc(l_q[b], 1)
                for b in both:
                    dve.wait_ge(l_nps[b], after("l_nps"))
                    two = ps[:, NC * b + 2:NC * b + 4, 0:2 * (D + H)].rearrange("p a (c n) -> p a c n", n=D + H)
                    link(dve.tensor_scalar(rz[:, b].rearrange("p (a c) h -> p a c h", c=2), two[:, :, :, D:], 1e-8, None, ALU.add))
                    link(dve.reciprocal(rz[:, b], rz[:, b]))
                    for c in range(NC):
                        last = dve.tensor_tensor(o[:, b, c].rearrange("p (h e) -> p h e", e=HD),
                                                 two[:, c // 2, c % 2, 0:D].rearrange("p (h e) -> p h e", e=HD),
                                                 rz[:, b, c].unsqueeze(2).broadcast_to([P, H, HD]), ALU.mult)
                    last.then_inc(o_fin[b], 1)
                for b in both:
                    tail(2, b, 1)
                    if stages > 5:
                        norm_stats(5, b)
            if stages > 5:
                for b in both:
                    norm_apply(5, b)
                for b in both:
                    dve.wait_ge(xnl_ready[b], 3)
                    dve.tensor_tensor(xnTl[:, b], xnT[:, b], xnTh[:, b].bitcast(F32), ALU.subtract).then_inc(xnl_ready[b], 1)

                def wl(e, part):
                    dve.wait_ge(f_wh, 3 * e + part + 1)
                    if e >= 2:
                        dve.wait_ge(f_y, B * (e - 1))
                    at = slice(part * I1, (part + 1) * I1)
                    dve.tensor_tensor(fwl[:, e % 2, at], fw[:, e % 2, at], fwh[:, e % 2, at].bitcast(F32),
                                      ALU.subtract).then_inc(f_wl, 1)

                def each(v):
                    return v.unsqueeze(1).broadcast_to([P, NC, E])

                for b in both:
                    dve.wait_ge(g_ps[b], after("g_ps", 2))
                    dve.tensor_tensor(lg[:, b], route_bank(1, b)[:, 0:NC * E].rearrange("p (c e) -> p c e", e=E), each(R["fb"]),
                                      ALU.add).then_inc(f_z[b], 1)

                def bids(b):
                    dve.wait_ge(f_ez[b], after("f_ez"))
                    link(dve.tensor_scalar(lg[:, b], pe_[:, b], 1.0, None, ALU.add))
                    link(dve.reciprocal(lg[:, b], lg[:, b]))
                    link(dve.tensor_tensor(lg[:, b], lg[:, b], each(R["fw"]), ALU.mult))
                    link(ranks(b, lg[:, b]))
                    link(dve.tensor_reduce(gm[:, b], lg[:, b], AX.X, ALU.max))
                    dve.tensor_tensor(lg[:, b], lg[:, b], per_chunk(gm[:, b]), ALU.subtract).then_inc(f_bs[b], 1)

                def shares(b):
                    dve.wait_ge(f_eb[b], after("f_eb"))
                    link(dve.tensor_tensor(pe_[:, b], pe_[:, b], sel[:, b], ALU.mult))
                    link(dve.tensor_reduce(gs[:, b], pe_[:, b], AX.X, ALU.add))
                    link(dve.reciprocal(gs[:, b], gs[:, b]))
                    dve.tensor_tensor(comb[:, b, :, 0:E], pe_[:, b], per_chunk(gs[:, b]), ALU.mult).then_inc(f_comb[b], 1)

                bids(0)
                shares(0)
                bids(1)
                comb_low(2, 0)
                shares(1)
                for n_ in range(E * B * NI):
                    k, i = divmod(n_, NI)
                    e, part = k // B, n_ % (B * NI) - NI
                    if n_ == 3:
                        comb_low(2, 1)
                    dve.wait_ge(f_s, n_ + 1)
                    dve.wait_ge(f_cb, k + 1)
                    if k >= 2:
                        dve.wait_ge(f_al, n_ - 2 * NI + 1)
                    link(dve.tensor_tensor(fa[:, k % 2, i], sg[:, n_ % 2], ps[:, 6 + k % 2], ALU.mult))
                    dve.wait_ge(f_u, n_ + 1)
                    dve.tensor_tensor(fa[:, k % 2, i], fa[:, k % 2, i], ps[:, 2 * (n_ % 2) + 1], ALU.mult).then_inc(f_a, 1)
                    if 0 <= part < 3 and e < E - 1:
                        wl(e + 1, part)
                for b in both:
                    moe_add(2, b, ps[:, 6 + b])

        @block.tensor
        def _(pe):
            def xnt(k, b):
                for c in range(NC):
                    pe.wait_ge(xn_ready[b], NC * k + c + 1)
                    last = pe.transpose(bank(b, 0)[:, c * P:(c + 1) * P], xn[:, b, c], ident)
                last.then_inc(xnt_ps[b], 1)

            def ot(n_, b, i):
                for c in range(NC):
                    last = pe.transpose(bank(b, i)[:, c * P:(c + 1) * P], o[:, b, c], ident)
                last.then_inc(ot_ps[b], 1)

            def wo(n_, b, i, w):
                pe.wait_ge(ot_ready[b], n_ + 1)
                for c in range(NC):
                    last = pe.matmul(bank(b, i)[:, c * D:(c + 1) * D], oT[:, b, c * P:(c + 1) * P], W[w],
                                     start=True, stop=True)
                last.then_inc(y_ps[b], 1)

            def comb_rows(l, b, made):
                pe.wait_ge(dve_step[b], after(made))
                for c in range(NC):
                    last = pe.transpose(route_bank(l, b)[:, c * P:(c + 1) * P], comb[:, b, c], ident)
                last.then_inc(m_ct[b], 1)

            def spread(dst, l, e, b):
                pe.matmul(dst, pick[l][:, e], combTh[l][:, b], start=True, stop=False)
                return pe.matmul(dst, pick[l][:, e], combTl[l][:, b], start=False, stop=True)

            def moe_turn(n_, b, dst):
                pe.wait_ge(m_yt[b], after("m_yt", n_))
                for c in range(NC):
                    last = pe.transpose(dst[:, c * P:(c + 1) * P], oT[:, b, c * P:(c + 1) * P], ident)
                last.then_inc(m_yp[b], 1)

            pe.wait_ge(d_w, 16 * 2)
            for b in both:
                pe.matmul(bank(b, 3)[:, 0:TK], W["cWk"], ctxT[:, b], start=True, stop=True)
                for i, w in enumerate(("cWv", "lWk", "lWv")):
                    last = pe.matmul(bank(b, 3)[0:TK, (i + 1) * 128:(i + 2) * 128], ctxT[:, b], W[w], start=True, stop=True)
                last.then_inc(k_ps[b], 1)
            pe.wait_ge(d_cst, 16)
            for b in both:
                xnt(0, b)
            for b in both:
                pe.wait_ge(xnt_ready[b], 1)
                pe.matmul(bank(b, 1), W["aQK"], xnT[:, b], start=True, stop=True).then_inc(a_proj[b], 1)
                for c in range(NC):
                    last = pe.matmul(bank(b, 2)[:, c * D:(c + 1) * D], xnT[:, b, c * P:(c + 1) * P], W["aVO"],
                                     start=True, stop=True)
                last.then_inc(a_proj[b], 1)
            for b in both:
                pe.wait_ge(k_sb[b], after("k_sb"))
                pe.matmul(bank(b, 3)[:, 0:D], lk[:, b], lv[:, b], start=True, stop=True)
                pe.matmul(bank(b, 3)[:, D:D + H], lk[:, b], ones[0:TK, 0:H], start=True, stop=True).then_inc(k_ps[b], 1)
            for b in both:
                pe.wait_ge(a_q[b], after("a_q"))
                for c in range(NC):
                    if SBANK[c] == 2:
                        pe.wait_ge(a_v[b], after("a_v"))
                    if SBANK[c] == 3:
                        pe.wait_ge(k_sb[b], after("k_sb", 2))
                    pe.matmul(bank(b, SBANK[c]), xqkT[:, b, c * P:(c + 1) * P], xnT[:, b], start=True, stop=True)\
                        .then_inc(a_s[b], 1)
            for b in both:
                pe.wait_ge(a_e[b], NC)
                for u in range(NC):
                    for c in range(NC):
                        last = pe.transpose(bank(b, SBANK[u])[:, c * P:(c + 1) * P], prob[:, b, c, u * P:(u + 1) * P], ident)
                    last.then_inc(a_t[b], 1)
            for b in both:
                pe.wait_ge(a_pt[b], NC)
                for c in range(NC):
                    for u in range(NC):
                        last = pe.matmul(bank(b, 0)[:, c * D:(c + 1) * D], probT[:, b, u, c * P:(c + 1) * P], xvo[:, b, u],
                                         start=(u == 0), stop=(u == NC - 1))
                last.then_inc(a_o[b], 1)

            if stages > 1:
                for b in both:
                    xnt(1, b)
                for b in both:
                    pe.wait_ge(xnt_ready[b], 2)
                    pe.matmul(bank(b, 1), W["cWq"], xnT[:, b], start=True, stop=True).then_inc(c_qps[b], 1)
                def scores(c, b):
                    if c == 0:
                        pe.wait_ge(consts, 3 + B)
                        pe.wait_ge(c_q[b], after("c_q"))
                    else:
                        pe.wait_ge(c_pt[b], NC * c)
                    for a in range(3):
                        last = pe.matmul(bank(b, a)[:, 0:HPB * TK], cqT[:, b, c * P:(c + 1) * P],
                                         ckb[:, b, a * HPB:(a + 1) * HPB].rearrange("p h k -> p (h k)"),
                                         start=True, stop=True)
                    last.then_inc(c_s[b], 1)

                def turns(c, b):
                    pe.wait_ge(c_e[b], c + 1)
                    if c:
                        pe.wait_ge(c_on[b], c)
                    for j in range(QH):
                        for g in range(H // QH):
                            h = QH * g + j
                            last = pe.transpose(bank(b, TBANK[j])[0:TK, g * P:(g + 1) * P],
                                                cprob[:, b, h * TK:(h + 1) * TK], ident)
                        last.then_inc(c_t[b], 1)

                def values(c, b):
                    pe.wait_ge(c_pt[b], NC * (c + 1))
                    for j in range(QH):
                        for g in range(H // QH):
                            last = pe.matmul(bank(b, 3)[g * QC:(g + 1) * QC, c * P:(c + 1) * P], cvp[:, b, QH * g + j],
                                             cprobT[:, b, j, g * P:(g + 1) * P], start=(j == 0), stop=(j == QH - 1))
                    last.then_inc(c_o[b], 1)

                for b in both:
                    scores(0, b)
                for c in range(NC):
                    for b in both:
                        turns(c, b)
                        if (c, b) != (0, 0):
                            values(*divmod(B * c + b - 1, B))
                        if c + 1 < NC:
                            scores(c + 1, b)
                values(NC - 1, B - 1)
                for b in both:
                    pe.wait_ge(o_fin[b], after("o_fin"))
                    ot(0, b, 0)
                for b in both:
                    wo(0, b, 1, "cWo")

            if stages > 2:
                pe.wait_ge(w12_split, 1)
                for b in both:
                    xnt(2, b)
                for b in both:
                    pe.wait_ge(xnt_ready[b], 3)
                    for c in range(NC):
                        last = pe.matmul(bank(b, 3)[:, c * E:(c + 1) * E], xnT[:, b, c * P:(c + 1) * P], W["mG"],
                                         start=True, stop=True)
                    last.then_inc(g_ps[b], 1)

                def hidden(e, b):
                    if e == 0:
                        pe.wait_ge(xnl_ready[b], 2)
                    if e >= 2:
                        pe.wait_ge(m_h[b], e - 1)
                    mm3(pe, bank(b, e % 2), w12h[:, 0, e], w12l[:, 0, e], xnTh[:, b], xnTl[:, b]).then_inc(m_hps[b], 1)

                for e in range(2):
                    for b in both:
                        hidden(e, b)
                for b in both:
                    pe.wait_ge(g_sel[b], after("g_sel"))
                for b in both:
                    last = pe.matmul(bank(0, 3)[:, 64:64 + NC * E], ones[:, :], sel[:, b].rearrange("p c e -> p (c e)"),
                                     start=(b == 0), stop=(b == B - 1))
                last.then_inc(g_cnt, 1)
                for b in both:
                    comb_rows(0, b, "g_comb")

                def weights(e, b):
                    if e == 0:
                        pe.wait_ge(m_cl[b], after("m_cl"))
                    else:
                        pe.wait_ge(m_hc[b], e)
                    spread(bank(b, 3), 0, e, b).then_inc(m_cb[b], 1)

                for b in both:
                    weights(0, b)
                for e in range(E):
                    if e + 1 < E:
                        for b in both:
                            if e:
                                hidden(e + 1, b)
                        for b in both:
                            weights(e + 1, b)
                    for b in both:
                        pe.wait_ge(m_hl[b], e + 1)
                        mm3(pe, bank(b, 2), w12h[:, 1, e], w12l[:, 1, e], hidh[:, b, e % 2], hidl[:, b, e % 2],
                            start=(e == 0), stop=False).then_inc(m_y[b], 1)
                for b in both:
                    mm3(pe, bank(b, 2), b2h[:, :], b2l[:, :], combTh0[:, b], combTl0[:, b], start=False)\
                        .then_inc(m_b[b], 1)
                for b in both:
                    moe_turn(1, b, bank(b, 1))

            if stages > 3:
                pe.wait_ge(mask_ready, 2)
                for b in both:
                    xnt(3, b)
                for b in both:
                    pe.wait_ge(xnt_ready[b], 4)
                    if b:
                        pe.wait_ge(s_e[0], 2 * GROUPS)
                        pe.wait_ge(s_pt[0][VBANK - 4], 2 * GROUPS // 3)
                    for c in range(NC):
                        last = pe.matmul(ps[:, VBANK, c * D:(c + 1) * D], xnT[:, b, c * P:(c + 1) * P], W["sWv"],
                                         start=True, stop=True)
                    last.then_inc(q_vps[b], 1)
                    for u in range(2 * SLOTS):
                        if u == 4:
                            pe.wait_ge(xnt_ready[1], 4)
                            if b:
                                pe.wait_ge(s_pt[0][0], 2 * GROUPS // 3)
                        if b and u == 5:
                            pe.wait_ge(s_pt[0][1], 2 * GROUPS // 3)
                        if b and u == 6:
                            pe.wait_ge(s_on[0], 1)
                        if u == 7:
                            pe.wait_ge(q_v[b], after("q_v"))
                        w = W["sWk" if u % 2 else "sWq"][:, u // 2 * KR:(u // 2 + 1) * KR]
                        pe.matmul(ps[0:KR, PBANK[u]], w, xnT[:, b], start=True, stop=True).then_inc(p_ps[b], 1)

                    def scores(n):
                        kind, par = n % 3, n % 2
                        pair = n // 3
                        if n < 2:
                            pe.wait_ge(p_done[b], 4 - 2 * (1 - n))
                        if kind == 0:
                            pe.wait_ge(p_head[b], 2 * pair + 2)
                        at, w = NEARCOLS[kind]
                        for j in range(2):
                            i_ = 2 * pair + j
                            if n >= 2:
                                pe.wait_ge(s_e[b], 2 * n - 3 + j)
                            dst = ps[:, 2 * par + j]

                            def qk(i, c, k0, k1, to, **flags):
                                return pe.matmul(dst[:, to:to + k1 - k0], reps[:, b, i, i_ // QH, c * P:(c + 1) * P],
                                                 khead[:, i_, k0:k1], **flags)

                            c = NC - 1 - kind
                            qk(QA, c, 0, c * P - CLIP, 0, start=True, stop=True)
                            pe.matmul(dst[:, at:at + w], identb, maskb[:, 0:w], start=True, stop=False)
                            last = qk(QS, c, c * P - CLIP, (c + 1) * P, at, start=False, stop=(kind < 2))
                            if kind == 2:
                                last = qk(QS, 0, 0, P, at + WL, start=False, stop=True)
                        last.then_inc(s_s[b], 1)

                    def turns(n):
                        kind, par = n % 3, n % 2
                        for j in range(2):
                            m = 2 * n + j
                            pe.wait_ge(s_e[b], m + 1)
                            if m >= 3:
                                pe.wait_ge(s_pt[b][m % 3], m // 3)
                            else:
                                pe.wait_ge(p_done[b], (5, 6, 8)[m])
                            for i in range(UNIT[kind] // P):
                                last = pe.transpose(ps[:, 4 + m % 3, i * P:(i + 1) * P], sprob[:, par, j, i * P:(i + 1) * P], ident)
                            last.then_inc(s_t[b], 1)

                    def values(n):
                        kind, pair = n % 3, n // 3
                        for j in range(2):
                            m = 2 * n + j
                            pe.wait_ge(s_pt[b][m % 3], m // 3 + 1)
                        if n == 0:
                            pe.wait_ge(p_done[b], 2 * SLOTS)
                        c = NC - 1 - kind
                        blocks = [(c, u, u) for u in range(c + 1)] + ([(0, 2, 0)] if kind == 2 else [])
                        for c, i, u in blocks:
                            for j in range(2):
                                h = head(pair, j)
                                tile = slice(h // QH * QC, (h // QH + 1) * QC)
                                last = pe.matmul(ps[tile, 7, c * P:(c + 1) * P], svp[:, b, u, h],
                                                 sprobT[:, (2 * n + j) % 4, i * P:(i + 1) * P],
                                                 start=(pair < 2 and kind == 0 and u == 0),
                                                 stop=(pair >= 2 * QH - 2 and (c, u) == (0, 0)))
                        last.then_inc(s_o[b], 2)

                    scores(0)
                    scores(1)
                    for n in range(GROUPS):
                        if n + 2 < GROUPS:
                            scores(n + 2)
                        turns(n)
                        if n:
                            values(n - 1)
                    values(GROUPS - 1)
                for b in both:
                    pe.wait_ge(o_fin[b], after("o_fin", 2))
                    ot(1, b, 0)
                for b in both:
                    wo(1, b, 1, "sWo")
            if stages > 4:
                for b in both:
                    xnt(4, b)
                for b in both:
                    pe.wait_ge(xnt_ready[b], 5)
                    pe.matmul(bank(b, 1), W["lWq"], xnT[:, b], start=True, stop=True).then_inc(l_qps[b], 1)
                for b in both:
                    pe.wait_ge(l_q[b], after("l_q"))
                    for c in range(NC):
                        at = (c % 2) * (D + H)
                        last = pe.matmul(bank(b, 2 + c // 2)[:, at:at + D + H], cqT[:, b, c * P:(c + 1) * P], lkv[:, b],
                                         start=True, stop=True)
                    last.then_inc(l_nps[b], 1)
                for b in both:
                    pe.wait_ge(o_fin[b], after("o_fin", 3))
                    ot(2, b, 0)
                for b in both:
                    wo(2, b, 1, "lWo")
            if stages > 5:
                for b in both:
                    xnt(5, b)
                for b in both:
                    pe.wait_ge(xnt_ready[b], 6)
                    for c in range(NC):
                        last = pe.matmul(route_bank(1, b)[:, c * E:(c + 1) * E], xnT[:, b, c * P:(c + 1) * P], W["fG"],
                                         start=True, stop=True)
                    last.then_inc(g_ps[b], 1)

                def gate_up(n_):
                    k, i = divmod(n_, NI)
                    e, b = divmod(k, B)
                    if k % B == 0 and i == 0:
                        pe.wait_ge(f_wl, 3 * (e + 1))
                    if n_ in (0, NI):
                        pe.wait_ge(xnl_ready[b], 4)
                    if n_ >= 2:
                        pe.wait_ge(f_a, n_ - 1)
                    for half, done in ((0, f_g), (1, f_u)):
                        at = slice(half * I1 + i * P, half * I1 + (i + 1) * P)
                        mm3(pe, ps[:, 2 * (n_ % 2) + half], fwh[:, e % 2, at], fwl[:, e % 2, at], xnTh[:, b], xnTl[:, b])\
                            .then_inc(done, 1)

                def weights(k):
                    e, b = divmod(k, B)
                    if k >= 2:
                        pe.wait_ge(f_a, NI * (k - 1))
                    spread(ps[:, 6 + k % 2], 1, e, b).then_inc(f_cb, 1)

                def down(k):
                    e, b = divmod(k, B)
                    for i in range(NI):
                        pe.wait_ge(f_al, NI * k + i + 1)
                        at = slice(2 * I1 + i * P, 2 * I1 + (i + 1) * P)
                        last = mm3(pe, ps[:, 4 + b], fwh[:, e % 2, at], fwl[:, e % 2, at], fah[:, k % 2, i], fal[:, k % 2, i],
                                   start=(e == 0 and i == 0), stop=(e == E - 1 and i == NI - 1))
                    last.then_inc(f_y if e < E - 1 else m_b[b], 1)

                gate_up(0)
                comb_rows(1, 0, "f_comb")
                gate_up(1)
                pe.wait_ge(v_ones, 4)
                pe.wait_ge(m_cl[0], after("m_cl", 2))
                weights(0)
                for n_ in range(E * B * NI):
                    if n_ == NI:
                        pe.wait_ge(m_cl[1], after("m_cl", 2))
                    if n_ % NI == 0 and n_:
                        weights(n_ // NI)
                    if n_ >= 2:
                        gate_up(n_)
                    if n_ == 2:
                        comb_rows(1, 1, "f_comb")
                    if n_ % NI == 2 and n_ > NI:
                        down(n_ // NI - 1)
                pe.wait_ge(f_a, NI * (E * B - 1))
                moe_turn(2, 0, ps[:, 6])
                down(E * B - 1)
                pe.wait_ge(f_a, NI * E * B)
                moe_turn(2, 1, ps[:, 7])


def head(pair, j):
    i = 2 * pair + j
    return i % (H // QH) * QH + i // (H // QH)


GROUPS = 3 * H // 2
GROUP = [[(0, 4 * P, 0)], [(0, 3 * P, 0)], [(0, 2 * P, 0), (2 * P, P, 2)]]
NEARCOLS = [(3 * P - CLIP, WL), (2 * P - CLIP, WL), (P - CLIP, NEAR2)]
UNIT = [4 * P, 3 * P, 3 * P]
SBANK = [0, 3, 1, 2]
VBANK = 6
PBANK = [0, 1, 2, 3, 4, 5, 7, 6]
TBANK = [3, 0, 1, 2]


def constants():
    p = np.arange(P)
    heads = (p[:, None] // HD == np.arange(H)).astype(np.float32)
    blockd = (p[:, None] // HD == p // HD).astype(np.float32)
    away = p[:, None] + CLIP - np.arange(WL)
    dist = np.where(away < 0, -1, np.minimum(away, CLIP)).astype(np.float32)
    dist = np.concatenate([dist, dist[:, CLIP:]], 1)
    mask = np.where(dist < 0, BIG, 0.0).astype(np.float32)
    low = (np.arange(E)[None, :] < np.arange(E)[:, None]).astype(np.float32).reshape(1, E * E)
    r = p[:, None] // HD % 3
    q = np.float32(HD ** -0.5)
    signs = np.concatenate([np.where(r == 2, -q, q), np.where(r == 2, q, 0), np.where(r == 1, -1, 1), np.where(r == 1, 1, 0)],
                           1).astype(np.float32)
    rowhead = (p[:, None] // (3 * HD) == np.arange(QH)).astype(np.float32)
    return np.ascontiguousarray(np.concatenate(
        [np.eye(P, dtype=np.float32), blockd, dist, np.repeat(low, P, 0), heads, mask, signs, rowhead], 1))


def slots(w):
    w = w.reshape(D, H // QH, QH, HD).transpose(0, 2, 1, 3)
    return np.repeat(w[:, :, :, None], 3, 3).reshape(D, SLOTS * KR)


STAGES = 6


def kernel(**a):
    import concourse.bacc as bacc
    from concourse.bass_utils import run_bass_kernel_spmd

    a = {k: np.asarray(v) for k, v in a.items()}
    w = {"aQK": a["L0_attn_QK"], "aVO": a["L0_attn_VO"],
         "cWq": a["L0_xattn_Wq"].T, "cWk": a["L0_xattn_Wk"].T, "cWv": a["L0_xattn_Wv"].T, "cWo": a["L0_xattn_Wo"].T,
         "mG": a["L0_ffn_gate_w"].T,
         "sWq": slots(a["L1_attn_Wq"]), "sWk": slots(a["L1_attn_Wk"]), "sWv": a["L1_attn_Wv"], "sWo": a["L1_attn_Wo"],
         "lWq": a["L1_xattn_Wq"].T, "lWk": a["L1_xattn_Wk"].T, "lWv": a["L1_xattn_Wv"].T, "lWo": a["L1_xattn_Wo"].T,
         "fG": a["L1_ffn_conf_w"].T}
    r = {"cbv": "L0_xattn_bv", "cbo": "L0_xattn_bo", "sbo": "L1_attn_bo", "lbk": "L1_xattn_bk", "lbv": "L1_xattn_bv",
         "lbo": "L1_xattn_bo", "fb": "L1_ffn_conf_b", "fw": "L1_ffn_wealth", "rel": "L1_attn_rel_emb"}
    c = {"cbq": "L0_xattn_bq", "cbk": "L0_xattn_bk", "lbq": "L1_xattn_bq"}
    cc = np.ascontiguousarray
    arrays = {
        "x": cc(a["x"]),
        "cst": constants(),
        "wts": cc(np.concatenate([w[n] for n in WEIGHTS], 1)),
        "rows": cc(np.concatenate([a[r[n]] for n in ROWS])),
        "cols": cc(np.concatenate([a[c[n]][:, None] for n in COLS] + [a["L0_ffn_b1"].T], 1)),
        "ctxT": cc(a["ctx_1024"].transpose(2, 0, 1)),
        "b2": cc(np.concatenate([a["L0_ffn_b2"], np.zeros((P - E, D), np.float32)])),
        "w12": cc(np.stack([a["L0_ffn_w1"].transpose(2, 0, 1), a["L0_ffn_w2"].transpose(2, 0, 1)], 1)),
        "fgu": cc(np.stack([a["L1_ffn_gate_w"].transpose(2, 0, 1), a["L1_ffn_up_w"].transpose(2, 0, 1)], 2)),
        "fdn": cc(a["L1_ffn_down_w"].reshape(E, D, NI, P).transpose(3, 0, 2, 1)),
    }
    nc = bacc.Bacc("TRN2", target_bir_lowering=False, num_devices=1)
    d = {n: nc.dram_tensor(f"in_{n}", v.shape, mybir.dt.from_np(v.dtype), kind="ExternalInput").ap()
         for n, v in arrays.items()}
    out = nc.dram_tensor("out_x", (B, T, D), F32, kind="ExternalOutput").ap()
    build(nc, d, out, STAGES)
    got = run_bass_kernel_spmd(nc, [{f"in_{n}": v for n, v in arrays.items()}], core_ids=[0])
    return got.results[0]["out_x"]
```
